# Optimizing a Trainium2 kernel written in Bass

```python
import numpy as np
import jax
import jax.numpy as jnp

def _softmax(x, axis=-1):
    return jax.nn.softmax(x, axis=axis)

def _gelu(x):
    return jax.nn.gelu(x, approximate=True)

def _silu(x):
    return jax.nn.silu(x)

def _sigmoid(x):
    return jax.nn.sigmoid(x)

def _layernorm(x, axis=-1, eps=1e-05):
    m = jnp.mean(x, axis=axis, keepdims=True)
    v = jnp.var(x, axis=axis, keepdims=True)
    return (x - m) / jnp.sqrt(v + eps)

def _scatter_add(tgt, idx, src, axis=0):
    return tgt.at[idx].add(src)

def _segment_sum(src, seg, n):
    return jax.ops.segment_sum(src, seg, n)
kernel_name = 'mk_perceiver_d4_seqx_r8_7ef273'

def setup_inputs(seed: int=0):
    np.random.seed(seed)
    _w = jnp.asarray

    def _rec_inputs():
        import jax
        import jax.numpy as jnp
        _rk = jax.random.key(seed)
        x = -0.000125 + 0.9999 * jax.random.normal(jax.random.fold_in(_rk, 1), (64, 32, 128), jnp.float32)
        _lenS = 32 - jax.random.randint(jax.random.fold_in(_rk, 7), (64,), 0, max(1, 32 // 4) + 1, jnp.int32)
        _lenS2 = 257 - jax.random.randint(jax.random.fold_in(_rk, 8), (64,), 0, max(1, 257 // 4) + 1, jnp.int32)
        _ctx_1024P = jax.random.normal(jax.random.fold_in(_rk, 11), (64, 16, 128), jnp.float32)
        _ctx_1024c = jax.random.dirichlet(jax.random.fold_in(_rk, 511), 0.3 * jnp.ones((16,), jnp.float32), (64, 257))
        _ctx_1024t = jnp.einsum('bsk,bkd->bsd', _ctx_1024c, _ctx_1024P)
        _ctx_1024t = _ctx_1024t * jax.lax.rsqrt(jnp.mean(jnp.square(_ctx_1024t)) + 1e-12) * 0.953939
        ctx_1024 = -1.52775e-05 + 0.999936 * (_ctx_1024t + 0.3 * jax.random.normal(jax.random.fold_in(_rk, 611), (64, 257, 128), jnp.float32))
        return (x, ctx_1024)
    x, ctx_1024 = _rec_inputs()

    def _L0_xattn_setup():
        import jax, jax.numpy as jnp
        import numpy as np
        B, R, U, D = (16, 256, 256, 128)
        EPS_ATT = 1e-08
        EPS_LN = 1e-06
        key = jax.random.key(seed)
        ks = jax.random.split(key, 6)
        s = 1.0 / np.sqrt(D)
        return {'Q': jax.random.normal(ks[0], (B, R, D), dtype=jnp.float32), 'K': jax.random.normal(ks[1], (B, U, D), dtype=jnp.float32), 'V': jax.random.normal(ks[2], (B, U, D), dtype=jnp.float32), 'W1': jax.random.normal(ks[3], (D, D), dtype=jnp.float32) * s, 'b1': jnp.zeros((D,), dtype=jnp.float32), 'W2': jax.random.normal(ks[4], (D, D), dtype=jnp.float32) * s, 'b2': jnp.zeros((D,), dtype=jnp.float32), 'gamma': jnp.ones((D,), dtype=jnp.float32), 'beta': jnp.zeros((D,), dtype=jnp.float32)}
    _L0_xattn_all = _L0_xattn_setup()
    _L0_xattn_in = {k: v for k, v in _L0_xattn_all.items() if k in ('W1', 'b1', 'W2', 'b2', 'gamma', 'beta')}
    del _L0_xattn_all

    def _L0_attn_setup():
        import jax, jax.numpy as jnp
        import numpy as np
        EPS = 1e-06

        def rmsnorm(x, w):
            rms = jnp.sqrt(jnp.mean(x * x, axis=-1, keepdims=True) + EPS)
            return w * x / rms
        key = jax.random.key(seed)
        ks = jax.random.split(key, 12)
        B, L, D, S, E, H = (2, 256, 128, 16, 4, 256)
        x = jax.random.normal(ks[0], (B, L, D), jnp.float32)
        A_log = jnp.log(jax.random.uniform(ks[1], (D, S), jnp.float32) * 0.5 + 0.5)
        D_param = jnp.ones((D,), jnp.float32)
        W_delta = jax.random.normal(ks[2], (D, D), jnp.float32) * 0.02
        b_delta = jnp.zeros((D,), jnp.float32)
        W_B = jax.random.normal(ks[3], (D, S), jnp.float32) * 0.02
        W_C = jax.random.normal(ks[4], (D, S), jnp.float32) * 0.02
        W_router = jax.random.normal(ks[5], (D, E), jnp.float32) * 0.02
        Wg = jax.random.normal(ks[6], (E, D, H), jnp.float32) * 0.02
        Wu = jax.random.normal(ks[7], (E, D, H), jnp.float32) * 0.02
        Wd = jax.random.normal(ks[8], (E, H, D), jnp.float32) * 0.02
        wn_exp = jnp.ones((E, H), jnp.float32)
        norm_w = jnp.ones((D,), jnp.float32)
        return dict(x=x, A_log=A_log, D_param=D_param, W_delta=W_delta, b_delta=b_delta, W_B=W_B, W_C=W_C, W_router=W_router, Wg=Wg, Wu=Wu, Wd=Wd, wn_exp=wn_exp, norm_w=norm_w)
    _L0_attn_all = _L0_attn_setup()
    _L0_attn_in = {k: v for k, v in _L0_attn_all.items() if k in ('A_log', 'D_param', 'W_delta', 'b_delta', 'W_B', 'W_C', 'W_router', 'Wg', 'Wu', 'Wd', 'wn_exp', 'norm_w')}
    del _L0_attn_all

    def _L0_ffn_setup():
        import jax, jax.numpy as jnp
        import numpy as np
        B, S, D, H, E = (4, 256, 128, 16, 4)
        key = jax.random.key(seed)
        ks = jax.random.split(key, 8)
        w = lambda k, shape: jax.random.normal(k, shape, jnp.float32) * 0.02
        return {'x': jax.random.normal(ks[0], (B, S, D), jnp.float32), 'router_w': w(ks[1], (D, E)), 'router_b': jnp.zeros((E,), jnp.float32), 'wq': w(ks[2], (E, D, D)), 'bq': jnp.zeros((E, D), jnp.float32), 'wk': w(ks[3], (E, D, D)), 'bk': jnp.zeros((E, D), jnp.float32), 'wv': w(ks[4], (E, D, D)), 'bv': jnp.zeros((E, D), jnp.float32), 'wo': w(ks[5], (E, D, D)), 'bo': jnp.zeros((E, D), jnp.float32)}
    _L0_ffn_all = _L0_ffn_setup()
    _L0_ffn_in = {k: v for k, v in _L0_ffn_all.items() if k in ('router_w', 'router_b', 'wq', 'bq', 'wk', 'bk', 'wv', 'bv', 'wo', 'bo')}
    del _L0_ffn_all

    def _L1_xattn_setup():
        import jax, jax.numpy as jnp
        import numpy as np
        DIM = 128
        key = jax.random.key(seed)
        ks = jax.random.split(key, 9)
        B, S, D = (8, 256, DIM)
        inv = 1.0 / np.sqrt(D)
        return {'image_emb': jax.random.normal(ks[0], (B, S, D), dtype=jnp.float32), 'text_emb': jax.random.normal(ks[1], (B, S, D), dtype=jnp.float32), 'edge_index': jax.random.randint(ks[2], (2, 16), 0, 256, dtype=jnp.int64), 'Wq': jax.random.normal(ks[3], (D, D), dtype=jnp.float32) * inv, 'bq': jnp.zeros((D,), dtype=jnp.float32), 'Wk': jax.random.normal(ks[4], (D, D), dtype=jnp.float32) * inv, 'bk': jnp.zeros((D,), dtype=jnp.float32), 'Wv': jax.random.normal(ks[5], (D, D), dtype=jnp.float32) * inv, 'bv': jnp.zeros((D,), dtype=jnp.float32)}
    _L1_xattn_all = _L1_xattn_setup()
    _L1_xattn_in = {k: v for k, v in _L1_xattn_all.items() if k in ('edge_index', 'Wq', 'bq', 'Wk', 'bk', 'Wv', 'bv')}
    del _L1_xattn_all

    def _L1_attn_setup():
        import jax, jax.numpy as jnp
        import numpy as np
        EPS = 1.1920929e-07
        NUM_HEADS = 16
        SOFTCAP = 50.0

        def rms_norm(x):
            return x * jax.lax.rsqrt(jnp.mean(x * x, axis=-1, keepdims=True) + EPS)
        key = jax.random.key(seed)
        ks = jax.random.split(key, 5)
        B, S, D = (2, 256, 128)
        x = jax.random.normal(ks[0], (B, S, D), dtype=jnp.float32)
        w_q = jax.random.normal(ks[1], (D, D), dtype=jnp.float32) * 0.02
        w_k = jax.random.normal(ks[2], (D, D), dtype=jnp.float32) * 0.02
        w_v = jax.random.normal(ks[3], (D, D), dtype=jnp.float32) * 0.02
        w_o = jax.random.normal(ks[4], (D, D), dtype=jnp.float32) * 0.02
        return {'x': x, 'w_q': w_q, 'w_k': w_k, 'w_v': w_v, 'w_o': w_o}
    _L1_attn_all = _L1_attn_setup()
    _L1_attn_in = {k: v for k, v in _L1_attn_all.items() if k in ('w_q', 'w_k', 'w_v', 'w_o')}
    del _L1_attn_all

    def _L1_ffn_setup():
        import jax, jax.numpy as jnp
        import numpy as np
        N_EXPERTS = 8
        TOP_K = 2
        D_MODEL = 128
        HIDDEN = 512
        ROUTED_H = 128
        BATCH, SEQ = (2, 512)
        key = jax.random.key(seed)
        ks = jax.random.split(key, 8)
        std = 0.02
        return {'x': jax.random.normal(ks[0], (BATCH, SEQ, D_MODEL), dtype=jnp.float32), 'w12': std * jax.random.normal(ks[1], (N_EXPERTS, 2 * ROUTED_H, D_MODEL), dtype=jnp.float32), 'w3': std * jax.random.normal(ks[2], (N_EXPERTS, D_MODEL, ROUTED_H), dtype=jnp.float32), 'shared_w1': std * jax.random.normal(ks[3], (HIDDEN, D_MODEL), dtype=jnp.float32), 'shared_w2': std * jax.random.normal(ks[4], (HIDDEN, D_MODEL), dtype=jnp.float32), 'shared_w3': std * jax.random.normal(ks[5], (D_MODEL, HIDDEN), dtype=jnp.float32), 'router_w': std * jax.random.normal(ks[6], (N_EXPERTS, D_MODEL), dtype=jnp.float32), 'expert_bias': jnp.zeros((N_EXPERTS,), dtype=jnp.float32)}
    _L1_ffn_all = _L1_ffn_setup()
    _L1_ffn_in = {k: v for k, v in _L1_ffn_all.items() if k in ('w12', 'w3', 'shared_w1', 'shared_w2', 'shared_w3', 'router_w', 'expert_bias')}
    del _L1_ffn_all

    def _L2_xattn_setup():
        import jax, jax.numpy as jnp
        import numpy as np
        B, LQ, LK = (8, 256, 256)
        HIST_DIM, COMB_DIM, FUSION_DIM = (128, 128, 128)

        def _linear_params(key, in_dim, out_dim):
            k1, k2 = jax.random.split(key)
            bound = 1.0 / np.sqrt(in_dim)
            W = jax.random.uniform(k1, (out_dim, in_dim), jnp.float32, -bound, bound)
            b = jax.random.uniform(k2, (out_dim,), jnp.float32, -bound, bound)
            return (W, b)

        def _lin(x, W, b):
            return jnp.einsum('bld,fd->blf', x, W) + b
        key = jax.random.key(seed)
        ks = jax.random.split(key, 8)
        hW, hb = _linear_params(ks[0], HIST_DIM, FUSION_DIM)
        cW, cb = _linear_params(ks[1], COMB_DIM, FUSION_DIM)
        qW, qb = _linear_params(ks[2], FUSION_DIM, FUSION_DIM)
        kW, kb = _linear_params(ks[3], FUSION_DIM, FUSION_DIM)
        vW, vb = _linear_params(ks[4], FUSION_DIM, FUSION_DIM)
        oW, ob = _linear_params(ks[5], FUSION_DIM, FUSION_DIM)
        return {'history_features': jax.random.normal(ks[6], (B, LQ, HIST_DIM), jnp.float32), 'combined_features': jax.random.normal(ks[7], (B, LK, COMB_DIM), jnp.float32), 'hW': hW, 'hb': hb, 'cW': cW, 'cb': cb, 'qW': qW, 'qb': qb, 'kW': kW, 'kb': kb, 'vW': vW, 'vb': vb, 'oW': oW, 'ob': ob}
    _L2_xattn_all = _L2_xattn_setup()
    _L2_xattn_in = {k: v for k, v in _L2_xattn_all.items() if k in ('hW', 'hb', 'cW', 'cb', 'qW', 'qb', 'kW', 'kb', 'vW', 'vb', 'oW', 'ob')}
    del _L2_xattn_all

    def _L2_attn_setup():
        import jax, jax.numpy as jnp
        import numpy as np
        D_MODEL = 128
        N_HEADS = 16
        key = jax.random.key(seed)
        ks = jax.random.split(key, 9)
        B, L, D = (4, 256, D_MODEL)
        s = 1.0 / np.sqrt(D)
        return {'x': jax.random.normal(ks[0], (B, L, D), dtype=jnp.float32), 'wq': jax.random.normal(ks[1], (D, D), dtype=jnp.float32) * s, 'bq': jnp.zeros((D,), dtype=jnp.float32), 'wk': jax.random.normal(ks[2], (D, D), dtype=jnp.float32) * s, 'bk': jnp.zeros((D,), dtype=jnp.float32), 'wv': jax.random.normal(ks[3], (D, D), dtype=jnp.float32) * s, 'bv': jnp.zeros((D,), dtype=jnp.float32), 'wo': jax.random.normal(ks[4], (D, D), dtype=jnp.float32) * s, 'bo': jnp.zeros((D,), dtype=jnp.float32)}
    _L2_attn_all = _L2_attn_setup()
    _L2_attn_in = {k: v for k, v in _L2_attn_all.items() if k in ('wq', 'bq', 'wk', 'bk', 'wv', 'bv', 'wo', 'bo')}
    del _L2_attn_all

    def _L2_ffn_setup():
        import jax, jax.numpy as jnp
        import numpy as np
        CAPACITY_FACTOR = 1.25
        key = jax.random.key(seed)
        k1, k2, k3, k4 = jax.random.split(key, 4)
        B, S, D, E, H = (2, 256, 128, 16, 512)
        inputs = jax.random.normal(k1, (B, S, D), dtype=jnp.float32)
        gate_w = jax.random.normal(k2, (E, D), dtype=jnp.float32) / np.float32(np.sqrt(D))
        w1 = jax.random.normal(k3, (E, D, H), dtype=jnp.float32) / np.float32(np.sqrt(D))
        w2 = jax.random.normal(k4, (E, H, D), dtype=jnp.float32) / np.float32(np.sqrt(H))
        return {'inputs': inputs, 'gate_w': gate_w, 'w1': w1, 'w2': w2}
    _L2_ffn_all = _L2_ffn_setup()
    _L2_ffn_in = {k: v for k, v in _L2_ffn_all.items() if k in ('gate_w', 'w1', 'w2')}
    del _L2_ffn_all

    def _L3_xattn_setup():
        import jax, jax.numpy as jnp
        import numpy as np
        DIM = 128
        DIM_HEAD = 64
        HEADS = 16
        INNER = DIM_HEAD * HEADS
        EPS = 1e-05

        def layer_norm(x, g, b):
            m = jnp.mean(x, axis=-1, keepdims=True)
            v = jnp.mean(jnp.square(x - m), axis=-1, keepdims=True)
            return (x - m) * jax.lax.rsqrt(v + EPS) * g + b
        key = jax.random.key(seed)
        ks = jax.random.split(key, 8)
        B, N_IMG, N_LAT = (4, 512, 64)
        std = 1.0 / np.sqrt(DIM)
        return {'image_embeds': jax.random.normal(ks[0], (B, N_IMG, DIM), dtype=jnp.float32), 'latents': jax.random.normal(ks[1], (B, N_LAT, DIM), dtype=jnp.float32), 'ln1_g': jnp.ones((DIM,), jnp.float32), 'ln1_b': jnp.zeros((DIM,), jnp.float32), 'ln2_g': jnp.ones((DIM,), jnp.float32), 'ln2_b': jnp.zeros((DIM,), jnp.float32), 'Wq': jax.random.normal(ks[2], (DIM, INNER), dtype=jnp.float32) * std, 'Wkv': jax.random.normal(ks[3], (DIM, 2 * INNER), dtype=jnp.float32) * std, 'Wo': jax.random.normal(ks[4], (INNER, DIM), dtype=jnp.float32) * std}
    _L3_xattn_all = _L3_xattn_setup()
    _L3_xattn_in = {k: v for k, v in _L3_xattn_all.items() if k in ('ln1_g', 'ln1_b', 'ln2_g', 'ln2_b', 'Wq', 'Wkv', 'Wo')}
    del _L3_xattn_all

    def _L3_attn_setup():
        import jax, jax.numpy as jnp
        import numpy as np
        H = 16
        G = 4
        DIM = 128
        HD = DIM // H // G
        key = jax.random.key(seed)
        k1, k2, k3 = jax.random.split(key, 3)
        x = jax.random.normal(k1, (8, 512, DIM), dtype=jnp.float32)
        w_qkvw = jax.random.normal(k2, (DIM, 4 * DIM), dtype=jnp.float32) * 0.02
        w_out = jax.random.normal(k3, (DIM, DIM), dtype=jnp.float32) * 0.02
        return {'x': x, 'w_qkvw': w_qkvw, 'w_out': w_out}
    _L3_attn_all = _L3_attn_setup()
    _L3_attn_in = {k: v for k, v in _L3_attn_all.items() if k in ('w_qkvw', 'w_out')}
    del _L3_attn_all

    def _L3_ffn_setup():
        import jax, jax.numpy as jnp
        import numpy as np
        B, S, D, H, E, F, K = (2, 128, 128, 16, 8, 512, 2)
        EPS = 1e-05

        def _layernorm(x, g, b):
            mu = jnp.mean(x, axis=-1, keepdims=True)
            var = jnp.mean(jnp.square(x - mu), axis=-1, keepdims=True)
            return (x - mu) * jax.lax.rsqrt(var + EPS) * g + b
        key = jax.random.key(seed)
        ks = jax.random.split(key, 12)
        w = lambda k, shape: jax.random.normal(k, shape, dtype=jnp.float32) * 0.02
        return {'x': jax.random.normal(ks[0], (B, S, D), dtype=jnp.float32), 'ln1_g': jnp.ones((D,), jnp.float32), 'ln1_b': jnp.zeros((D,), jnp.float32), 'ln2_g': jnp.ones((D,), jnp.float32), 'ln2_b': jnp.zeros((D,), jnp.float32), 'Wq': w(ks[1], (D, D)), 'Wk': w(ks[2], (D, D)), 'Wv': w(ks[3], (D, D)), 'Wo': w(ks[4], (D, D)), 'Wg': w(ks[5], (D, E)), 'W1': w(ks[6], (E, D, F)), 'b1': jnp.zeros((E, F), jnp.float32), 'W2': w(ks[7], (E, F, D)), 'b2': jnp.zeros((E, D), jnp.float32)}
    _L3_ffn_all = _L3_ffn_setup()
    _L3_ffn_in = {k: v for k, v in _L3_ffn_all.items() if k in ('ln1_g', 'ln1_b', 'ln2_g', 'ln2_b', 'Wq', 'Wk', 'Wv', 'Wo', 'Wg', 'W1', 'b1', 'W2', 'b2')}
    del _L3_ffn_all
    return {'x': x, 'ctx_1024': ctx_1024, 'L0_xattn_W1': _L0_xattn_in['W1'], 'L0_xattn_b1': _L0_xattn_in['b1'], 'L0_xattn_W2': _L0_xattn_in['W2'], 'L0_xattn_b2': _L0_xattn_in['b2'], 'L0_xattn_gamma': _L0_xattn_in['gamma'], 'L0_xattn_beta': _L0_xattn_in['beta'], 'L0_attn_A_log': _L0_attn_in['A_log'], 'L0_attn_D_param': _L0_attn_in['D_param'], 'L0_attn_W_delta': _L0_attn_in['W_delta'], 'L0_attn_b_delta': _L0_attn_in['b_delta'], 'L0_attn_W_B': _L0_attn_in['W_B'], 'L0_attn_W_C': _L0_attn_in['W_C'], 'L0_attn_W_router': _L0_attn_in['W_router'], 'L0_attn_Wg': _L0_attn_in['Wg'], 'L0_attn_Wu': _L0_attn_in['Wu'], 'L0_attn_Wd': _L0_attn_in['Wd'], 'L0_attn_wn_exp': _L0_attn_in['wn_exp'], 'L0_attn_norm_w': _L0_attn_in['norm_w'], 'L0_ffn_router_w': _L0_ffn_in['router_w'], 'L0_ffn_router_b': _L0_ffn_in['router_b'], 'L0_ffn_wq': _L0_ffn_in['wq'], 'L0_ffn_bq': _L0_ffn_in['bq'], 'L0_ffn_wk': _L0_ffn_in['wk'], 'L0_ffn_bk': _L0_ffn_in['bk'], 'L0_ffn_wv': _L0_ffn_in['wv'], 'L0_ffn_bv': _L0_ffn_in['bv'], 'L0_ffn_wo': _L0_ffn_in['wo'], 'L0_ffn_bo': _L0_ffn_in['bo'], 'L1_xattn_edge_index': _L1_xattn_in['edge_index'], 'L1_xattn_Wq': _L1_xattn_in['Wq'], 'L1_xattn_bq': _L1_xattn_in['bq'], 'L1_xattn_Wk': _L1_xattn_in['Wk'], 'L1_xattn_bk': _L1_xattn_in['bk'], 'L1_xattn_Wv': _L1_xattn_in['Wv'], 'L1_xattn_bv': _L1_xattn_in['bv'], 'L1_attn_w_q': _L1_attn_in['w_q'], 'L1_attn_w_k': _L1_attn_in['w_k'], 'L1_attn_w_v': _L1_attn_in['w_v'], 'L1_attn_w_o': _L1_attn_in['w_o'], 'L1_ffn_w12': _L1_ffn_in['w12'], 'L1_ffn_w3': _L1_ffn_in['w3'], 'L1_ffn_shared_w1': _L1_ffn_in['shared_w1'], 'L1_ffn_shared_w2': _L1_ffn_in['shared_w2'], 'L1_ffn_shared_w3': _L1_ffn_in['shared_w3'], 'L1_ffn_router_w': _L1_ffn_in['router_w'], 'L1_ffn_expert_bias': _L1_ffn_in['expert_bias'], 'L2_xattn_hW': _L2_xattn_in['hW'], 'L2_xattn_hb': _L2_xattn_in['hb'], 'L2_xattn_cW': _L2_xattn_in['cW'], 'L2_xattn_cb': _L2_xattn_in['cb'], 'L2_xattn_qW': _L2_xattn_in['qW'], 'L2_xattn_qb': _L2_xattn_in['qb'], 'L2_xattn_kW': _L2_xattn_in['kW'], 'L2_xattn_kb': _L2_xattn_in['kb'], 'L2_xattn_vW': _L2_xattn_in['vW'], 'L2_xattn_vb': _L2_xattn_in['vb'], 'L2_xattn_oW': _L2_xattn_in['oW'], 'L2_xattn_ob': _L2_xattn_in['ob'], 'L2_attn_wq': _L2_attn_in['wq'], 'L2_attn_bq': _L2_attn_in['bq'], 'L2_attn_wk': _L2_attn_in['wk'], 'L2_attn_bk': _L2_attn_in['bk'], 'L2_attn_wv': _L2_attn_in['wv'], 'L2_attn_bv': _L2_attn_in['bv'], 'L2_attn_wo': _L2_attn_in['wo'], 'L2_attn_bo': _L2_attn_in['bo'], 'L2_ffn_gate_w': _L2_ffn_in['gate_w'], 'L2_ffn_w1': _L2_ffn_in['w1'], 'L2_ffn_w2': _L2_ffn_in['w2'], 'L3_xattn_ln1_g': _L3_xattn_in['ln1_g'], 'L3_xattn_ln1_b': _L3_xattn_in['ln1_b'], 'L3_xattn_ln2_g': _L3_xattn_in['ln2_g'], 'L3_xattn_ln2_b': _L3_xattn_in['ln2_b'], 'L3_xattn_Wq': _L3_xattn_in['Wq'], 'L3_xattn_Wkv': _L3_xattn_in['Wkv'], 'L3_xattn_Wo': _L3_xattn_in['Wo'], 'L3_attn_w_qkvw': _L3_attn_in['w_qkvw'], 'L3_attn_w_out': _L3_attn_in['w_out'], 'L3_ffn_ln1_g': _L3_ffn_in['ln1_g'], 'L3_ffn_ln1_b': _L3_ffn_in['ln1_b'], 'L3_ffn_ln2_g': _L3_ffn_in['ln2_g'], 'L3_ffn_ln2_b': _L3_ffn_in['ln2_b'], 'L3_ffn_Wq': _L3_ffn_in['Wq'], 'L3_ffn_Wk': _L3_ffn_in['Wk'], 'L3_ffn_Wv': _L3_ffn_in['Wv'], 'L3_ffn_Wo': _L3_ffn_in['Wo'], 'L3_ffn_Wg': _L3_ffn_in['Wg'], 'L3_ffn_W1': _L3_ffn_in['W1'], 'L3_ffn_b1': _L3_ffn_in['b1'], 'L3_ffn_W2': _L3_ffn_in['W2'], 'L3_ffn_b2': _L3_ffn_in['b2']}

def reference(x, ctx_1024, L0_xattn_W1, L0_xattn_b1, L0_xattn_W2, L0_xattn_b2, L0_xattn_gamma, L0_xattn_beta, L0_attn_A_log, L0_attn_D_param, L0_attn_W_delta, L0_attn_b_delta, L0_attn_W_B, L0_attn_W_C, L0_attn_W_router, L0_attn_Wg, L0_attn_Wu, L0_attn_Wd, L0_attn_wn_exp, L0_attn_norm_w, L0_ffn_router_w, L0_ffn_router_b, L0_ffn_wq, L0_ffn_bq, L0_ffn_wk, L0_ffn_bk, L0_ffn_wv, L0_ffn_bv, L0_ffn_wo, L0_ffn_bo, L1_xattn_edge_index, L1_xattn_Wq, L1_xattn_bq, L1_xattn_Wk, L1_xattn_bk, L1_xattn_Wv, L1_xattn_bv, L1_attn_w_q, L1_attn_w_k, L1_attn_w_v, L1_attn_w_o, L1_ffn_w12, L1_ffn_w3, L1_ffn_shared_w1, L1_ffn_shared_w2, L1_ffn_shared_w3, L1_ffn_router_w, L1_ffn_expert_bias, L2_xattn_hW, L2_xattn_hb, L2_xattn_cW, L2_xattn_cb, L2_xattn_qW, L2_xattn_qb, L2_xattn_kW, L2_xattn_kb, L2_xattn_vW, L2_xattn_vb, L2_xattn_oW, L2_xattn_ob, L2_attn_wq, L2_attn_bq, L2_attn_wk, L2_attn_bk, L2_attn_wv, L2_attn_bv, L2_attn_wo, L2_attn_bo, L2_ffn_gate_w, L2_ffn_w1, L2_ffn_w2, L3_xattn_ln1_g, L3_xattn_ln1_b, L3_xattn_ln2_g, L3_xattn_ln2_b, L3_xattn_Wq, L3_xattn_Wkv, L3_xattn_Wo, L3_attn_w_qkvw, L3_attn_w_out, L3_ffn_ln1_g, L3_ffn_ln1_b, L3_ffn_ln2_g, L3_ffn_ln2_b, L3_ffn_Wq, L3_ffn_Wk, L3_ffn_Wv, L3_ffn_Wo, L3_ffn_Wg, L3_ffn_W1, L3_ffn_b1, L3_ffn_W2, L3_ffn_b2):
    import jax
    import jax.numpy as jnp

    def _L0_xattn_ref(Q, K, V, W1, b1, W2, b2, gamma, beta):
        import jax, jax.numpy as jnp
        import numpy as np
        B, R, U, D = (16, 256, 256, 128)
        EPS_ATT = 1e-08
        EPS_LN = 1e-06
        d_model = Q.shape[-1]
        scale = jnp.sqrt(jnp.asarray(d_model, jnp.float32) + EPS_ATT)
        scores = jnp.einsum('brd,bud->bru', Q, K) / scale
        att = jax.nn.softmax(scores, axis=-1)
        V_att = jnp.einsum('bru,bud->brd', att, V)

        def layer_norm(x):
            mu = jnp.mean(x, axis=-1, keepdims=True)
            var = jnp.mean(jnp.square(x - mu), axis=-1, keepdims=True)
            return gamma * (x - mu) / jnp.sqrt(var + EPS_LN) + beta
        X = layer_norm(Q + V_att)
        ffn = jnp.maximum(X @ W1 + b1, 0.0) @ W2 + b2
        return layer_norm(ffn + X)

    def _L0_attn_ref(x, A_log, D_param, W_delta, b_delta, W_B, W_C, W_router, Wg, Wu, Wd, wn_exp, norm_w):
        import jax, jax.numpy as jnp
        import numpy as np
        EPS = 1e-06

        def rmsnorm(x, w):
            rms = jnp.sqrt(jnp.mean(x * x, axis=-1, keepdims=True) + EPS)
            return w * x / rms
        B, L, D = x.shape
        delta = jax.nn.softplus(x @ W_delta + b_delta)
        Bm = x @ W_B
        Cm = x @ W_C
        A = -jnp.exp(A_log)
        S = A.shape[1]
        h0 = jnp.zeros((B, D, S), x.dtype)
        xs = (jnp.moveaxis(x, 1, 0), jnp.moveaxis(delta, 1, 0), jnp.moveaxis(Bm, 1, 0), jnp.moveaxis(Cm, 1, 0))

        def step(h, inp):
            x_t, d_t, B_t, C_t = inp
            bar_A = jnp.exp(jnp.minimum(d_t[..., None] * A, 10.0))
            bar_B = jnp.clip(d_t[..., None] * B_t[:, None, :], -10.0, 10.0)
            h = jnp.clip(bar_A * h + bar_B * x_t[..., None], -10000.0, 10000.0)
            y_t = jnp.sum(h * C_t[:, None, :], axis=-1) + x_t * D_param
            return (h, y_t)
        _, ys = jax.lax.scan(step, h0, xs)
        ssm_out = jnp.moveaxis(ys, 0, 1)
        flat = ssm_out.reshape(-1, D)
        probs = jax.nn.softmax(flat @ W_router, axis=-1)
        w2, idx2 = jax.lax.top_k(probs, 2)
        w2 = w2 / (jnp.sum(w2, axis=-1, keepdims=True) + 1e-09)

        def expert(xf, wg, wu, wd, wn):
            g = jax.nn.silu(xf @ wg) * (xf @ wu)
            g = rmsnorm(g, wn)
            return g @ wd
        all_out = jax.vmap(expert, in_axes=(None, 0, 0, 0, 0))(flat, Wg, Wu, Wd, wn_exp)
        tok = jnp.arange(flat.shape[0])
        moe = w2[:, 0, None] * all_out[idx2[:, 0], tok] + w2[:, 1, None] * all_out[idx2[:, 1], tok]
        out = rmsnorm(ssm_out + moe.reshape(B, L, D), norm_w)
        return out

    def _L0_ffn_ref(x, router_w, router_b, wq, bq, wk, bk, wv, bv, wo, bo):
        import jax, jax.numpy as jnp
        import numpy as np
        B, S, D, H, E = (4, 256, 128, 16, 4)
        b, s, d = x.shape
        e_total = router_w.shape[-1]
        h = H
        hd = d // h
        sm_scale = 0.5
        logits = x @ router_w + router_b
        probs = jax.nn.softmax(logits, axis=-1)
        _, top2 = jax.lax.top_k(probs, 2)
        out = jnp.zeros_like(x)
        bidx = jnp.arange(b)[:, None]
        for e in range(e_total):
            member = (top2 == e).any(-1)
            w_tok = jnp.where(member, probs[..., e], 0.0)
            order = jnp.argsort((~member).astype(jnp.int32), axis=-1, stable=True)
            xg = jnp.take_along_axis(x, order[..., None], axis=1)
            validg = jnp.take_along_axis(member, order, axis=1)
            wg = jnp.take_along_axis(w_tok, order, axis=1)
            q = (xg @ wq[e] + bq[e]).reshape(b, s, h, hd)
            k = (xg @ wk[e] + bk[e]).reshape(b, s, h, hd)
            v = (xg @ wv[e] + bv[e]).reshape(b, s, h, hd)
            att = jnp.einsum('bqhd,bkhd->bhqk', q, k) * sm_scale
            att = jnp.where(validg[:, None, None, :], att, -1000000000.0)
            att = jax.nn.softmax(att, axis=-1)
            y = jnp.einsum('bhqk,bkhd->bqhd', att, v).reshape(b, s, d)
            y = y @ wo[e] + bo[e]
            out = out.at[bidx, order].add(wg[..., None] * y)
        return out

    def _L1_xattn_ref(image_emb, text_emb, edge_index, Wq, bq, Wk, bk, Wv, bv):
        import jax, jax.numpy as jnp
        import numpy as np
        DIM = 128
        D = image_emb.shape[-1]
        scale = D ** (-0.5)
        q = jnp.einsum('bsd,ed->bse', image_emb, Wq) + bq
        k = jnp.einsum('bsd,ed->bse', text_emb, Wk) + bk
        v = jnp.einsum('bsd,ed->bse', text_emb, Wv) + bv
        scores = jnp.einsum('bqd,bkd->bqk', q, k) * scale
        probs = jax.nn.softmax(scores, axis=-1)
        attended = jnp.einsum('bqk,bkd->bqd', probs, v)
        return attended

    def _L1_attn_ref(x, w_q, w_k, w_v, w_o):
        import jax, jax.numpy as jnp
        import numpy as np
        EPS = 1.1920929e-07
        NUM_HEADS = 16
        SOFTCAP = 50.0

        def rms_norm(x):
            return x * jax.lax.rsqrt(jnp.mean(x * x, axis=-1, keepdims=True) + EPS)
        B, S, D = x.shape
        H = NUM_HEADS
        dk = D // H

        def split_heads(y):
            return y.reshape(B, S, H, dk).transpose(0, 2, 1, 3)
        q = split_heads(x @ w_q.T)
        k = split_heads(x @ w_k.T)
        v = split_heads(x @ w_v.T)
        q = rms_norm(q)
        k = rms_norm(k)
        scores = jnp.einsum('bhqd,bhkd->bhqk', q, k) / jnp.sqrt(jnp.float32(dk))
        scores = jnp.tanh(scores / SOFTCAP) * SOFTCAP
        causal = jnp.tril(jnp.ones((S, S), dtype=bool))
        scores = jnp.where(causal[None, None], scores, -jnp.inf)
        probs = jax.nn.softmax(scores, axis=-1)
        y = jnp.einsum('bhqk,bhkd->bhqd', probs, v)
        y = y.transpose(0, 2, 1, 3).reshape(B, S, D)
        return y @ w_o.T

    def _L1_ffn_ref(x, w12, w3, shared_w1, shared_w2, shared_w3, router_w, expert_bias):
        import jax, jax.numpy as jnp
        import numpy as np
        N_EXPERTS = 8
        TOP_K = 2
        D_MODEL = 128
        HIDDEN = 512
        ROUTED_H = 128
        BATCH, SEQ = (2, 512)
        b, s, d = x.shape
        xf = x.reshape(-1, d)
        shared = jax.nn.silu(xf @ shared_w1.T) * (xf @ shared_w2.T) @ shared_w3.T
        scores = jax.nn.sigmoid(xf @ router_w.T)
        _, top_idx = jax.lax.top_k(scores + expert_bias, TOP_K)
        mask = jax.nn.one_hot(top_idx, N_EXPERTS, dtype=xf.dtype).sum(axis=-2)
        gates = scores * mask
        h12 = jnp.einsum('td,ehd->teh', xf, w12)
        h1, h2 = jnp.split(h12, 2, axis=-1)
        h = jax.nn.silu(h1) * h2 * gates[:, :, None]
        routed = jnp.einsum('teh,edh->td', h, w3)
        return (shared + routed).reshape(b, s, d)

    def _L2_xattn_ref(history_features, combined_features, hW, hb, cW, cb, qW, qb, kW, kb, vW, vb, oW, ob):
        import jax, jax.numpy as jnp
        import numpy as np
        B, LQ, LK = (8, 256, 256)
        HIST_DIM, COMB_DIM, FUSION_DIM = (128, 128, 128)

        def _linear_params(key, in_dim, out_dim):
            k1, k2 = jax.random.split(key)
            bound = 1.0 / np.sqrt(in_dim)
            W = jax.random.uniform(k1, (out_dim, in_dim), jnp.float32, -bound, bound)
            b = jax.random.uniform(k2, (out_dim,), jnp.float32, -bound, bound)
            return (W, b)

        def _lin(x, W, b):
            return jnp.einsum('bld,fd->blf', x, W) + b
        h = _lin(history_features, hW, hb)
        c = _lin(combined_features, cW, cb)
        q = _lin(h, qW, qb)
        k = _lin(c, kW, kb)
        v = _lin(c, vW, vb)
        scale = 1.0 / jnp.sqrt(jnp.float32(FUSION_DIM))
        scores = jnp.einsum('bqf,bkf->bqk', q, k) * scale
        attn = jax.nn.softmax(scores, axis=-1)
        attn_out = jnp.einsum('bqk,bkf->bqf', attn, v)
        return _lin(attn_out + q, oW, ob)

    def _L2_attn_ref(x, wq, bq, wk, bk, wv, bv, wo, bo):
        import jax, jax.numpy as jnp
        import numpy as np
        D_MODEL = 128
        N_HEADS = 16
        B, L, D = x.shape
        H = N_HEADS
        d_k = D // H
        scale = 1.0 / np.sqrt(d_k).astype(np.float32)

        def proj(w, b):
            return (x @ w.T + b).reshape(B, L, H, d_k).transpose(0, 2, 1, 3)
        Q = proj(wq, bq)
        K = proj(wk, bk)
        V = proj(wv, bv)
        scores = jnp.einsum('bhqd,bhkd->bhqk', Q, K) * scale
        u = min(L, max(1, int(np.log(L))))
        top_u = jax.lax.top_k(scores.max(axis=-1), u)[1]
        q_sel = jnp.take_along_axis(Q, top_u[..., None], axis=2)
        attn = jax.nn.softmax(jnp.einsum('bhud,bhkd->bhuk', q_sel, K) * scale, axis=-1)
        ctx = jnp.einsum('bhuk,bhkd->bhud', attn, V)
        bi = jnp.arange(B)[:, None, None]
        hi = jnp.arange(H)[None, :, None]
        padded = jnp.zeros((B, H, L, d_k), dtype=x.dtype).at[bi, hi, top_u].set(ctx)
        out = padded.transpose(0, 2, 1, 3).reshape(B, L, D)
        return out @ wo.T + bo

    def _L2_ffn_ref(inputs, gate_w, w1, w2):
        import jax, jax.numpy as jnp
        import numpy as np
        CAPACITY_FACTOR = 1.25
        orig_shape = inputs.shape
        D = orig_shape[-1]
        tokens = inputs.reshape(-1, D)
        T = tokens.shape[0]
        E = gate_w.shape[0]
        C = int(CAPACITY_FACTOR * T / E)
        logits = tokens @ gate_w.T
        probs = jax.nn.softmax(logits, axis=-1)
        expert_idx = jnp.argmax(probs, axis=-1)
        mask = jax.nn.one_hot(expert_idx, E, dtype=jnp.int32)
        locations = jnp.cumsum(mask, axis=0) - 1
        mask = mask * (locations < C)
        loc_oh = jax.nn.one_hot(locations, C, dtype=probs.dtype)
        sec_mask = mask[:, :, None].astype(probs.dtype) * loc_oh
        combine_weights = probs[:, :, None] * sec_mask
        dispatch = jnp.einsum('tec,td->ecd', sec_mask, tokens)
        h = jax.nn.relu(jnp.einsum('ecd,edh->ech', dispatch, w1))
        expert_out = jnp.einsum('ech,ehd->ecd', h, w2)
        ans = jnp.einsum('tec,ecd->td', combine_weights, expert_out)
        return ans.reshape(orig_shape)

    def _L3_xattn_ref(image_embeds, latents, ln1_g, ln1_b, ln2_g, ln2_b, Wq, Wkv, Wo):
        import jax, jax.numpy as jnp
        import numpy as np
        DIM = 128
        DIM_HEAD = 64
        HEADS = 16
        INNER = DIM_HEAD * HEADS
        EPS = 1e-05

        def layer_norm(x, g, b):
            m = jnp.mean(x, axis=-1, keepdims=True)
            v = jnp.mean(jnp.square(x - m), axis=-1, keepdims=True)
            return (x - m) * jax.lax.rsqrt(v + EPS) * g + b
        B, S_lat, _ = latents.shape
        x = layer_norm(image_embeds, ln1_g, ln1_b)
        l = layer_norm(latents, ln2_g, ln2_b)
        q = l @ Wq
        kv_in = jnp.concatenate([x, l], axis=1)
        kv = kv_in @ Wkv
        k, v = jnp.split(kv, 2, axis=-1)

        def to_heads(t):
            return t.reshape(t.shape[0], t.shape[1], HEADS, DIM_HEAD).transpose(0, 2, 1, 3)
        q, k, v = (to_heads(q), to_heads(k), to_heads(v))
        scale = 1.0 / np.sqrt(np.sqrt(DIM_HEAD))
        w = jnp.einsum('bhqd,bhkd->bhqk', q * scale, k * scale)
        w = jax.nn.softmax(w.astype(jnp.float32), axis=-1).astype(q.dtype)
        out = jnp.einsum('bhqk,bhkd->bhqd', w, v)
        out = out.transpose(0, 2, 1, 3).reshape(B, S_lat, INNER)
        return out @ Wo

    def _L3_attn_ref(x, w_qkvw, w_out):
        import jax, jax.numpy as jnp
        import numpy as np
        H = 16
        G = 4
        DIM = 128
        HD = DIM // H // G
        B, S, dim = x.shape
        qkvw = x @ w_qkvw
        chunks = jnp.split(qkvw, G, axis=-1)
        subs = [jnp.split(t, G, axis=-1) for t in chunks]
        q = jnp.concatenate([subs[i][0] for i in range(4)], axis=0)
        k = jnp.concatenate([subs[i][1] for i in range(4)], axis=0)
        v = jnp.concatenate([subs[i][2] for i in range(4)], axis=0)
        w = jnp.concatenate([subs[i][3] for i in range(4)], axis=0)

        def shp(t):
            return t.reshape(B * G, H, -1, HD).swapaxes(1, 2)
        q, k, v = (shp(q), shp(k), shp(v))
        w = w.reshape(B * G, H, -1, HD)
        scale = HD ** (-0.5)
        scores = q @ k.swapaxes(-2, -1) * scale
        attn = jax.nn.softmax(scores, axis=-1)
        o = (attn @ v).swapaxes(1, 2).reshape(B, S, dim)
        return o * w.reshape(B, S, dim) @ w_out

    def _L3_ffn_ref(x, ln1_g, ln1_b, ln2_g, ln2_b, Wq, Wk, Wv, Wo, Wg, W1, b1, W2, b2):
        import jax, jax.numpy as jnp
        import numpy as np
        B, S, D, H, E, F, K = (2, 128, 128, 16, 8, 512, 2)
        EPS = 1e-05

        def _layernorm(x, g, b):
            mu = jnp.mean(x, axis=-1, keepdims=True)
            var = jnp.mean(jnp.square(x - mu), axis=-1, keepdims=True)
            return (x - mu) * jax.lax.rsqrt(var + EPS) * g + b
        Bb, Ss, Dd = x.shape
        Dh = Dd // H
        h = _layernorm(x, ln1_g, ln1_b)
        q = (h @ Wq).reshape(Bb, Ss, H, Dh)
        k = (h @ Wk).reshape(Bb, Ss, H, Dh)
        v = (h @ Wv).reshape(Bb, Ss, H, Dh)
        scores = jnp.einsum('bqhd,bkhd->bhqk', q, k) / jnp.sqrt(jnp.float32(Dh))
        attn = jax.nn.softmax(scores, axis=-1)
        ctx = jnp.einsum('bhqk,bkhd->bqhd', attn, v).reshape(Bb, Ss, Dd)
        x = x + ctx @ Wo
        m = _layernorm(x, ln2_g, ln2_b)
        xt = m.reshape(-1, Dd)
        T = xt.shape[0]
        probs = jax.nn.softmax(xt @ Wg, axis=-1)
        wts, idx = jax.lax.top_k(probs, K)
        wts = wts / jnp.sum(wts, axis=-1, keepdims=True)
        h1 = jax.nn.gelu(jnp.einsum('td,edf->etf', xt, W1) + b1[:, None, :])
        ye = jnp.einsum('etf,efd->etd', h1, W2) + b2[:, None, :]
        sel = ye[idx, jnp.arange(T)[:, None], :]
        moe_out = jnp.sum(wts[..., None] * sel, axis=1).reshape(Bb, Ss, Dd)
        return x + moe_out
    x = x + _L0_xattn_ref(_layernorm(x, axis=-1), ctx_1024, ctx_1024, L0_xattn_W1, L0_xattn_b1, L0_xattn_W2, L0_xattn_b2, L0_xattn_gamma, L0_xattn_beta)
    x = x + _L0_attn_ref(_layernorm(x, axis=-1), L0_attn_A_log, L0_attn_D_param, L0_attn_W_delta, L0_attn_b_delta, L0_attn_W_B, L0_attn_W_C, L0_attn_W_router, L0_attn_Wg, L0_attn_Wu, L0_attn_Wd, L0_attn_wn_exp, L0_attn_norm_w)
    x = x + _L0_ffn_ref(_layernorm(x, axis=-1), L0_ffn_router_w, L0_ffn_router_b, L0_ffn_wq, L0_ffn_bq, L0_ffn_wk, L0_ffn_bk, L0_ffn_wv, L0_ffn_bv, L0_ffn_wo, L0_ffn_bo)
    x = x + _L1_xattn_ref(_layernorm(x, axis=-1), ctx_1024, L1_xattn_edge_index, L1_xattn_Wq, L1_xattn_bq, L1_xattn_Wk, L1_xattn_bk, L1_xattn_Wv, L1_xattn_bv)
    x = x + _L1_attn_ref(_layernorm(x, axis=-1), L1_attn_w_q, L1_attn_w_k, L1_attn_w_v, L1_attn_w_o)
    x = x + _L1_ffn_ref(_layernorm(x, axis=-1), L1_ffn_w12, L1_ffn_w3, L1_ffn_shared_w1, L1_ffn_shared_w2, L1_ffn_shared_w3, L1_ffn_router_w, L1_ffn_expert_bias)
    x = x + _L2_xattn_ref(_layernorm(x, axis=-1), ctx_1024, L2_xattn_hW, L2_xattn_hb, L2_xattn_cW, L2_xattn_cb, L2_xattn_qW, L2_xattn_qb, L2_xattn_kW, L2_xattn_kb, L2_xattn_vW, L2_xattn_vb, L2_xattn_oW, L2_xattn_ob)
    x = x + _L2_attn_ref(_layernorm(x, axis=-1), L2_attn_wq, L2_attn_bq, L2_attn_wk, L2_attn_bk, L2_attn_wv, L2_attn_bv, L2_attn_wo, L2_attn_bo)
    x = x + _L2_ffn_ref(_layernorm(x, axis=-1), L2_ffn_gate_w, L2_ffn_w1, L2_ffn_w2)
    x = x + _L3_xattn_ref(ctx_1024, _layernorm(x, axis=-1), L3_xattn_ln1_g, L3_xattn_ln1_b, L3_xattn_ln2_g, L3_xattn_ln2_b, L3_xattn_Wq, L3_xattn_Wkv, L3_xattn_Wo)
    x = x + _L3_attn_ref(_layernorm(x, axis=-1), L3_attn_w_qkvw, L3_attn_w_out)
    x = x + _L3_ffn_ref(_layernorm(x, axis=-1), L3_ffn_ln1_g, L3_ffn_ln1_b, L3_ffn_ln2_g, L3_ffn_ln2_b, L3_ffn_Wq, L3_ffn_Wk, L3_ffn_Wv, L3_ffn_Wo, L3_ffn_Wg, L3_ffn_W1, L3_ffn_b1, L3_ffn_W2, L3_ffn_b2)
    return x

_drawn_inputs = setup_inputs


def setup_inputs(seed=0):
    import zlib

    import numpy as np

    out = dict(_drawn_inputs(seed))
    spreads = {'L0_xattn_b1': (0.0, 0.1),
     'L0_xattn_b2': (0.0, 0.1),
     'L0_xattn_gamma': (1.0, 0.2),
     'L0_xattn_beta': (0.0, 0.1),
     'L0_attn_D_param': (1.0, 0.2),
     'L0_attn_b_delta': (0.0, 0.75),
     'L0_attn_wn_exp': (1.0, 0.6),
     'L0_attn_norm_w': (1.0, 0.2),
     'L0_ffn_router_b': (0.0, 0.8),
     'L0_ffn_bq': (0.0, 0.8),
     'L0_ffn_bk': (0.0, 2.0),
     'L0_ffn_bv': (0.0, 0.8),
     'L0_ffn_bo': (0.0, 0.453),
     'L1_xattn_bq': (0.0, 0.756),
     'L1_xattn_bk': (0.0, 2.0),
     'L1_xattn_bv': (0.0, 0.1),
     'L1_ffn_expert_bias': (0.0, 0.8),
     'L2_attn_bq': (0.0, 0.416),
     'L2_attn_bk': (0.0, 0.395),
     'L2_attn_bv': (0.0, 0.8),
     'L2_attn_bo': (0.0, 0.1),
     'L3_xattn_ln1_g': (1.0, 0.2),
     'L3_xattn_ln1_b': (0.0, 0.1),
     'L3_xattn_ln2_g': (1.0, 0.2),
     'L3_xattn_ln2_b': (0.0, 0.329),
     'L3_ffn_ln1_g': (1.0, 0.6),
     'L3_ffn_ln1_b': (0.0, 0.8),
     'L3_ffn_ln2_g': (1.0, 0.6),
     'L3_ffn_ln2_b': (0.0, 0.8),
     'L3_ffn_b1': (0.0, 0.8),
     'L3_ffn_b2': (0.0, 1.353)}
    factors = {'L0_attn_A_log': 4.716,
     'L0_attn_W_delta': 3.384,
     'L0_ffn_router_w': 4.45,
     'L0_ffn_wq': 8.0,
     'L0_ffn_wk': 8.0,
     'L0_ffn_wv': 8.0,
     'L0_ffn_wo': 8.0,
     'L1_attn_w_q': 7.441,
     'L1_attn_w_k': 7.778,
     'L1_attn_w_v': 4.646,
     'L1_attn_w_o': 4.886,
     'L1_ffn_w12': 8.0,
     'L1_ffn_w3': 8.0,
     'L1_ffn_shared_w1': 8.0,
     'L1_ffn_shared_w2': 8.0,
     'L1_ffn_shared_w3': 7.931,
     'L1_ffn_router_w': 8.0,
     'L2_xattn_hb': 7.891,
     'L2_xattn_cb': 7.718,
     'L2_xattn_qb': 4.656,
     'L2_xattn_kW': 8.0,
     'L2_xattn_kb': 64.0,
     'L2_xattn_vb': 4.923,
     'L2_xattn_ob': 2.861,
     'L3_attn_w_qkvw': 8.0,
     'L3_attn_w_out': 8.0,
     'L3_ffn_Wq': 8.0,
     'L3_ffn_Wk': 8.0,
     'L3_ffn_Wv': 7.154,
     'L3_ffn_Wo': 7.274,
     'L3_ffn_Wg': 3.406,
     'L3_ffn_W1': 6.212,
     'L3_ffn_W2': 5.63}
    for name, (base, spread) in spreads.items():
        noise = np.random.default_rng([zlib.crc32(name.encode()), seed]).standard_normal(out[name].shape)
        drawn = base * np.exp(spread * noise) if base else spread * noise
        out[name] = jnp.asarray(drawn.astype(out[name].dtype))
    for name, factor in factors.items():
        out[name] = (out[name] * factor).astype(out[name].dtype)
    return out
```

```python
from contextlib import ExitStack

import numpy as np

import concourse.bass as bass
from concourse import mybir

F32 = mybir.dt.float32
BF16 = mybir.dt.bfloat16
I32 = mybir.dt.int32
ALU = mybir.AluOpType
ACT = mybir.ActivationFunctionType
AXX = mybir.AxisListType.X

P = 128
NB, S, D = 64, 32, 128
NTOK = NB * S
NT = NTOK // P
BT = P // S
NQ = 4
QW = NTOK // NQ
U = 257
UA = U - 1
H, HD = 16, 8
HG = 4
NG = H // HG
BIG = 1.0e30
LAYERS = range(12)


class Lane:

    def __init__(self, sem):
        self.sem, self.n, self.steps, self.waited = sem, 0, [], {}

    @property
    def last(self):
        return (self.sem, self.n)

    def wait(self, marks):
        for m in marks:
            if m is None:
                continue
            if isinstance(m, list):
                self.wait(m)
                continue
            sem, value = m
            if value > self.waited.get(id(sem), 0):
                self.waited[id(sem)] = value
                self.steps.append(lambda e, sem=sem, value=value: e.wait_ge(sem, value))

    def do(self, fn, marks=()):
        self.wait(marks)
        self.n += 1
        self.steps.append(lambda e: fn(e).then_inc(self.sem, 1))
        return self.last

    def quiet(self, fn, marks=()):
        self.wait(marks)
        self.steps.append(fn)

    def play(self, engine):
        for step in self.steps:
            step(engine)


class Arrivals:

    def __init__(self, sem):
        self.sem, self.total = sem, 0

    @property
    def mark(self):
        return (self.sem, self.total)


def transfer(lane, out, in_, arrivals, *marks):
    lane.wait(marks)
    arrivals.total += 16
    lane.steps.append(lambda e: e.dma_start(out, in_).then_inc(arrivals.sem, 16))
    return arrivals.mark


class Region:

    def __init__(self, arena, lo, hi):
        self.arena, self.at, self.hi = arena, lo, hi

    def take(self, *shape, parts=P):
        n = int(np.prod(shape))
        lo = self.at
        self.at += n
        assert self.at <= self.hi, ("region full", self.at, self.hi)
        ap = self.arena[0:parts, lo:lo + n]
        if len(shape) == 2:
            ap = ap.rearrange("p (a b) -> p a b", a=shape[0])
        if len(shape) == 3:
            ap = ap.rearrange("p (a b c) -> p a b c", a=shape[0], b=shape[1])
        return ap


L0_PACK = [("x0_W1", D), ("x0_W2", D), ("x0_b1", 1), ("x0_b2", D), ("x0_gamma", D), ("x0_beta", D),
           ("a0_A", 16), ("a0_D", 1), ("a0_Wdelta", D), ("a0_bdelta", 1), ("a0_WB", 16), ("a0_WC", 16),
           ("a0_Wr", 4), ("a0_Wg", 4 * 256), ("a0_Wu", 4 * 256), ("a0_Wd", 4 * 2 * D), ("a0_wn", 8),
           ("a0_normw", D),
           ("f0_rw", 4), ("f0_rb", 4), ("f0_wq", 4 * D), ("f0_wk", 4 * D), ("f0_wv", 4 * D), ("f0_wo", 4 * D),
           ("f0_bq", 4), ("f0_bk", 4), ("f0_bv", 4), ("f0_bo", 4 * D)]
MID_PACK = [("x1_WqT", D), ("x1_Wk", D), ("x1_WvT", D), ("x1_bq", 1), ("x1_bk", 1), ("x1_bv", D),
            ("a1_wqT", D), ("a1_wkT", D), ("a1_wvT", D), ("a1_woT", D),
            ("f1_w12T", 8 * 256), ("f1_w3T", 8 * D), ("f1_s1T", 512), ("f1_s2T", 512), ("f1_s3T", 4 * D),
            ("f1_rwT", 8), ("f1_eb", 8),
            ("x2_hWT", D), ("x2_cW", D), ("x2_cWT", D), ("x2_qWT", D), ("x2_kW", D), ("x2_kWT", D),
            ("x2_vWT", D), ("x2_oWT", D),
            ("x2_hb", 1), ("x2_cb", 1), ("x2_qb", 1), ("x2_kb", 1), ("x2_vb", 1), ("x2_ob", D),
            ("a2_wqT", D), ("a2_wkT", D), ("a2_wvT", D), ("a2_woT", D), ("a2_bq", 1), ("a2_bk", 1),
            ("a2_bv", D), ("a2_bo", D), ("f2_gwT", 16)]
LATE_PACK = [("x3_g1", D), ("x3_b1", D), ("x3_g2", D), ("x3_b2", D),
             ("x3_left", 2048), ("x3_right", 2048),
             ("a3_w", 512), ("a3_wo", D),
             ("f3_g1", D), ("f3_b1", D), ("f3_g2", D), ("f3_b2", D),
             ("f3_Wq", D), ("f3_Wk", D), ("f3_Wv", D), ("f3_Wo", D), ("f3_Wg", 8),
             ("f3_W1", 8 * 512), ("f3_b1f", 8 * 4), ("f3_W2", 8 * 4 * D), ("f3_bo", D)]
CONST_PACK = [("ident", P), ("ones", P), ("upto", P), ("block", P), ("headmask", HG), ("rowmask", BT),
              ("causal", S), ("ramp", S), ("rowid", S), ("slotbase", 16), ("minus_half", 1)]


def width(pack):
    return sum(w for _, w in pack)


def columns(pack, ap):
    out, at = {}, 0
    for name, w in pack:
        out[name] = ap[:, at:at + w]
        at += w
    return out


def program(nc, t, out):
    with ExitStack() as stack:
        def sem(name):
            return stack.enter_context(nc.semaphore(name))

        ARENA = 53200
        arena = stack.enter_context(nc.sbuf_tensor("arena", [P, ARENA], F32))
        PS = stack.enter_context(nc.psum_tensor("PS", [P, 8, 512], F32))

        PE, V, A, G, SP = (Lane(sem(f"s_{n}")) for n in ("pe", "dve", "act", "pool", "sp"))
        lanes = (PE, V, A, G, SP)

        keep = Region(arena, 0, 7200)
        X, XN = keep.take(NT, D), keep.take(NT, D)
        XT = keep.take(NTOK)
        const_words = keep.take(width(CONST_PACK))
        C = columns(CONST_PACK, const_words)
        LATE_LO = keep.hi
        MID_LO = LATE_LO + width(LATE_PACK)
        MID_HI = MID_LO + width(MID_PACK)
        W0_LO = ARENA - width(L0_PACK)
        scratch = {0: (LATE_LO, W0_LO), 1: (LATE_LO, W0_LO), 2: (MID_HI, W0_LO)}
        for n in range(3, 9):
            scratch[n] = (MID_HI, ARENA)
        for n in range(9, 12):
            scratch[n] = (MID_LO, ARENA)
        w0_words, mid_words, late_words = arena[:, W0_LO:ARENA], arena[:, MID_LO:MID_HI], arena[:, LATE_LO:MID_LO]
        W = {**columns(L0_PACK, w0_words), **columns(MID_PACK, mid_words), **columns(LATE_PACK, late_words)}

        free = [[] for _ in range(8)]
        turn = {"at": 0}

        def bank():
            b = turn["at"] = (turn["at"] + 1) % 8
            return b, free[b]

        def hibank():
            b = turn["at"] = 4 + (turn["at"] + 1) % 4
            return b, free[b]

        def barrier():
            marks = [lane.last for lane in lanes if lane is not SP]
            for lane in lanes:
                lane.wait(marks)
            for f in free:
                f.clear()

        def tt(lane, o, a, b, op, *marks, chain=True):
            return lane.do(lambda e: e.tensor_tensor(o, a, b, op), [*marks, lane.last if chain else None])

        def ts(lane, o, a, s1, s2, op0, op1, *marks, chain=True):
            marks = [*marks, lane.last if chain else None]
            if op1 is None:
                return lane.do(lambda e: e.tensor_scalar(o, a, s1, None, op0), marks)
            return lane.do(lambda e: e.tensor_scalar(o, a, s1, s2, op0, op1), marks)

        def stt(o, a, s, b, op0, op1, *marks, chain=True):
            return V.do(lambda e: e.scalar_tensor_tensor(out=o, in0=a, scalar=s, in1=b, op0=op0, op1=op1),
                        [*marks, V.last if chain else None])

        def red(o, a, op, *marks, chain=True):
            return V.do(lambda e: e.tensor_reduce(o, a, AXX, op), [*marks, V.last if chain else None])

        def recip(o, a, *marks):
            return V.do(lambda e: e.reciprocal(o, a), [*marks, V.last])

        def root(x, ready):
            half = C["minus_half"][0:x.shape[0]]
            for ax in range(2, len(x.shape)):
                half = half.unsqueeze(ax)
            return tt(G, x, x, half.broadcast_to(list(x.shape)), ALU.pow, ready)

        def inverse_root(x):
            m = root(x, V.last)
            V.wait([m])
            return m

        def copy(lane, o, a, *marks, chain=False):
            marks = [*marks, lane.last if chain else None]
            if lane is A:
                return A.do(lambda e: e.copy(o, a), marks)
            return lane.do(lambda e: e.tensor_copy(o, a), marks)

        def act(o, a, func, *marks, chain=False, **kw):
            return A.do(lambda e: e.activation(o, a, func, **kw), [*marks, A.last if chain else None])

        def mm(o, l, r, *marks, start=True, stop=True, mark=False, check=True):
            fn = (lambda e: e.matmul(o, l, r, start=start, stop=stop, skip_group_check=not check))
            return PE.do(fn, marks) if mark else PE.quiet(fn, marks)

        def tr(o, a, *marks, mark=False):
            n = a.shape[0]
            fn = (lambda e: e.transpose(o, a, C["ident"][0:n, 0:n]))
            return PE.do(fn, marks) if mark else PE.quiet(fn, marks)

        def spread(ap, shape, *axes):
            for ax in axes:
                ap = ap.unsqueeze(ax)
            return ap.broadcast_to(shape)

        def over_rows(ap):
            return spread(ap, [P, NT, D], 1)

        def per_token(ap, n=NT, w=D):
            return spread(ap, [P, n, w], 2)

        def normalise(dst, src, eps, small, ready=(), gamma=None, beta=None):
            done = []
            stats, mv = small[:, :, 0:6], small[:, :, 6:8]
            for q in range(NQ):
                V.wait(ready[q] if ready else [])
                for t_ in range(4 * q, 4 * q + 4):
                    m = V.do(lambda e, t_=t_: e.bn_stats(stats[:, t_, :], src[:, t_, :]), [V.last if t_ == 4 * q else None])
                for t_ in range(4 * q, 4 * q + 4):
                    m = V.do(lambda e, t_=t_: e.bn_aggr(mv[:, t_, :], stats[:, t_, :]), [m])
                var = quarter(mv, q)[:, :, 1]
                v = ts(V, var, var, eps, None, ALU.add, None, m)
                done.append(root(var, v))
            for q in range(NQ):
                V.wait([done[q]])
                for t_ in range(4 * q, 4 * q + 4):
                    m = ts(V, dst[:, t_, :], src[:, t_, :], mv[:, t_, 0:1], mv[:, t_, 1:2], ALU.subtract, ALU.mult,
                           chain=False)
                if gamma is not None:
                    tt(V, quarter(dst, q), quarter(dst, q), spread(gamma, [P, 4, D], 1), ALU.mult)
                    m = tt(V, quarter(dst, q), quarter(dst, q), spread(beta, [P, 4, D], 1), ALU.add)
                done[q] = m
            return done

        def rows_to_cols(dst, src, ready, nextbank=bank, by_position=False):
            done = []
            for q in range(NQ):
                b, freed = nextbank()
                for j in range(4):
                    m = tr(PS[:, b, P * j:P * j + P], src[:, 4 * q + j, :], freed, ready[q], mark=j == 3)
                lane = (A, V)[q % 2]
                o, i = dst[:, QW * q:QW * q + QW], PS[:, b, :]
                if by_position:
                    nb = NB // NQ
                    o = dst.rearrange("p (h r b) -> p b h r", b=NB, r=2)[:, nb * q:nb * q + nb]
                    i = i.rearrange("p (b h r) -> p b h r", b=nb, r=2)
                m = copy(lane, o, i, m)
                free[b] = [m]
                done.append(m)
            return done

        def cols_to_rows(dst, src, ready, nextbank=bank):
            done = []
            for q in range(NQ):
                b, freed = nextbank()
                for j in range(4):
                    at = QW * q + P * j
                    m = tr(PS[:, b, P * j:P * j + P], src[:, at:at + P], freed, ready[q], mark=j == 3)
                lane = (A, V)[q % 2]
                m = copy(lane, dst[:, 4 * q:4 * q + 4, :], PS[:, b, :].rearrange("p (a d) -> p a d", a=4), m)
                free[b] = [m]
                done.append(m)
            return done

        def linear_cols(dst, w, src, ready, bias=None, nextbank=bank):
            done = []
            for q in range(NQ):
                b, freed = nextbank()
                n = dst.shape[0]
                m = mm(PS[0:n, b, :], w, src[:, QW * q:QW * q + QW], freed, ready[q], mark=True)
                o, i = dst[:, QW * q:QW * q + QW], PS[0:n, b, :]
                if bias is None:
                    m = copy((A, V)[q % 2], o, i, m)
                elif q % 2:
                    m = ts(V, o, i, bias, None, ALU.add, None, m, chain=False)
                else:
                    m = act(o, i, ACT.Identity, m, bias=bias)
                free[b] = [m]
                done.append(m)
            return done

        def linear_rows(src, w, ready, take, nextbank=bank):
            n = w.shape[-1]
            done = []
            for q in range(NQ):
                b, freed = nextbank()
                for j in range(4):
                    at = QW * q + P * j
                    m = mm(PS[:, b, n * j:n * j + n], src[:, at:at + P], w, freed, ready[q], mark=j == 3)
                m = take(q, PS[:, b, 0:4 * n].rearrange("p (a d) -> p a d", a=4), m)
                free[b] = [m]
                done.append(m)
            return done

        def quarter(ap, q):
            return ap[:, 4 * q:4 * q + 4, :]

        def to_rows(dst, bias=None, base=None):
            def take(q, ps, m):
                if bias is not None:
                    m = tt(V, quarter(dst, q), ps, spread(bias, [P, 4, ps.shape[-1]], 1), ALU.add, m)
                    if base is not None:
                        m = tt(V, quarter(dst, q), quarter(dst, q), quarter(base, q), ALU.add, m)
                elif base is not None:
                    m = tt(V, quarter(dst, q), ps, quarter(base, q), ALU.add, m)
                else:
                    m = copy((A, V)[q % 2], quarter(dst, q), ps, m)
                return m
            return take

        def softmax_rows(x, e, small, *marks):
            wide = [P, NT, e]
            red(small, x, ALU.max, *marks)
            m = tt(V, x, x, spread(small, wide, 2), ALU.subtract)
            m = act(x, x, ACT.Exp, m)
            red(small, x, ALU.add, m)
            recip(small, small)
            return tt(V, x, x, spread(small, wide, 2), ALU.mult)

        def pick_largest(sel, v, rows, n, k, room, *marks):
            r = Region(room.arena, room.at, room.hi)
            key, hit = r.take(rows, n), r.take(rows, n)
            top, first = r.take(rows), r.take(rows)
            wide = [P, rows, n]
            ramp = spread(C["ramp"][:, 0:n], wide, 1)
            V.wait(marks)
            for i in range(k):
                red(top, v, ALU.max)
                tt(V, key, v, spread(top, wide, 2), ALU.is_equal)
                tt(V, key, key, ramp, ALU.mult)
                red(first, key, ALU.max)
                tgt = sel if i == 0 else hit
                m = tt(V, tgt, key, spread(first, wide, 2), ALU.is_equal)
                if i + 1 < k:
                    stt(v, tgt, -BIG, v, ALU.mult, ALU.add)
                if i:
                    m = tt(V, sel, sel, hit, ALU.add)
            return m

        NS_CTX = 4
        key_slots = [Arrivals(sem(f"s_ctx_keys{i}")) for i in range(NS_CTX)]
        row_slots = [Arrivals(sem(f"s_ctx_rows{i}")) for i in range(NS_CTX)]

        def cross_attention(room, qT, ready, scale, O, row_term=None, then=None):
            NS = NS_CTX
            kT = [room.take(BT * U) for _ in range(NS)]
            kR = [room.take(BT * 2, D) for _ in range(NS)]
            kL = [room.take(D, parts=BT) for _ in range(NS)]
            pr = [room.take(U) for _ in range(2)]
            lastp = [room.take(BT) for _ in range(2)]
            pT = [room.take(2 * P) for _ in range(2)]
            pL = [room.take(P, parts=BT) for _ in range(2)]
            st = [room.take(4) for _ in range(3)]
            tile_done, turned, summed = {}, {}, {}

            def load_keys(i, *marks):
                if i < NT:
                    keys_in[i] = transfer(SP, kT[i % NS], t["ctxT"][i], key_slots[i % NS], *marks)

            def load_rows(i, *marks):
                if i < NT:
                    a = row_slots[i % NS]
                    transfer(SP, kR[i % NS], t["ctxR"][i].rearrange("p (a d) -> p a d", d=D), a, *marks)
                    rows_in[i] = transfer(SP, kL[i % NS], t["ctxL"][i], a)

            keys_in, rows_in = {}, {}
            for i in range(NS):
                load_keys(i)
                load_rows(i)
            if then is not None:
                then()

            def scores(i):
                s, h = i % NS, i % 2
                b, freed = bank()
                for j in range(BT):
                    m = mm(PS[S * j:S * j + S, b, 0:U], qT[:, P * i + S * j:P * i + S * j + S],
                           kT[s][:, U * j:U * j + U], freed, ready[i // 4], keys_in[i], start=True,
                           stop=row_term is None, mark=j == BT - 1)
                if row_term is not None:
                    m = mm(PS[:, b, 0:U], row_term[:, P * i:P * i + P], C["ones_row"], start=False, stop=True, mark=True)
                load_keys(i + NS, m)
                mx, nm, sm, rs = (st[i % 3][:, k:k + 1] for k in range(4))
                red(mx, PS[:, b, 0:U], ALU.max, m)
                m = ts(V, nm, mx, -scale, None, ALU.mult, None)
                m = act(pr[h], PS[:, b, 0:U], ACT.Exp, m, turned.get(i - 2), bias=nm, scale=scale, accum_out=sm)
                free[b] = [m]
                return m

            def turn(i, m):
                h = i % 2
                recip(st[i % 3][:, 3:4], st[i % 3][:, 2:3], m)
                alone = tt(V, lastp[h], pr[h][:, UA:U].broadcast_to([P, BT]), C["rowmask"], ALU.mult)
                b, freed = bank()
                for j in range(2):
                    x = tr(PS[:, b, P * j:P * j + P], pr[h][:, P * j:P * j + P], freed, m, mark=j == 1)
                c0 = copy(A, pT[h], PS[:, b, 0:2 * P], x, summed.get(i - 2))
                free[b] = [c0]
                b, freed = bank()
                x = tr(PS[0:BT, b, 0:P], lastp[h], freed, alone, mark=True)
                c1 = copy(V, pL[h], PS[0:BT, b, 0:P], x, summed.get(i - 2))
                free[b] = [c1]
                turned[i] = x
                return [c0, c1]

            def sums(i, marks):
                s, h = i % NS, i % 2
                b, freed = bank()
                for j in range(BT):
                    for k in range(2):
                        mm(PS[S * j:S * j + S, b, 0:D], pT[h][:, P * k + S * j:P * k + S * j + S],
                           kR[s][:, 2 * j + k, :], freed, marks, rows_in[i], start=k == 0, stop=False)
                m = mm(PS[:, b, 0:D], pL[h], kL[s], start=False, stop=True, mark=True)
                summed[i] = [m]
                load_rows(i + NS, m)
                m = ts(V, O[:, i, :], PS[:, b, 0:D], st[i % 3][:, 3:4], None, ALU.mult, None, m)
                free[b] = [m]
                tile_done[i] = m

            exps, copies = {0: scores(0)}, {}
            for i in range(NT + 1):
                if i + 1 < NT:
                    exps[i + 1] = scores(i + 1)
                if i < NT:
                    copies[i] = turn(i, exps.pop(i))
                if i:
                    sums(i - 1, copies.pop(i - 1))
            return [tile_done[4 * q + 3] for q in range(NQ)]

        def repeat(dst, xT, i, *marks):
            d4 = dst.rearrange("p (b h k) -> p b h k", b=BT, h=HG)
            x3 = xT[:, P * i:P * i + P].rearrange("p (b k) -> p b k", b=BT)
            return copy(G, d4, spread(x3, [P, BT, HG, S], 2), *marks)

        def head_attention(room, qT, kT, ready, xT, wv, scale, OT, *, key_mask=None, softcap=None,
                           bias_col=None, bias_row=None, choose=None, repeated=None):
            keepall = choose is not None
            NK = 3
            kB = [room.take(BT * HG * S) for _ in range(NK)]
            if repeated is None:
                xR = [room.take(BT * HG * S) for _ in range(3)]
            pr = [room.take(H, S) for _ in range(NT if keepall else 3)]
            pT = [room.take(NG * P) for _ in range(2)]
            vB = [room.take(BT * D) for _ in range(3)]
            mx, sm = room.take(NT, H), room.take(NT, H)
            kb_used, pt_used, vb_used, pr_used, xr_used = {}, {}, {}, {}, {}
            s_used = [free[g] for g in range(NG)]
            st = {}
            pend_av = {}

            def spread_keys(i):
                src = kT[:, P * i:P * i + P].rearrange("p (b k) -> p b k", b=BT)
                dst = kB[i % NK].rearrange("p (b h k) -> p b h k", b=BT, h=HG)
                for b in range(BT):
                    m = tt(G, dst[:, b], spread(src[:, b, :], [P, HG, S], 1),
                           spread(C["headmask"], [P, HG, S], 2), ALU.mult,
                           ready[i // 4], kb_used.get(i - NK), chain=False)
                return m

            def scores(i):
                m = st.pop(("k", i))
                c = 0
                for g in range(NG):
                    for b in range(BT):
                        at = P * i + S * b
                        r = slice(S * g, S * g + S)
                        k = mm(PS[S * b:S * b + S, g, c:c + P], qT[r, at:at + S], kB[i % NK][r, P * b:P * b + P], m,
                               s_used, start=True, stop=key_mask is None, mark=(g, b) == (NG - 1, BT - 1))
                kb_used[i] = k
                for g in range(NG if key_mask is not None else 0):
                    k = mm(PS[:, g, c:c + P], C["block"], spread(key_mask(i), [P, HG, S], 1), start=False, stop=True,
                           mark=g == NG - 1)
                sc = PS[:, 0:NG, c:c + P].rearrange("p g (h k) -> p g h k", h=HG)
                p = pr[i % len(pr)]
                p4 = p.rearrange("p (g h) k -> p g h k", g=NG)
                m4 = mx[:, i, :].rearrange("p (g h) -> p g h", g=NG)
                if softcap is not None:
                    m = None
                    for g in range(NG):
                        m = act(p4[:, g], sc[:, g], ACT.Tanh, k, pr_used.get(i - len(pr)), scale=scale / softcap)
                    s_used[:] = [m]
                    stt(p, p, softcap, spread(C["causal"], [P, H, S], 1), ALU.mult, ALU.add, m)
                    red(mx[:, i, :], p, ALU.max)
                    m = tt(V, p, p, spread(mx[:, i, :], [P, H, S], 2), ALU.subtract)
                    m = act(p, p, ACT.Exp, m)
                else:
                    red(m4, sc, ALU.max, k)
                    m = tt(V, p4, sc, spread(m4, [P, NG, HG, S], 3), ALU.subtract, pr_used.get(i - len(pr)))
                    s_used[:] = [m]
                    m = act(p, p, ACT.Exp, m, scale=scale)
                return m

            def repeat_tokens(i):
                if repeated is not None:
                    return repeated[i]
                return xR[i % 3], repeat(xR[i % 3], xT, i, ready[i // 4], xr_used.get(i - 3))

            def values(i):
                xr, xm = st.pop(("x", i))
                b, freed = hibank()
                for j in range(BT):
                    m = mm(PS[:, b, D * j:D * j + D], xr[:, P * j:P * j + P], wv, freed, xm,
                           start=True, stop=bias_row is None, mark=j == BT - 1)
                    if bias_row is not None:
                        m = mm(PS[:, b, D * j:D * j + D], C["ones"][0:1, :], bias_row, start=False, stop=True,
                               mark=j == BT - 1)
                xr_used[i] = m
                m = tt(V, vB[i % 3].rearrange("p (g h d) -> p g h d", h=HG, d=HD),
                       PS[:, b, :].rearrange("p (g h d) -> p g h d", h=HG, d=HD),
                       spread(spread(C["rowmask"], [P, BT * NG, HG], 1), [P, BT * NG, HG, HD], 3), ALU.mult,
                       m, vb_used.get(i - 3), chain=False)
                free[b] = [m]
                return m

            def total(i, m):
                red(sm[:, i, :], pr[i % len(pr)], ALU.add, m)
                return recip(sm[:, i, :], sm[:, i, :])

            def normal(i, m):
                p = pr[i % len(pr)]
                return tt(G, p, p, spread(sm[:, i, :], [P, H, S], 2), ALU.mult, m)

            def turn_weights(i, m):
                b, freed = hibank()
                p = pr[i % len(pr)].rearrange("p (g h) k -> p g (h k)", g=NG)
                for g in range(NG):
                    m = tr(PS[:, b, P * g:P * g + P], p[:, g, :], freed, m, mark=g == NG - 1)
                pr_used[i] = m
                m = copy(A, pT[i % 2], PS[:, b, :], m, pt_used.get(i - 2))
                free[b] = [m]
                return m

            def average(i, m):
                b, freed = hibank()
                for j in range(BT):
                    for g in range(NG):
                        k = mm(PS[S * g:S * g + S, b, S * j:S * j + S], vB[i % 3][:, D * j + S * g:D * j + S * g + S],
                               pT[i % 2][:, P * g + S * j:P * g + S * j + S], freed, m, st[("v", i)],
                               mark=(j, g) == (BT - 1, NG - 1))
                pt_used[i] = vb_used[i] = k
                o = OT[:, P * i:P * i + P]
                m = copy(A, o, PS[:, b, 0:P], k) if bias_col is None else \
                    act(o, PS[:, b, 0:P], ACT.Identity, k, bias=bias_col)
                free[b] = [m]
                pend_av[i] = m

            if not keepall:
                def keys_ahead(i):
                    if i < NT:
                        st[("k", i)] = spread_keys(i)
                        st[("x", i)] = repeat_tokens(i)

                keys_ahead(0)
                keys_ahead(1)
                for i in range(NT + 2):
                    if 0 <= i - 1 < NT:
                        m = total(i - 1, st.pop(("p", i - 1)))
                        st[("n", i - 1)] = normal(i - 1, m)
                    keys_ahead(i + 2)
                    if i < NT:
                        st[("p", i)] = scores(i)
                        st[("v", i)] = values(i)
                    if 0 <= i - 1 < NT:
                        st[("t", i - 1)] = turn_weights(i - 1, st.pop(("n", i - 1)))
                    if 0 <= i - 2 < NT:
                        average(i - 2, st.pop(("t", i - 2)))
            else:
                st[("k", 0)] = spread_keys(0)
                for i in range(NT + 1):
                    if i + 1 < NT:
                        st[("k", i + 1)] = spread_keys(i + 1)
                    if i < NT:
                        st[("p", i)] = scores(i)
                    if i:
                        red(sm[:, i - 1, :], pr[i - 1], ALU.add, st.pop(("p", i - 1)))
                chosen = choose(mx, sm)
                for i in range(NT + 1):
                    if i < NT:
                        st[("x", i)] = repeat_tokens(i)
                        st[("v", i)] = values(i)
                        st[("t", i)] = turn_weights(i, normal(i, chosen))
                    if i >= 1:
                        average(i - 1, st.pop(("t", i - 1)))
            for g in range(NG):
                free[g] = list(s_used)
            return [pend_av[4 * q + 3] for q in range(NQ)]

        arrived = {n: Arrivals(sem(f"s_{n}")) for n in ("const", "x", "w0", "mid", "late", "scratch", "scattered", "gathered", "out")}
        transfer(SP, X, t["x"].rearrange("(t p) d -> p t d", p=P), arrived["x"])
        transfer(SP, const_words, t["const"], arrived["const"])

        def load_first_weights():
            transfer(SP, w0_words, t["w0"], arrived["w0"])

        if min(LAYERS) > 0:
            load_first_weights()
        for lane in (PE, V, A, G):
            lane.wait([arrived["const"].mark, arrived["x"].mark])
        C["ones_row"] = keep.take(U, parts=1)
        ones_row = V.do(lambda e: e.memset(C["ones_row"], 1.0))
        PE.wait([ones_row])

        def start_layer(room, eps=1e-5, by_position=False):
            m = normalise(XN, X, eps, Region(arena, room.hi - 8 * NT, room.hi).take(NT, 8))
            return rows_to_cols(XT, XN, m, by_position=by_position)

        def L0_xattn(room):
            xt = start_layer(room)
            O = room.take(NT, D)
            o = cross_attention(room, XT, xt, 1.0 / float(np.sqrt(np.float32(D) + np.float32(1e-8))), O,
                                then=load_first_weights)
            for lane in (PE, V, A, G):
                lane.wait([arrived["w0"].mark])
            tmp, small = room.take(NT, D), room.take(NT, 8)
            m = tt(V, O, O, XN, ALU.add, *o)
            m = normalise(O, O, 1e-6, small, [[m]] * NQ, gamma=W["x0_gamma"], beta=W["x0_beta"])
            oT, hT = room.take(NTOK), room.take(NTOK)
            ot = rows_to_cols(oT, O, m)
            done = []
            for q in range(NQ):
                b, freed = bank()
                m = mm(PS[:, b, :], W["x0_W1"], oT[:, QW * q:QW * q + QW], freed, ot[q], mark=True)
                m = act(hT[:, QW * q:QW * q + QW], PS[:, b, :], ACT.Relu, m, bias=W["x0_b1"])
                free[b] = [m]
                done.append(m)
            f = linear_rows(hT, W["x0_W2"], done, to_rows(tmp, bias=W["x0_b2"], base=O))
            normalise(O, tmp, 1e-6, small, [[a, b, V.last] for a, b in zip(f, ot)], gamma=W["x0_gamma"], beta=W["x0_beta"])
            tt(V, X, X, O, ALU.add)

        def L0_attn(room):
            SN, E, F = 16, 4, 256
            CH = 512
            NBC = CH // S
            xt = start_layer(room)
            delta, negA = room.take(NTOK), room.take(SN)
            G.wait(xt), V.wait(xt), A.wait(xt)
            m = act(negA, W["a0_A"], ACT.Exp)
            ts(V, negA, negA, -1.0, None, ALU.mult, None, m)
            dab = room.take(NTOK)
            for q in range(NQ):
                b, freed = bank()
                c = slice(QW * q, QW * q + QW)
                m = mm(PS[:, b, :], W["a0_Wdelta"], XT[:, c], freed, xt[q], mark=True)
                m = ts(V, delta[:, c], PS[:, b, :], W["a0_bdelta"], None, ALU.add, None, m)
                free[b] = [m]
                m = act(dab[:, c], delta[:, c], ACT.Abs, m)
                m = act(dab[:, c], dab[:, c], ACT.Exp, m, scale=-1.0)
                m = act(dab[:, c], dab[:, c], ACT.Ln, m, bias=1.0)
                dm = stt(delta[:, c], delta[:, c], 0.0, dab[:, c], ALU.max, ALU.add, m)
            yT = dab
            Ab = [room.take(SN, CH) for _ in range(2)]
            Ub = [room.take(SN, CH) for _ in range(2)]
            hs = room.take(NBC, SN)
            a_used, u_used = [[], []], [[], []]

            def prepare(c):
                col = slice(CH * c, CH * c + CH)
                for s in range(SN):
                    a = act(Ab[c % 2][:, s, :], delta[:, col], ACT.Exp, dm, V.last if c == 0 else None,
                            a_used[c % 2], scale=negA[:, s:s + 1])
                    b, freed = bank()
                    m = mm(PS[:, b, :], W["a0_WB"][:, s:s + 1].broadcast_to([P, P]), XT[:, col], freed, mark=True)
                    u = Ub[c % 2][:, s, :]
                    m = tt(V, u, PS[:, b, :], delta[:, col], ALU.mult, m, u_used[c % 2])
                    free[b] = [m]
                    m = ts(V, u, u, -10.0, 10.0, ALU.max, ALU.min)
                    g = tt(G, u, u, XT[:, col], ALU.mult, m, chain=False)
                return [a, g]

            def scan(c, ready):
                a4 = Ab[c % 2].rearrange("p s (b t) -> p t b s", t=S)
                u4 = Ub[c % 2].rearrange("p s (b t) -> p t b s", t=S)
                for t_ in range(S):
                    if t_:
                        tt(V, hs, u4[:, t_ - 1], a4[:, t_], ALU.mult, *ready)
                        tt(V, hs, hs, u4[:, t_], ALU.add)
                        m = ts(V, u4[:, t_], hs, -1.0e4, 1.0e4, ALU.max, ALU.min)
                    else:
                        m = ts(V, u4[:, 0], u4[:, 0], -1.0e4, 1.0e4, ALU.max, ALU.min, *ready)
                a_used[c % 2] = [m]
                return m

            def read_out(c, m):
                col = slice(CH * c, CH * c + CH)
                yb, yfree = c % 2, free[c % 2]
                for s in range(SN):
                    b, freed = 2 + s % 6, free[2 + s % 6]
                    k = mm(PS[:, b, :], W["a0_WC"][:, s:s + 1].broadcast_to([P, P]), XT[:, col], freed, mark=True)
                    u = Ub[c % 2][:, s, :]
                    k = tt(V, u, PS[:, b, :], u, ALU.mult, k, m)
                    free[b] = [k]
                    st_[("r", s)] = k
                    if s:
                        add(c, s - 1, yb, yfree)
                m = add(c, SN - 1, yb, yfree)
                u_used[c % 2] = [m]
                m = stt(yT[:, col], XT[:, col], W["a0_D"], PS[:, yb, :], ALU.mult, ALU.add, m)
                free[yb] = [m]
                return m

            st_ = {}

            def add(c, s, yb, yfree):
                return mm(PS[:, yb, :], C["ident"], Ub[c % 2][:, s, :], yfree, st_[("r", s)],
                          start=s == 0, stop=s == SN - 1, mark=s == SN - 1)

            ys = []
            ready = prepare(0)
            for c in range(NTOK // CH):
                m = scan(c, ready)
                if c + 1 < NTOK // CH:
                    ready = prepare(c + 1)
                ys.append(read_out(c, m))

            barrier()
            room = Region(arena, LATE_LO + 2 * NTOK + SN, room.hi)
            y = room.take(NT, D)
            yr = cols_to_rows(y, yT, ys)
            probs, small, sel, work = room.take(NT, E), room.take(NT), room.take(NT, E), room.take(NT, E)
            lg = linear_rows(yT, W["a0_Wr"], ys, to_rows(probs))
            m = softmax_rows(probs, E, small, *lg)
            copy(V, work, probs, m, chain=True)
            pick_largest(sel, work, NT, E, 2, room)
            tt(V, probs, probs, sel, ALU.mult)
            red(small, probs, ALU.add)
            ts(V, small, small, 1e-9, None, ALU.add, None)
            recip(small, small)
            tt(V, probs, probs, spread(small, [P, NT, E], 2), ALU.mult)
            room.take(200)
            ms, gate = room.take(NT), room.take(NT)
            acc, tmp = room.take(NT, D), [room.take(4, D) for _ in range(2)]
            sg = [room.take(2, QW) for _ in range(2)]
            gT = [room.take(2, QW) for _ in range(2)]
            sq = [room.take(2, QW) for _ in range(2)]
            wd = room.take(E * 2, D)
            for i in range(E * 2):
                wd_m = ts(V, wd[:, i, :], W["a0_Wd"][:, D * i:D * i + D], W["a0_wn"][:, i:i + 1], None, ALU.mult, None)
            acc_m = copy(V, acc, y, *yr, chain=True)
            gT_used, sq_used, tmp_used = [[], []], [[], []], [[], []]
            n = 0
            for e in range(E):
                for q in range(NQ):
                    k2 = n % 2
                    n += 1
                    col = slice(QW * q, QW * q + QW)
                    for f in range(2):
                        b1, f1 = bank()
                        at = F * e + P * f
                        m1 = mm(PS[:, b1, :], W["a0_Wg"][:, at:at + P], yT[:, col], f1, ys[q], mark=True)
                        b2, f2 = bank()
                        m2 = mm(PS[:, b2, :], W["a0_Wu"][:, at:at + P], yT[:, col], f2, mark=True)
                        m = act(sg[k2][:, f, :], PS[:, b1, :], ACT.Silu, m1, gT_used[k2])
                        free[b1] = [m]
                        gm = tt(V, gT[k2][:, f, :], PS[:, b2, :], sg[k2][:, f, :], ALU.mult, m, m2, gT_used[k2])
                        free[b2] = [gm]
                        sm_ = tt(G, sq[k2][:, f, :], gT[k2][:, f, :], gT[k2][:, f, :], ALU.mult, gm, sq_used[k2],
                                 chain=False)
                    b1, f1 = bank()
                    b2, f2 = bank()
                    for j in range(4):
                        for f in range(2):
                            c = slice(P * j, P * j + P)
                            mm(PS[:, b2, D * j:D * j + D], gT[k2][:, f, c], wd[:, 2 * e + f, :], f2, gm, wd_m,
                               start=f == 0, stop=f == 1)
                    for j in range(4):
                        for f in range(2):
                            c = slice(P * j, P * j + P)
                            m = mm(PS[:, b1, j:j + 1], sq[k2][:, f, c], C["ones"][:, 0:1], f1, sm_, start=f == 0,
                                   stop=f == 1, mark=(j, f) == (3, 1))
                    gT_used[k2] = sq_used[k2] = [m]
                    ms_q, gt_q = ms[:, 4 * q:4 * q + 4], gate[:, 4 * q:4 * q + 4]
                    m = ts(V, ms_q, PS[:, b1, 0:4], 1.0 / F, 1e-6, ALU.mult, ALU.add, m)
                    free[b1] = [m]
                    inverse_root(ms_q)
                    tt(V, gt_q, ms_q, probs[:, 4 * q:4 * q + 4, e], ALU.mult)
                    m = tt(V, tmp[k2], PS[:, b2, :].rearrange("p (a d) -> p a d", a=4),
                           spread(gt_q, [P, 4, D], 2), ALU.mult, tmp_used[k2])
                    free[b2] = [m]
                    am = tt(G, quarter(acc, q), quarter(acc, q), tmp[k2], ALU.add, m, acc_m)
                    tmp_used[k2] = [am]
            sqr = y
            m = act(sqr, acc, ACT.Square, am)
            red(ms, sqr, ALU.add, m)
            ts(V, ms, ms, 1.0 / D, 1e-6, ALU.mult, ALU.add)
            inverse_root(ms)
            tt(V, acc, acc, per_token(ms), ALU.mult)
            tt(V, acc, acc, over_rows(W["a0_normw"]), ALU.mult)
            tt(V, X, X, acc, ALU.add)

        def L0_ffn(room):
            E = 4
            xt = start_layer(room)
            probs, small, sel, work = room.take(NT, E), room.take(NT), room.take(NT, E), room.take(NT, E)
            lg = linear_rows(XT, W["f0_rw"], xt, to_rows(probs, bias=W["f0_rb"]))
            m = softmax_rows(probs, E, small, *lg)
            copy(V, work, probs, m, chain=True)
            pick_largest(sel, work, NT, E, 2, room)
            tt(V, probs, probs, sel, ALU.mult)
            m = ts(V, sel, sel, 1.0e9, -1.0e9, ALU.mult, ALU.add)
            diag = room.take(NT, S)
            qT, kT, OT = room.take(NTOK), room.take(NTOK), room.take(NTOK)
            tmp = [room.take(4, D) for _ in range(2)]
            tmp_used = [[], []]
            late_room = Region(arena, LATE_LO, MID_LO)
            xR = [late_room.take(BT * HG * S) for _ in range(NT)]
            repeated = [(xR[i], repeat(xR[i], XT, i, xt[i // 4])) for i in range(NT)]
            at = room.at
            for e in range(E):
                r = Region(arena, at, room.hi)
                c = slice(D * e, D * e + D)
                dm = tt(V, diag, spread(C["rowid"], [P, NT, S], 1), spread(sel[:, :, e], [P, NT, S], 2), ALU.mult)
                qm = linear_cols(qT, W["f0_wq"][:, c], XT, xt, bias=W["f0_bq"][:, e:e + 1])
                km = linear_cols(kT, W["f0_wk"][:, c], XT, xt, bias=W["f0_bk"][:, e:e + 1])
                om = head_attention(r, qT, kT, [[a, b, dm] for a, b in zip(qm, km)], XT, W["f0_wv"][:, c], 0.5, OT,
                                    key_mask=lambda i: diag[:, i, :], bias_col=W["f0_bv"][:, e:e + 1],
                                    repeated=repeated)

                def take(q, ps, m, e=e, c=c):
                    w = tmp[q % 2]
                    m = tt(V, w, ps, spread(W["f0_bo"][:, c], [P, 4, D], 1), ALU.add, m, tmp_used[q % 2])
                    m2 = tt(V, w, w, spread(probs[:, 4 * q:4 * q + 4, e], [P, 4, D], 2), ALU.mult)
                    tmp_used[q % 2] = [tt(G, quarter(X, q), quarter(X, q), w, ALU.add, m2)]
                    return m
                linear_rows(OT, W["f0_wo"][:, c], om, take)
                barrier()

        def L1_xattn(room):
            xt = start_layer(room)
            qT, kqT, qb = room.take(NTOK), room.take(NTOK), room.take(NTOK, parts=1)
            qm = linear_cols(qT, W["x1_WqT"], XT, xt, bias=W["x1_bq"])
            km = linear_cols(kqT, W["x1_Wk"], qT, qm)
            bm = linear_cols(qb, W["x1_bk"], qT, qm)
            O = room.take(NT, D)
            o = cross_attention(room, kqT, [[a, b] for a, b in zip(km, bm)], float(D) ** -0.5, O, row_term=qb)
            ot = rows_to_cols(qT, O, o)
            linear_rows(qT, W["x1_WvT"], ot, add_to_x(W["x1_bv"], room))

        def add_to_x(bias, room):
            tmp = [room.take(4, D) for _ in range(2)] if bias is not None else None

            def take(q, ps, m):
                if bias is None:
                    return tt(V, quarter(X, q), ps, quarter(X, q), ALU.add, m)
                m = tt(V, tmp[q % 2], ps, spread(bias, [P, 4, D], 1), ALU.add, m)
                tt(V, quarter(X, q), quarter(X, q), tmp[q % 2], ALU.add)
                return m
            return take

        def L1_attn(room):
            xt = start_layer(room)
            qr = room.take(NT, D)
            sq, ms = room.take(NT, D), room.take(NT, H)
            qT, kT = room.take(NTOK), room.take(NTOK)
            for w, dst in (("a1_wqT", qT), ("a1_wkT", kT)):
                m = linear_rows(XT, W[w], [[a, PE.last] for a in xt], to_rows(qr))
                m = act(sq, qr, ACT.Square, *m)
                red(ms.rearrange("p t h -> p (t h)"), sq.rearrange("p t (h d) -> p (t h) d", d=HD), ALU.add, m)
                m = ts(V, ms, ms, 1.0 / HD, 1.1920929e-07, ALU.mult, ALU.add)
                m = act(ms, ms, ACT.Sqrt, m)
                recip(ms, ms, m)
                m = tt(V, qr.rearrange("p t (h d) -> p (t h) d", d=HD), qr.rearrange("p t (h d) -> p (t h) d", d=HD),
                       spread(ms.rearrange("p t h -> p (t h)"), [P, NT * H, HD], 2), ALU.mult)
                done = rows_to_cols(dst, qr, [m] * NQ)
                A.wait(done), V.wait(done)
            OT = room.take(NTOK)
            om = head_attention(room, qT, kT, [[done]] * NQ, XT, W["a1_wvT"], float(1.0 / np.sqrt(np.float32(HD))), OT,
                                softcap=50.0)
            linear_rows(OT, W["a1_woT"], om, add_to_x(None, room))

        def gated_experts(room, experts, add_gate, n_hidden, hidden, down):
            hT = [room.take(n_hidden, QW) for _ in range(2)]
            tmp = [room.take(4, D) for _ in range(2)]
            h_used, tmp_used = [[], []], [[], []]
            pend = None

            def finish(e, q, k2, m):
                b, freed = bank()
                for j in range(4):
                    for f in range(n_hidden):
                        k = mm(PS[:, b, D * j:D * j + D], hT[k2][:, f, P * j:P * j + P], down(e, f), freed, *m,
                               start=f == 0, stop=f == n_hidden - 1, mark=(j, f) == (3, n_hidden - 1))
                h_used[k2] = [k]
                ps = PS[:, b, :].rearrange("p (a d) -> p a d", a=4)
                g = add_gate(e, q)
                if g is None:
                    k = copy(V, tmp[k2], ps, k, tmp_used[k2])
                else:
                    k = tt(V, tmp[k2], ps, spread(g, [P, 4, D], 2), ALU.mult, k, tmp_used[k2])
                free[b] = [k]
                tmp_used[k2] = [tt(G, quarter(X, q), quarter(X, q), tmp[k2], ALU.add, k)]

            n = 0
            for e in experts:
                for q in range(NQ):
                    k2 = n % 2
                    n += 1
                    ms = [hidden(e, q, f, hT[k2][:, f, :], h_used[k2]) for f in range(n_hidden)]
                    if pend is not None:
                        finish(*pend)
                    pend = (e, q, k2, ms)
            finish(*pend)

        def L1_ffn(room):
            E, HS = 8, 512
            xt = start_layer(room)
            sc, sel, work = room.take(NT, E), room.take(NT, E), room.take(NT, E)
            lg = linear_rows(XT, W["f1_rwT"], xt, to_rows(sc))
            m = act(sc, sc, ACT.Exp, *lg, scale=-1.0)
            ts(V, sc, sc, 1.0, None, ALU.add, None, m)
            recip(sc, sc)
            tt(V, work, sc, spread(W["f1_eb"], [P, NT, E], 1), ALU.add)
            pick_largest(sel, work, NT, E, 2, room)
            gm = tt(V, sc, sc, sel, ALU.mult)
            room.take(600)
            sg = [room.take(QW) for _ in range(3)]
            sg_used = [[] for _ in range(3)]
            turns = {"n": 0}

            def hidden(e, q, f, dst, marks):
                if e < E:
                    w1 = W["f1_w12T"][:, 256 * e:256 * e + P]
                    w2 = W["f1_w12T"][:, 256 * e + P:256 * e + 2 * P]
                else:
                    at = P * (4 * (e - E) + f)
                    w1, w2 = W["f1_s1T"][:, at:at + P], W["f1_s2T"][:, at:at + P]
                col = slice(QW * q, QW * q + QW)
                k = turns["n"] % 3
                turns["n"] += 1
                b1, f1 = bank()
                m1 = mm(PS[:, b1, :], w1, XT[:, col], f1, xt[q], mark=True)
                b2, f2 = bank()
                m2 = mm(PS[:, b2, :], w2, XT[:, col], f2, mark=True)
                m = act(sg[k], PS[:, b1, :], ACT.Silu, m1, sg_used[k])
                free[b1] = [m]
                m = tt(V, dst, PS[:, b2, :], sg[k], ALU.mult, m, m2, marks, chain=False)
                free[b2] = [m]
                sg_used[k] = [m]
                return m

            G.wait([gm])
            r = Region(arena, room.at, room.hi)
            gated_experts(r, range(E), lambda e, q: sc[:, 4 * q:4 * q + 4, e], 1, hidden,
                          lambda e, f: W["f1_w3T"][:, D * e:D * e + D])
            G.wait([PE.last])
            gated_experts(r, [E], lambda e, q: None, HS // P, hidden,
                          lambda e, f: W["f1_s3T"][:, D * f:D * f + D])

        def L2_xattn(room):
            xt = start_layer(room)
            hT, qT, cqT = room.take(NTOK), room.take(NTOK), room.take(NTOK)
            qb, kc = room.take(NTOK, parts=1), room.take(1)
            hm = linear_cols(hT, W["x2_hWT"], XT, xt, bias=W["x2_hb"])
            qm = linear_cols(qT, W["x2_qWT"], hT, hm, bias=W["x2_qb"])
            b, freed = bank()
            m = mm(PS[:, b, 0:1], W["x2_kWT"], W["x2_cb"], freed, mark=True)
            kcm = tt(V, kc, PS[:, b, 0:1], W["x2_kb"], ALU.add, m)
            free[b] = [kcm]
            km = linear_cols(hT, W["x2_kW"], qT, [[a, qm[-1]] for a in qm])
            cm = linear_cols(cqT, W["x2_cW"], hT, km)
            bm = linear_cols(qb, kc, qT, [[a, kcm] for a in qm])
            O = room.take(NT, D)
            o = cross_attention(room, cqT, [[a, b] for a, b in zip(cm, bm)], float(1.0 / np.sqrt(np.float32(D))), O,
                                row_term=qb)
            ot = rows_to_cols(cqT, O, o)
            c1 = linear_cols(hT, W["x2_cWT"], cqT, ot, bias=W["x2_cb"])
            v1 = linear_cols(cqT, W["x2_vWT"], hT, [[a, c1[-1]] for a in c1], bias=W["x2_vb"])
            m = tt(V, cqT, cqT, qT, ALU.add, *v1)
            linear_rows(cqT, W["x2_oWT"], [m] * NQ, add_to_x(W["x2_ob"], room))

        def L2_attn(room):
            KEEP = min(S, max(1, int(np.log(S))))
            xt = start_layer(room)
            qT, kT = room.take(NTOK), room.take(NTOK)
            qm = linear_cols(qT, W["a2_wqT"], XT, xt, bias=W["a2_bq"])
            km = linear_cols(kT, W["a2_wkT"], XT, xt, bias=W["a2_bk"])

            def choose(mx, sm):
                r = Region(arena, room.at, room.hi)
                v, sel = r.take(2 * BT, S), r.take(2 * BT, S)
                mf = mx.rearrange("p t h -> p (t h)")
                b, freed = hibank()
                for g in range(2):
                    m = tr(PS[:, b, P * g:P * g + P], mf[:, P * g:P * g + P], freed, V.last, mark=g == 1)
                m = copy(V, v, PS[:, b, 0:2 * P].rearrange("p (a s) -> p a s", s=S), m, chain=True)
                free[b] = [m]
                m = pick_largest(sel, v, 2 * BT, S, KEEP, r)
                b, freed = hibank()
                sf = sel.rearrange("p a s -> p (a s)")
                for g in range(2):
                    m = tr(PS[:, b, P * g:P * g + P], sf[:, P * g:P * g + P], freed, m, mark=g == 1)
                recip(sm, sm)
                smf = sm.rearrange("p t h -> p (t h)")
                m = tt(V, smf, smf, PS[:, b, 0:2 * P], ALU.mult, m)
                free[b] = [m]
                return m

            OT = room.take(NTOK)
            om = head_attention(room, qT, kT, [[a, b] for a, b in zip(qm, km)], XT, W["a2_wvT"],
                                float(np.float32(1.0) / np.sqrt(np.float32(HD))), OT, bias_row=W["a2_bv"][0:1, :],
                                choose=choose)
            linear_rows(OT, W["a2_woT"], om, add_to_x(W["a2_bo"], room))

        def L2_ffn(room):
            E, F = 16, 512
            CAP = int(1.25 * NTOK / E)
            NSLOT = E * CAP
            xt = start_layer(room)
            probs, small, sel, work = room.take(NT, E), room.take(NT), room.take(NT, E), room.take(NT, E)
            zero = room.take(NSLOT // P * D)
            wslot = [(room.take(4 * P), room.take(4 * D)) for _ in range(4)]
            w_used = [[] for _ in range(4)]
            w_arr = [Arrivals(sem(f"s_w2_{i}")) for i in range(4)]

            def load(e):
                k = e % 4
                transfer(SP, wslot[k][0], t["f2_w1"][e], w_arr[k], *w_used[k])
                return transfer(SP, wslot[k][1], t["f2_w2"][e], w_arr[k])

            m = V.do(lambda e: e.memset(zero, 0.0))
            zeroed = transfer(SP, t["slots_in"].rearrange("(p a) d -> p (a d)", p=P), zero, arrived["scratch"], m)
            w_landed = {e: load(e) for e in range(4)}
            lg = linear_rows(XT, W["f2_gwT"], xt, to_rows(probs))
            m = softmax_rows(probs, E, small, *lg)
            copy(V, work, probs, m, chain=True)
            pick_largest(sel, work, NT, E, 1, room)
            room.take(1200)
            selh = room.take(NT * E // 2).bitcast(BF16)
            upto, ones = room.take(P // 2).bitcast(BF16), room.take(P // 2).bitcast(BF16)
            copy(V, selh, sel.rearrange("p t e -> p (t e)"), chain=True)
            before, other = room.take(NT, E), room.take(NT, E)
            V.do(lambda e: e.memset(before[:, 0:1, :], 0.0))
            copy(V, before[:, 1:NT, :], sel[:, 0:NT - 1, :])
            d = 1
            while d < NT:
                copy(V, other[:, 0:d, :], before[:, 0:d, :], chain=True)
                tt(V, other[:, d:NT, :], before[:, d:NT, :], before[:, 0:NT - d, :], ALU.add)
                before, other, d = other, before, 2 * d
            beforeh = room.take(NT * E // 2).bitcast(BF16)
            copy(V, beforeh, before.rearrange("p t e -> p (t e)"), chain=True)
            copy(V, upto, C["upto"])
            m = copy(V, ones, C["ones"])
            b, freed = bank()
            mm(PS[:, b, 0:NT * E], upto, selh, freed, m, start=True, stop=False)
            m = mm(PS[:, b, 0:NT * E], ones, beforeh, start=False, stop=True, mark=True)
            loc = PS[:, b, 0:NT * E].rearrange("p (t e) -> p t e", e=E)
            fit = work
            ts(V, fit, loc, float(CAP) + 0.5, None, ALU.is_lt, None, m)
            tt(V, fit, fit, sel, ALU.mult)
            place = sel
            m = stt(place, loc, -1.0, spread(C["slotbase"], [P, NT, E], 1), ALU.add, ALU.add)
            free[b] = [m]
            ts(V, place, place, -float(2 * NSLOT), None, ALU.add, None)
            tt(V, place, place, fit, ALU.mult)
            slotf, slot, gate = room.take(NT), room.take(NT).bitcast(I32), room.take(NT)
            red(slotf, place, ALU.add)
            ts(V, slotf, slotf, float(2 * NSLOT), None, ALU.add, None)
            sm_ = copy(V, slot, slotf, chain=True)
            tt(V, probs, probs, fit, ALU.mult)
            gm = red(gate, probs, ALU.add)
            slot_u = slot.bitcast(mybir.dt.uint32)
            back = room.take(NT, D)
            m0 = V.do(lambda e: e.memset(back, 0.0))
            G.wait([sm_, zeroed, m0])
            for i in range(NT):
                G.steps.append(lambda e, i=i: e.indirect_dma_start(
                    t["slots_in"][:, :], bass.IndirectOffsetOnAxis(ap=slot_u[:, i:i + 1], axis=0), XN[:, i, :], None,
                    bounds_check=NSLOT - 1, oob_is_err=False).then_inc(arrived["scattered"].sem, 16))
                arrived["scattered"].total += 16
            NST = NSLOT // P
            rows = room.take(NST, D)
            got = transfer(SP, rows, t["slots_in"].rearrange("(a p) d -> p a d", p=P), arrived["scratch"],
                           arrived["scattered"].mark)
            sT = room.take(NSLOT)
            turned = []
            for a in range(NST // 4):
                b, freed = bank()
                for j in range(4):
                    m = tr(PS[:, b, P * j:P * j + P], rows[:, 4 * a + j, :], freed, got, mark=j == 3)
                m = copy((A, V)[a % 2], sT[:, 512 * a:512 * a + 512], PS[:, b, :], m)
                free[b] = [m]
                turned.append(m)
            HC = CAP // 2
            hT = [room.take(4, CAP) for _ in range(2)]
            yo = [room.take(2, D, parts=HC) for _ in range(2)]
            h_used, y_used = [[], []], [[], []]
            y_arr = [Arrivals(sem(f"s_y2_{i}")) for i in range(2)]
            for e in range(E):
                k, k2 = e % 4, e % 2
                w1, w2 = wslot[k]
                c = slice(CAP * e, CAP * e + CAP)
                for f in range(4):
                    b, freed = bank()
                    m = mm(PS[:, b, 0:CAP], w1[:, P * f:P * f + P], sT[:, c], freed, w_landed[e], *turned, mark=True)
                    m = act(hT[k2][:, f, :], PS[:, b, 0:CAP], ACT.Relu, m, h_used[k2])
                    free[b] = [m]
                b, freed = bank()
                for j in range(2):
                    for f in range(4):
                        m2 = mm(PS[0:HC, b, D * j:D * j + D], hT[k2][:, f, HC * j:HC * j + HC],
                                w2[:, D * f:D * f + D], freed, m, start=f == 0, stop=f == 3, mark=(j, f) == (1, 3))
                h_used[k2] = w_used[k] = [m2]
                m = copy(V, yo[k2], PS[0:HC, b, 0:2 * D].rearrange("p (a d) -> p a d", a=2), m2, y_used[k2])
                free[b] = [m]
                y_used[k2] = [transfer(SP, t["slots_out"][c, :].rearrange("(a p) d -> p a d", p=HC), yo[k2],
                                       y_arr[k2], m)]
                if e + 4 < E:
                    w_landed[e + 4] = load(e + 4)
            G.wait([y_arr[0].mark, y_arr[1].mark])
            for i in range(NT):
                G.steps.append(lambda e, i=i: e.indirect_dma_start(
                    back[:, i, :], None, t["slots_out"][:, :], bass.IndirectOffsetOnAxis(ap=slot_u[:, i:i + 1], axis=0),
                    bounds_check=NSLOT - 1, oob_is_err=False).then_inc(arrived["gathered"].sem, 16))
                arrived["gathered"].total += 16
            V.wait([arrived["gathered"].mark])
            tt(V, back, back, per_token(gate), ALU.mult)
            tt(V, X, X, back, ALU.add)

        def L3_xattn(room):
            NH, DH = 16, 64
            UL = U + S
            lat, small = XN, room.take(NT, 8)
            xt0 = normalise(XN, X, 1e-5, small)
            lm = normalise(lat, XN, 1e-5, small, [[m] for m in xt0], gamma=W["x3_g2"], beta=W["x3_b2"])
            lt = rows_to_cols(XT, lat, lm)
            n3 = S + 1
            v3 = room.take(NB, D, parts=n3)
            last, lsq, lst = room.take(D, parts=NB), room.take(D, parts=NB), room.take(2, parts=NB)
            lastT = room.take(NB)
            a = arrived["scratch"]
            wrote = transfer(SP, t["lat_rows"].rearrange("(t p) d -> p t d", p=P), lat, a, *lm)
            transfer(SP, last, t["ctx_last"], a)
            V.wait([a.mark])
            g1, b1 = W["x3_g1"], W["x3_b1"]

            def norm_small(x, sq, st2, n):
                m = red(st2[:, 0:1], x, ALU.add)
                ts(V, st2[:, 0:1], st2[:, 0:1], -1.0 / D, None, ALU.mult, None)
                ts(V, x, x, st2[:, 0:1], None, ALU.add, None)
                tt(V, sq, x, x, ALU.mult)
                red(st2[:, 1:2], sq, ALU.add)
                ts(V, st2[:, 1:2], st2[:, 1:2], 1.0 / D, 1e-5, ALU.mult, ALU.add)
                inverse_root(st2[:, 1:2])
                stt(x, x, st2[:, 1:2], g1[0:n, :], ALU.mult, ALU.mult)
                return tt(V, x, x, b1[0:n, :], ALU.add)

            m = norm_small(last, lsq, lst, NB)
            wl = transfer(SP, t["last_rows"], last, a, m)
            transfer(SP, v3[0:S], t["lat_rows"].rearrange("(b s) d -> s b d", s=S), a, a.mark)
            v3m = transfer(SP, v3[S:n3], t["last_rows"].rearrange("b d -> (b d)").unsqueeze(0).rearrange(
                "o (b d) -> o b d", d=D), a)
            b, freed = bank()
            m = tr(PS[:, b, 0:NB], last, freed, m, mark=True)
            lastTm = copy(V, lastT, PS[:, b, 0:NB], m)
            free[b] = [lastTm]
            qk, vo = room.take(NH, D), room.take(NH, D)
            for dst, half in ((qk, slice(0, DH)), (vo, slice(DH, 2 * DH))):
                for g in range(4):
                    b, freed = bank()
                    for j in range(4):
                        h = 4 * g + j
                        m = mm(PS[:, b, P * j:P * j + P], W["x3_left"][half, P * h:P * h + P],
                               W["x3_right"][half, P * h:P * h + P],
                               freed, mark=j == 3)
                    m = copy((A, V)[g % 2], dst[:, 4 * g:4 * g + 4, :], PS[:, b, :].rearrange("p (a d) -> p a d", a=4), m)
                    free[b] = [m]
                    PE.wait([m])
            NS = 2
            kr = [room.take(BT * 2, D) for _ in range(NS)]
            kst = room.take(BT * 2, 8)
            kt = [room.take(BT, UL) for _ in range(NS)]
            qt = [W[f"x3_{side}"].rearrange("p (b n) -> p b n", b=BT) for side in ("left", "right")]
            spent = PE.last
            pr = [room.take(4, UL) for _ in range(2)]
            pT = [room.take(3, NH * S) for _ in range(2)]
            oT = [room.take(NH, P) for _ in range(2)]
            st = room.take(2, 16)
            kr_used, kt_used, qt_used = [[], []], [[], []], [[spent], [spent]]
            oT_used, pT_used, pr_used = [[], []], [[], []], [[], []]
            s_used = [free[g] for g in range(4)]
            scale = float(1.0 / np.sqrt(np.float32(DH)))
            arr = row_slots

            def load(i):
                return transfer(SP, kr[i % NS], t["ctxR"][i].rearrange("p (a d) -> p a d", d=D), arr[i % NS],
                                *kr_used[i % NS])

            landed = {i: load(i) for i in range(NS)}

            def key_stats(i):
                k = kr[i % NS]
                V.wait([landed[i]])
                for j in range(BT * 2):
                    V.do(lambda e, j=j: e.bn_stats(kst[:, j, 0:6], k[:, j, :]), [])
                m = V.last
                for j in range(BT * 2):
                    m = V.do(lambda e, j=j: e.bn_aggr(kst[:, j, 6:8], kst[:, j, 0:6]), [m])
                var = kst[:, :, 7]
                return root(var, ts(V, var, var, 1e-5, None, ALU.add, None, m))

            def key_norm(i, m):
                k = kr[i % NS]
                w = [P, BT * 2, D]
                V.wait([m])
                for j in range(BT * 2):
                    m = ts(V, k[:, j, :], k[:, j, :], kst[:, j, 6:7], kst[:, j, 7:8], ALU.subtract, ALU.mult, chain=False)
                tt(G, k, k, spread(g1, w, 1), ALU.mult, m)
                m = tt(G, k, k, spread(b1, w, 1), ALU.add)
                kk = kt[i % NS]
                c0 = copy(G, kk[:, :, UA:UA + S], XT[:, P * i:P * i + P].rearrange("p (b s) -> p b s", s=S),
                          kt_used[i % NS], lt)
                c1 = copy(G, kk[:, :, UA + S:UL], lastT[:, BT * i:BT * i + BT].unsqueeze(2), lastTm)
                return [m, c0, c1]

            def key_turn(i, marks):
                k, kk = kr[i % NS], kt[i % NS]
                out_marks = list(marks)
                for g in range(2):
                    b, freed = hibank()
                    for j in range(4):
                        x = tr(PS[:, b, P * j:P * j + P], k[:, 4 * g + j, :], freed, marks, mark=j == 3)
                    c = copy(A, kk[:, 2 * g:2 * g + 2, 0:UA], PS[:, b, :].rearrange("p (b s) -> p b s", s=UA), x,
                             kt_used[i % NS])
                    free[b] = [c]
                    out_marks.append(c)
                return out_marks

            def queries(i):
                marks = []
                for g in range(4):
                    b, freed = hibank()
                    for j in range(4):
                        m = mm(PS[:, b, P * j:P * j + P], qk[:, 4 * g + j, :], XT[:, P * i:P * i + P], freed, lt,
                               mark=j == 3)
                    src = PS[:, b, :].rearrange("p (h b s) -> p h b s", h=4, s=S)
                    dst = qt[i % 2].rearrange("p b (h s) -> p h b s", s=S)[:, 4 * g:4 * g + 4]
                    for j in range(4):
                        m2 = copy((A, V)[g % 2], dst[:, j], src[:, j], m, qt_used[i % 2])
                    free[b] = [m2]
                    marks.append(m2)
                return marks

            def scores(n, ready):
                i, j, h = n // BT, n % BT, n % 2
                for g in range(4):
                    m = mm(PS[:, g, 0:UL], qt[i % 2][:, j, P * g:P * g + P], kt[i % NS][:, j, :], s_used, ready,
                           mark=g == 3)
                if j == BT - 1:
                    qt_used[i % 2], kt_used[i % NS] = [m], [m]
                mx, nm, sm = (st[:, h, 4 * k:4 * k + 4] for k in range(3))
                red(mx, PS[:, 0:4, 0:UL], ALU.max, m)
                m = ts(V, nm, mx, -scale, None, ALU.mult, None)
                for g in range(4):
                    m = act(pr[h][:, g, :], PS[:, g, 0:UL], ACT.Exp, m, pr_used[h], bias=nm[:, g:g + 1], scale=scale,
                            accum_out=sm[:, g:g + 1])
                s_used[:] = [m]
                return m

            def normal(n, m):
                h = n % 2
                rs = st[:, h, 12:16]
                recip(rs, st[:, h, 8:12], m)
                m = V.last
                for g in range(4):
                    k = ts(V, pr[h][:, g, :], pr[h][:, g, :], rs[:, g:g + 1], None, ALU.mult, None, m, chain=False)
                return k

            def turn(n, m):
                h, marks = n % 2, []
                for k in range(3):
                    b, freed = hibank()
                    n_, c = (P, slice(P * k, P * k + P)) if k < 2 else (n3, slice(UA, UL))
                    for g in range(4):
                        x = tr(PS[0:n_, b, P * g:P * g + P], pr[h][:, g, c], freed, m, mark=g == 3)
                    x = copy((A, V, A)[k], pT[h][0:n_, k, :], PS[0:n_, b, :], x, pT_used[h])
                    free[b] = [x]
                    marks.append(x)
                pr_used[h] = [PE.last]
                return marks

            def weigh(n, marks):
                i, j, h = n // BT, n % BT, n % 2
                b, freed = hibank()
                k, d = kr[i % NS], pT[h]
                mm(PS[:, b, :], k[:, 2 * j, :], d[:, 0, :], freed, marks, start=True, stop=False)
                mm(PS[:, b, :], k[:, 2 * j + 1, :], d[:, 1, :], start=False, stop=False)
                m = mm(PS[:, b, :], v3[:, n, :], d[0:n3, 2, :], v3m, start=False, stop=True, mark=True)
                pT_used[h] = [m]
                m = copy((A, V)[h], oT[i % 2][:, :, S * j:S * j + S],
                         PS[:, b, :].rearrange("p (h s) -> p h s", s=S), m, oT_used[i % 2])
                free[b] = [m]
                return m

            def project(i, marks):
                b, freed = hibank()
                for h in range(NH):
                    m = mm(PS[:, b, 0:D], oT[i % 2][:, h, :], vo[:, h, :], freed, marks, start=h == 0,
                           stop=h == NH - 1, mark=h == NH - 1)
                oT_used[i % 2] = [m]
                m = tt(V, X[:, i, :], PS[:, b, 0:D], X[:, i, :], ALU.add, m)
                free[b] = [m]

            ready = {0: [key_turn(0, key_norm(0, key_stats(0))), queries(0)]}
            outs = {i: [] for i in range(NT)}
            exps = {0: scores(0, ready[0])}
            turned = {}
            for n in range(NB + 1):
                i, j = n // BT, n % BT
                if n < NB:
                    scaled = normal(n, exps.pop(n))
                    if n + 1 < NB:
                        exps[n + 1] = scores(n + 1, ready[(n + 1) // BT])
                    turned[n] = turn(n, scaled)
                if n:
                    outs[(n - 1) // BT].append(weigh(n - 1, turned.pop(n - 1)))
                if j == 0 and n:
                    kr_used[(i - 1) % NS] = [PE.last]
                    if i - 1 + NS < NT:
                        landed[i - 1 + NS] = load(i - 1 + NS)
                    project(i - 1, outs[i - 1])
                if i + 1 < NT and j == 0:
                    ready[i + 1] = [queries(i + 1)]
                    stats_m = key_stats(i + 1)
                if i + 1 < NT and j == 1:
                    norm_m = key_norm(i + 1, stats_m)
                if i + 1 < NT and j == 2:
                    ready[i + 1].append(key_turn(i + 1, norm_m))

        def L3_attn(room):
            NP, J, Cn = 16, 16, 4
            xt = start_layer(room, by_position=True)
            V.wait(xt), A.wait(xt), G.wait(xt)
            z = room.take(NP, 4 * D)
            for h in range(NP):
                b, freed = bank()
                l = XT[:, P * h:P * h + P]
                m = mm(PS[:, b, :], l, W["a3_w"], freed, *xt, mark=True)
                zm = copy((A, V)[h % 2], z[:, h, :], PS[:, b, :], m)
                free[b] = [zm]
            zm = [A.last, V.last]
            z6 = z.rearrange("p h (c r j e) -> p c r h (j e)", c=Cn, r=4, e=2)
            sc = [room.take(J, NP * NP) for _ in range(2)]
            t2 = room.take(J, NP * NP)
            mx, sm = room.take(J * NP), room.take(J * NP)
            o = XN.rearrange("p t d -> p (t d)").rearrange("p (c h f) -> p c h f", c=Cn, h=NP)
            scale = float(2 ** -0.5)
            V.wait(zm), G.wait(zm)
            o_marks = []
            sc_used = [[], []]
            for c in range(Cn):
                q, k, v, w = (z6[:, c, r] for r in range(4))
                s = sc[c % 2]
                s4 = s.rearrange("p j (h g) -> p j h g", h=NP)
                u4 = t2.rearrange("p j (h g) -> p j h g", h=NP)

                def pick(x, e):
                    return x.rearrange("p h (j e) -> p e j h", e=2)[:, e]

                wide = [P, J, NP, NP]
                m0 = tt(V, s4, spread(pick(q, 0), wide, 3), spread(pick(k, 0), wide, 2), ALU.mult, sc_used[c % 2])
                m1 = tt(G, u4, spread(pick(q, 1), wide, 3), spread(pick(k, 1), wide, 2), ALU.mult, V.last if c else None)
                tt(V, s, s, t2, ALU.add, m1)
                sf = s.rearrange("p j (h g) -> p (j h) g", h=NP)
                red(mx, sf, ALU.max)
                m = tt(V, sf, sf, spread(mx, [P, J * NP, NP], 2), ALU.subtract)
                m = act(s, s, ACT.Exp, m, scale=scale)
                red(sm, sf, ALU.add, m)
                recip(sm, sm)
                uf = t2.rearrange("p j (h g) -> p (j h) g", h=NP)
                for e in range(2):
                    m = tt(G if e else V, u4, s4, spread(pick(v, e), wide, 2), ALU.mult, m, V.last)
                    red(mx, uf, ALU.add, m)
                    m = tt(V, mx, mx, sm, ALU.mult)
                    dst = pick(o[:, c], e)
                    m = tt(V, dst, mx.rearrange("p (j h) -> p j h", h=NP), pick(w, e), ALU.mult)
                sc_used[c % 2] = [m]
            a = arrived["scratch"]
            for c in range(Cn):
                for r in range(2):
                    transfer(SP, t["mixed"][c].rearrange("b (h r f) -> r b h f", h=NP, r=2)[r],
                             o[NB * r:NB * r + NB, c], a, m)
            got = transfer(SP, z.rearrange("p h f -> p (h f)")[:, 0:NT * D].rearrange("p (t d) -> p t d", d=D),
                           t["mixed"].rearrange("c b (i d) -> (c b i) d", d=D).rearrange("(t p) d -> p t d", p=P), a,
                           a.mark, V.last, G.last)
            oT = t2.rearrange("p j g -> p (j g)")[:, 0:NTOK]
            ot = rows_to_cols(oT, z.rearrange("p h f -> p (h f)")[:, 0:NT * D].rearrange("p (t d) -> p t d", d=D),
                              [[got, V.last, G.last]] * NQ)
            linear_rows(oT, W["a3_wo"], ot, add_to_x(None, room))

        def L3_ffn(room):
            E, F = 8, 512
            small = room.take(NT, 8)
            m = normalise(XN, X, 1e-5, small)
            hr = room.take(NT, D)
            m = normalise(hr, XN, 1e-5, small, [[k] for k in m], gamma=W["f3_g1"], beta=W["f3_b1"])
            xt = rows_to_cols(XT, hr, m)
            base = room.at
            qT, kT, OT = room.take(NTOK), room.take(NTOK), room.take(NTOK)
            qm = linear_cols(qT, W["f3_Wq"], XT, xt)
            km = linear_cols(kT, W["f3_Wk"], XT, xt)
            om = head_attention(room, qT, kT, [[a, b] for a, b in zip(qm, km)], XT, W["f3_Wv"],
                                float(1.0 / np.sqrt(np.float32(HD))), OT)
            linear_rows(OT, W["f3_Wo"], om, lambda q, ps, m: tt(V, quarter(XN, q), ps, quarter(XN, q), ALU.add, m))
            barrier()
            room = Region(arena, base, room.hi)
            m = normalise(hr, XN, 1e-5, small, gamma=W["f3_g2"], beta=W["f3_b2"])
            xm = tt(V, X, X, XN, ALU.add)
            xt = rows_to_cols(XT, hr, m)
            probs, sel, work, sm = room.take(NT, E), room.take(NT, E), room.take(NT, E), room.take(NT)
            lg = linear_rows(XT, W["f3_Wg"], xt, to_rows(probs))
            m = softmax_rows(probs, E, sm, *lg)
            copy(V, work, probs, m, chain=True)
            pick_largest(sel, work, NT, E, 2, room)
            room.take(600)
            tt(V, probs, probs, sel, ALU.mult)
            red(sm, probs, ALU.add)
            recip(sm, sm)
            gm = tt(V, probs, probs, spread(sm, [P, NT, E], 2), ALU.mult)
            G.wait([xm])
            wT = room.take(NTOK, parts=E)
            for q in range(NQ):
                b, freed = bank()
                for j in range(4):
                    m = tr(PS[0:E, b, P * j:P * j + P], probs[:, 4 * q + j, :], freed, gm, mark=j == 3)
                m = copy(A, wT[:, QW * q:QW * q + QW], PS[0:E, b, :], m)
                free[b] = [m]
                b, freed = bank()
                for j in range(4):
                    at = QW * q + P * j
                    m = mm(PS[:, b, D * j:D * j + D], wT[:, at:at + P], W["f3_bo"][0:E, :], freed, m, mark=j == 3)
                m = tt(V, quarter(X, q), PS[:, b, :].rearrange("p (a d) -> p a d", a=4), quarter(X, q), ALU.add, m)
                free[b] = [m]
            G.wait([V.last])

            def hidden(e, q, f, dst, marks):
                b, freed = bank()
                at = F * e + P * f
                m = mm(PS[:, b, :], W["f3_W1"][:, at:at + P], XT[:, QW * q:QW * q + QW], freed, xt[q], mark=True)
                m = act(dst, PS[:, b, :], ACT.Gelu_apprx_tanh, m, marks, bias=W["f3_b1f"][:, 4 * e + f:4 * e + f + 1])
                free[b] = [m]
                return m

            gated_experts(room, range(E), lambda e, q: probs[:, 4 * q:4 * q + 4, e], F // P, hidden,
                          lambda e, f: W["f3_W2"][:, D * (4 * e + f):D * (4 * e + f) + D])

        order = [L0_xattn, L0_attn, L0_ffn, L1_xattn, L1_attn, L1_ffn, L2_xattn, L2_attn, L2_ffn,
                 L3_xattn, L3_attn, L3_ffn]
        mid = late = None
        for n in LAYERS:
            if n >= 2 and mid is None:
                mid = transfer(SP, mid_words, t["mid"], arrived["mid"])
            if n >= 4 and late is None:
                late = transfer(SP, late_words, t["late"], arrived["late"])
            if n >= 1:
                for lane in (PE, V, A, G):
                    lane.wait([arrived["w0"].mark])
            if n >= 3:
                for lane in (PE, V, A, G):
                    lane.wait([mid])
                SP.wait([arrived["w0"].mark])
            if n >= 9:
                for lane in (PE, V, A, G):
                    lane.wait([late])
            order[n](Region(arena, *scratch[n]))
            barrier()

        rows_out = out.rearrange("b s d -> (b s) d").rearrange("(t p) d -> p t d", p=P)
        transfer(SP, rows_out, X, arrived["out"], V.last, G.last)
        SP.wait([a.mark for a in arrived.values()])

        block = stack.enter_context(nc.Block())

        @block.tensor
        def _(e):
            PE.play(e)

        @block.vector
        def _(e):
            V.play(e)

        @block.scalar
        def _(e):
            A.play(e)

        @block.gpsimd
        def _(e):
            G.play(e)

        @block.sync
        def _(e):
            SP.play(e)


def constants():
    p = np.arange(P)
    rows = {
        "ident": np.eye(P),
        "ones": np.ones((P, P)),
        "upto": p[:, None] <= p[None, :],
        "block": p[:, None] // S == p[None, :] // S,
        "headmask": (p[:, None] // HD) % HG == np.arange(HG),
        "rowmask": p[:, None] // S == np.arange(BT),
        "causal": np.where(np.arange(S)[None, :] <= p[:, None] % S, 0.0, -BIG),
        "ramp": np.broadcast_to(S - np.arange(S), (P, S)),
        "rowid": p[:, None] % S == np.arange(S),
        "minus_half": np.full((P, 1), -0.5),
        "slotbase": np.broadcast_to(np.arange(16) * int(1.25 * NTOK / 16), (P, 16)),
    }
    return np.concatenate([np.asarray(rows[n], np.float32) for n, _ in CONST_PACK], axis=1)


def kernel(**inputs):
    import concourse.bacc as bacc
    from concourse.bass_utils import run_bass_kernel_spmd

    a = {k: np.asarray(v) for k, v in inputs.items()}

    def col(v):
        return v.reshape(P, 1)

    def row(v):
        return np.broadcast_to(v.reshape(1, -1), (P, v.size))

    def stacked(w):
        return w.transpose(1, 0, 2).reshape(P, -1)

    def deep(w):
        return w.reshape(w.shape[0], -1, P, w.shape[-1]).transpose(2, 0, 1, 3).reshape(P, -1)

    def pad(w):
        return np.concatenate([w, np.zeros((P - w.shape[0],) + w.shape[1:], w.dtype)], axis=0)

    Wkv = a["L3_xattn_Wkv"]

    def heads_T(w):
        return w.reshape(P, 16, 64).transpose(2, 1, 0).reshape(64, -1)

    parts = {
        "x0_W1": a["L0_xattn_W1"], "x0_W2": a["L0_xattn_W2"], "x0_b1": col(a["L0_xattn_b1"]),
        "x0_b2": row(a["L0_xattn_b2"]), "x0_gamma": row(a["L0_xattn_gamma"]), "x0_beta": row(a["L0_xattn_beta"]),
        "a0_A": a["L0_attn_A_log"], "a0_D": col(a["L0_attn_D_param"]), "a0_Wdelta": a["L0_attn_W_delta"],
        "a0_bdelta": col(a["L0_attn_b_delta"]), "a0_WB": a["L0_attn_W_B"], "a0_WC": a["L0_attn_W_C"],
        "a0_Wr": a["L0_attn_W_router"], "a0_Wg": stacked(a["L0_attn_Wg"]), "a0_Wu": stacked(a["L0_attn_Wu"]),
        "a0_Wd": deep(a["L0_attn_Wd"]), "a0_wn": a["L0_attn_wn_exp"].reshape(8, P).T,
        "a0_normw": row(a["L0_attn_norm_w"]),
        "f0_rw": a["L0_ffn_router_w"], "f0_rb": row(a["L0_ffn_router_b"]), "f0_wq": stacked(a["L0_ffn_wq"]),
        "f0_wk": stacked(a["L0_ffn_wk"]), "f0_wv": stacked(a["L0_ffn_wv"]), "f0_wo": stacked(a["L0_ffn_wo"]),
        "f0_bq": a["L0_ffn_bq"].T, "f0_bk": a["L0_ffn_bk"].T, "f0_bv": a["L0_ffn_bv"].T, "f0_bo": row(a["L0_ffn_bo"]),
        "x1_WqT": a["L1_xattn_Wq"].T, "x1_Wk": a["L1_xattn_Wk"], "x1_WvT": a["L1_xattn_Wv"].T,
        "x1_bq": col(a["L1_xattn_bq"]), "x1_bk": col(a["L1_xattn_bk"]), "x1_bv": row(a["L1_xattn_bv"]),
        "a1_wqT": a["L1_attn_w_q"].T, "a1_wkT": a["L1_attn_w_k"].T, "a1_wvT": a["L1_attn_w_v"].T,
        "a1_woT": a["L1_attn_w_o"].T,
        "f1_w12T": a["L1_ffn_w12"].transpose(2, 0, 1).reshape(P, -1),
        "f1_w3T": a["L1_ffn_w3"].transpose(2, 0, 1).reshape(P, -1),
        "f1_s1T": a["L1_ffn_shared_w1"].T, "f1_s2T": a["L1_ffn_shared_w2"].T,
        "f1_s3T": deep(a["L1_ffn_shared_w3"].T[None]), "f1_rwT": a["L1_ffn_router_w"].T,
        "f1_eb": row(a["L1_ffn_expert_bias"]),
        "x2_hWT": a["L2_xattn_hW"].T, "x2_cW": a["L2_xattn_cW"], "x2_cWT": a["L2_xattn_cW"].T,
        "x2_qWT": a["L2_xattn_qW"].T, "x2_kW": a["L2_xattn_kW"], "x2_kWT": a["L2_xattn_kW"].T,
        "x2_vWT": a["L2_xattn_vW"].T, "x2_oWT": a["L2_xattn_oW"].T, "x2_hb": col(a["L2_xattn_hb"]),
        "x2_cb": col(a["L2_xattn_cb"]), "x2_qb": col(a["L2_xattn_qb"]), "x2_kb": col(a["L2_xattn_kb"]),
        "x2_vb": col(a["L2_xattn_vb"]), "x2_ob": row(a["L2_xattn_ob"]),
        "a2_wqT": a["L2_attn_wq"].T, "a2_wkT": a["L2_attn_wk"].T, "a2_wvT": a["L2_attn_wv"].T,
        "a2_woT": a["L2_attn_wo"].T, "a2_bq": col(a["L2_attn_bq"]), "a2_bk": col(a["L2_attn_bk"]),
        "a2_bv": row(a["L2_attn_bv"]), "a2_bo": row(a["L2_attn_bo"]), "f2_gwT": a["L2_ffn_gate_w"].T,
        "x3_g1": row(a["L3_xattn_ln1_g"]), "x3_b1": row(a["L3_xattn_ln1_b"]), "x3_g2": row(a["L3_xattn_ln2_g"]),
        "x3_b2": row(a["L3_xattn_ln2_b"]),
        "x3_left": np.concatenate([heads_T(a["L3_xattn_Wq"]), heads_T(Wkv[:, 1024:2048])], axis=0),
        "x3_right": np.concatenate([heads_T(Wkv[:, 0:1024]),
                                    a["L3_xattn_Wo"].reshape(16, 64, D).transpose(1, 0, 2).reshape(64, -1)], axis=0),
        "a3_w": a["L3_attn_w_qkvw"], "a3_wo": a["L3_attn_w_out"],
        "f3_g1": row(a["L3_ffn_ln1_g"]), "f3_b1": row(a["L3_ffn_ln1_b"]), "f3_g2": row(a["L3_ffn_ln2_g"]),
        "f3_b2": row(a["L3_ffn_ln2_b"]),
        "f3_Wq": a["L3_ffn_Wq"], "f3_Wk": a["L3_ffn_Wk"], "f3_Wv": a["L3_ffn_Wv"], "f3_Wo": a["L3_ffn_Wo"],
        "f3_Wg": a["L3_ffn_Wg"], "f3_W1": stacked(a["L3_ffn_W1"]),
        "f3_b1f": a["L3_ffn_b1"].reshape(32, P).T, "f3_W2": deep(a["L3_ffn_W2"]), "f3_bo": pad(a["L3_ffn_b2"]),
    }
    ctx = a["ctx_1024"]
    rows = ctx[:, 0:UA].reshape(NT, BT, 2, P, D)
    arrays = {
        "x": a["x"].reshape(NTOK, D),
        "const": constants(),
        "w0": np.concatenate([parts[n] for n, _ in L0_PACK], axis=1),
        "mid": np.concatenate([parts[n] for n, _ in MID_PACK], axis=1),
        "late": np.concatenate([parts[n] for n, _ in LATE_PACK], axis=1),
        "ctxT": ctx.reshape(NT, BT * U, D).transpose(0, 2, 1),
        "ctxR": rows.transpose(0, 3, 1, 2, 4).reshape(NT, P, -1),
        "ctxL": ctx[:, UA].reshape(NT, BT, D),
        "ctx_last": ctx[:, UA],
        "f2_w1": a["L2_ffn_w1"],
        "f2_w2": a["L2_ffn_w2"].reshape(16, 4, P, D).transpose(0, 2, 1, 3).reshape(16, P, -1),
    }
    arrays = {k: np.ascontiguousarray(v) for k, v in arrays.items()}
    nc = bacc.Bacc("TRN2", target_bir_lowering=False, num_devices=1)
    t = {k: nc.dram_tensor(f"in_{k}", v.shape, F32, kind="ExternalInput").ap() for k, v in arrays.items()}
    nslot = 16 * int(1.25 * NTOK / 16)
    for name, shape in (("slots_in", (nslot, D)), ("slots_out", (nslot, D)), ("lat_rows", (NTOK, D)),
                        ("last_rows", (NB, D)), ("mixed", (4, NB, S * S))):
        t[name] = nc.dram_tensor(name, shape, F32, kind="Internal").ap()
    out = nc.dram_tensor("out", (NB, S, D), F32, kind="ExternalOutput").ap()
    program(nc, t, out)
    r = run_bass_kernel_spmd(nc, [{f"in_{k}": v for k, v in arrays.items()}], core_ids=[0])
    return r.results[0]["out"]
```

```python
from contextlib import ExitStack

import numpy as np

import concourse.bass as bass
from concourse import mybir

F32 = mybir.dt.float32
BF16 = mybir.dt.bfloat16
I32 = mybir.dt.int32
ALU = mybir.AluOpType
ACT = mybir.ActivationFunctionType
AXX = mybir.AxisListType.X

P = 128
NB, S, D = 64, 32, 128
NTOK = NB * S
NT = NTOK // P
BT = P // S
NQ = 4
QW = NTOK // NQ
U = 257
UA = U - 1
H, HD = 16, 8
HG = 4
NG = H // HG
BIG = 1.0e30
LAYERS = range(12)


class Lane:

    def __init__(self, sem):
        self.sem, self.n, self.steps, self.waited = sem, 0, [], {}

    @property
    def last(self):
        return (self.sem, self.n)

    def wait(self, marks):
        for m in marks:
            if m is None:
                continue
            if isinstance(m, list):
                self.wait(m)
                continue
            sem, value = m
            if value > self.waited.get(id(sem), 0):
                self.waited[id(sem)] = value
                self.steps.append(lambda e, sem=sem, value=value: e.wait_ge(sem, value))

    def do(self, fn, marks=()):
        self.wait(marks)
        self.n += 1
        self.steps.append(lambda e: fn(e).then_inc(self.sem, 1))
        return self.last

    def quiet(self, fn, marks=()):
        self.wait(marks)
        self.steps.append(fn)

    def play(self, engine):
        for step in self.steps:
            step(engine)


class Arrivals:

    def __init__(self, sem):
        self.sem, self.total = sem, 0

    @property
    def mark(self):
        return (self.sem, self.total)


def transfer(lane, out, in_, arrivals, *marks):
    lane.wait(marks)
    arrivals.total += 16
    lane.steps.append(lambda e: e.dma_start(out, in_).then_inc(arrivals.sem, 16))
    return arrivals.mark


class Region:

    def __init__(self, arena, lo, hi):
        self.arena, self.at, self.hi = arena, lo, hi

    def take(self, *shape, parts=P):
        n = int(np.prod(shape))
        lo = self.at
        self.at += n
        assert self.at <= self.hi, ("region full", self.at, self.hi)
        ap = self.arena[0:parts, lo:lo + n]
        if len(shape) == 2:
            ap = ap.rearrange("p (a b) -> p a b", a=shape[0])
        if len(shape) == 3:
            ap = ap.rearrange("p (a b c) -> p a b c", a=shape[0], b=shape[1])
        return ap


L0_PACK = [("x0_W1", D), ("x0_W2", D), ("x0_b1", 1), ("x0_b2", D), ("x0_gamma", D), ("x0_beta", D),
           ("a0_A", 16), ("a0_D", 1), ("a0_Wdelta", D), ("a0_bdelta", 1), ("a0_WBC", 96),
           ("a0_Wr", 4), ("a0_Wg", 4 * 256), ("a0_Wu", 4 * 256), ("a0_Wd", 4 * 2 * D), ("a0_wn", 8),
           ("a0_normw", D),
           ("f0_rw", 4), ("f0_rb", 4), ("f0_wq", 4 * D), ("f0_wk", 4 * D), ("f0_wv", 4 * D), ("f0_wo", 4 * D),
           ("f0_bq", 4), ("f0_bk", 4), ("f0_bv", 4), ("f0_bo", 4 * D)]
MID_PACK = [("x1_WqT", D), ("x1_Wk", D), ("x1_WvT", D), ("x1_bq", 1), ("x1_bk", 1), ("x1_bv", D),
            ("a1_wqT", D), ("a1_wkT", D), ("a1_wvT", D), ("a1_woT", D),
            ("f1_w12T", 8 * 256), ("f1_w3T", 8 * D), ("f1_s1T", 512), ("f1_s2T", 512), ("f1_s3T", 4 * D),
            ("f1_rwT", 8), ("f1_eb", 8),
            ("x2_hWT", D), ("x2_cW", D), ("x2_cWT", D), ("x2_qWT", D), ("x2_kW", D), ("x2_kWT", D),
            ("x2_vWT", D), ("x2_oWT", D),
            ("x2_hb", 1), ("x2_cb", 1), ("x2_qb", 1), ("x2_kb", 1), ("x2_vb", 1), ("x2_ob", D),
            ("a2_wqT", D), ("a2_wkT", D), ("a2_wvT", D), ("a2_woT", D), ("a2_bq", 1), ("a2_bk", 1),
            ("a2_bv", D), ("a2_bo", D), ("f2_gwT", 16)]
LATE_PACK = [("x3_g1", D), ("x3_b1", D), ("x3_g2", D), ("x3_b2", D),
             ("x3_left", 2048), ("x3_right", 2048),
             ("a3_w", 512), ("a3_wo", D),
             ("f3_g1", D), ("f3_b1", D), ("f3_g2", D), ("f3_b2", D),
             ("f3_Wq", D), ("f3_Wk", D), ("f3_Wv", D), ("f3_Wo", D), ("f3_Wg", 8),
             ("f3_W1", 8 * 512), ("f3_b1f", 8 * 4), ("f3_W2", 8 * 4 * D), ("f3_bo", D)]
CONST_PACK = [("ident", P), ("ones", P), ("upto", P), ("block", P), ("headmask", HG), ("rowmask", BT),
              ("causal", S), ("ramp", S), ("rowid", S), ("slotbase", 16), ("minus_half", 1), ("select", 32)]


def width(pack):
    return sum(w for _, w in pack)


def columns(pack, ap):
    out, at = {}, 0
    for name, w in pack:
        out[name] = ap[:, at:at + w]
        at += w
    return out


def program(nc, t, out):
    with ExitStack() as stack:
        def sem(name):
            return stack.enter_context(nc.semaphore(name))

        ARENA = 53200
        arena = stack.enter_context(nc.sbuf_tensor("arena", [P, ARENA], F32))
        PS = stack.enter_context(nc.psum_tensor("PS", [P, 8, 512], F32))

        PE, V, A, G, SP = (Lane(sem(f"s_{n}")) for n in ("pe", "dve", "act", "pool", "sp"))
        lanes = (PE, V, A, G, SP)

        keep = Region(arena, 0, 7200)
        X, XN = keep.take(NT, D), keep.take(NT, D)
        XT = keep.take(NTOK)
        const_words = keep.take(width(CONST_PACK))
        C = columns(CONST_PACK, const_words)
        LATE_LO = keep.hi
        MID_LO = LATE_LO + width(LATE_PACK)
        MID_HI = MID_LO + width(MID_PACK)
        W0_LO = ARENA - width(L0_PACK)
        scratch = {0: (LATE_LO, W0_LO), 1: (LATE_LO, W0_LO), 2: (MID_HI, W0_LO)}
        for n in range(3, 9):
            scratch[n] = (MID_HI, ARENA)
        for n in range(9, 12):
            scratch[n] = (MID_LO, ARENA)
        w0_words, mid_words, late_words = arena[:, W0_LO:ARENA], arena[:, MID_LO:MID_HI], arena[:, LATE_LO:MID_LO]
        W = {**columns(L0_PACK, w0_words), **columns(MID_PACK, mid_words), **columns(LATE_PACK, late_words)}

        free = [[] for _ in range(8)]
        turn = {"at": 0}

        def bank():
            b = turn["at"] = (turn["at"] + 1) % 8
            return b, free[b]

        def hibank():
            b = turn["at"] = 4 + (turn["at"] + 1) % 4
            return b, free[b]

        def hibanks_from(b):
            turn["at"] = b + 3

        def barrier():
            marks = [lane.last for lane in lanes if lane is not SP]
            for lane in lanes:
                lane.wait(marks)
            for f in free:
                f.clear()

        def tt(lane, o, a, b, op, *marks, chain=True):
            return lane.do(lambda e: e.tensor_tensor(o, a, b, op), [*marks, lane.last if chain else None])

        def ts(lane, o, a, s1, s2, op0, op1, *marks, chain=True):
            marks = [*marks, lane.last if chain else None]
            if op1 is None:
                return lane.do(lambda e: e.tensor_scalar(o, a, s1, None, op0), marks)
            return lane.do(lambda e: e.tensor_scalar(o, a, s1, s2, op0, op1), marks)

        def stt(o, a, s, b, op0, op1, *marks, chain=True):
            return V.do(lambda e: e.scalar_tensor_tensor(out=o, in0=a, scalar=s, in1=b, op0=op0, op1=op1),
                        [*marks, V.last if chain else None])

        def red(o, a, op, *marks, chain=True):
            return V.do(lambda e: e.tensor_reduce(o, a, AXX, op), [*marks, V.last if chain else None])

        def recip(o, a, *marks):
            return V.do(lambda e: e.reciprocal(o, a), [*marks, V.last])

        def root(x, ready):
            half = C["minus_half"][0:x.shape[0]]
            for ax in range(2, len(x.shape)):
                half = half.unsqueeze(ax)
            return tt(G, x, x, half.broadcast_to(list(x.shape)), ALU.pow, ready)

        def inverse_root(x):
            m = root(x, V.last)
            V.wait([m])
            return m

        def copy(lane, o, a, *marks, chain=False):
            marks = [*marks, lane.last if chain else None]
            if lane is A:
                return A.do(lambda e: e.copy(o, a), marks)
            return lane.do(lambda e: e.tensor_copy(o, a), marks)

        def act(o, a, func, *marks, chain=False, **kw):
            return A.do(lambda e: e.activation(o, a, func, **kw), [*marks, A.last if chain else None])

        def mm(o, l, r, *marks, start=True, stop=True, mark=False, check=True):
            fn = (lambda e: e.matmul(o, l, r, start=start, stop=stop, skip_group_check=not check))
            return PE.do(fn, marks) if mark else PE.quiet(fn, marks)

        def tr(o, a, *marks, mark=False):
            n = a.shape[0]
            fn = (lambda e: e.transpose(o, a, C["ident"][0:n, 0:n]))
            return PE.do(fn, marks) if mark else PE.quiet(fn, marks)

        def spread(ap, shape, *axes):
            for ax in axes:
                ap = ap.unsqueeze(ax)
            return ap.broadcast_to(shape)

        def per_token(ap, n=NT, w=D):
            return spread(ap, [P, n, w], 2)

        def normalise(dst, src, eps, small, ready=(), gamma=None, beta=None):
            roots, done = {}, []
            stats, mv = small[:, :, 0:6], small[:, :, 6:8]

            def norm(q):
                V.wait([roots[q]])
                for t_ in range(4 * q, 4 * q + 4):
                    m = ts(V, dst[:, t_, :], src[:, t_, :], mv[:, t_, 0:1], mv[:, t_, 1:2], ALU.subtract, ALU.mult,
                           chain=False)
                if gamma is not None:
                    tt(V, quarter(dst, q), quarter(dst, q), spread(gamma, [P, 4, D], 1), ALU.mult)
                    m = tt(V, quarter(dst, q), quarter(dst, q), spread(beta, [P, 4, D], 1), ALU.add)
                done.append(m)

            for q in range(NQ):
                V.wait(ready[q] if ready else [])
                tiles = range(4 * q, 4 * q + 4)
                for t_ in tiles:
                    m = V.do(lambda e, t_=t_: e.bn_stats(stats[:, t_, :], src[:, t_, :]), [V.last if t_ == 4 * q else None])
                for t_ in tiles:
                    a = V.do(lambda e, t_=t_: e.bn_aggr(mv[:, t_, :], stats[:, t_, :]), [m])
                var = quarter(mv, q)[:, :, 1]
                roots[q] = root(var, ts(V, var, var, eps, None, ALU.add, None, a))
                if q - 1 in roots:
                    norm(q - 1)
            norm(q)
            return done

        def rows_to_cols(dst, src, ready, nextbank=bank, by_position=False):
            done = []
            for q in range(NQ):
                b, freed = nextbank()
                for j in range(4):
                    m = tr(PS[:, b, P * j:P * j + P], src[:, 4 * q + j, :], freed, ready[q], mark=j == 3)
                lane = (A, V)[q % 2]
                o, i = dst[:, QW * q:QW * q + QW], PS[:, b, :]
                if by_position:
                    nb = NB // NQ
                    o = dst.rearrange("p (h r b) -> p b h r", b=NB, r=2)[:, nb * q:nb * q + nb]
                    i = i.rearrange("p (b h r) -> p b h r", b=nb, r=2)
                m = copy(lane, o, i, m)
                free[b] = [m]
                done.append(m)
            return done

        def linear_cols(dst, w, src, ready, bias=None, nextbank=bank):
            done = []
            for q in range(NQ):
                b, freed = nextbank()
                n = dst.shape[0]
                m = mm(PS[0:n, b, :], w, src[:, QW * q:QW * q + QW], freed, ready[q], mark=True)
                o, i = dst[:, QW * q:QW * q + QW], PS[0:n, b, :]
                if bias is None:
                    m = copy((A, V)[q % 2], o, i, m)
                elif q % 2:
                    m = ts(V, o, i, bias, None, ALU.add, None, m, chain=False)
                else:
                    m = act(o, i, ACT.Identity, m, bias=bias)
                free[b] = [m]
                done.append(m)
            return done

        def linear_rows(src, w, ready, take, nextbank=bank):
            n = w.shape[-1]
            done = []
            for q in range(NQ):
                b, freed = nextbank()
                for j in range(4):
                    at = QW * q + P * j
                    m = mm(PS[:, b, n * j:n * j + n], src[:, at:at + P], w, freed, ready[q], mark=j == 3)
                m = take(q, PS[:, b, 0:4 * n].rearrange("p (a d) -> p a d", a=4), m)
                free[b] = [m]
                done.append(m)
            return done

        def quarter(ap, q):
            return ap[:, 4 * q:4 * q + 4, :]

        def to_rows(dst, bias=None, base=None):
            def take(q, ps, m):
                if bias is not None:
                    m = tt(V, quarter(dst, q), ps, spread(bias, [P, 4, ps.shape[-1]], 1), ALU.add, m)
                    if base is not None:
                        m = tt(V, quarter(dst, q), quarter(dst, q), quarter(base, q), ALU.add, m)
                elif base is not None:
                    m = tt(V, quarter(dst, q), ps, quarter(base, q), ALU.add, m)
                else:
                    m = copy((A, V)[q % 2], quarter(dst, q), ps, m)
                return m
            return take

        def softmax_rows(x, e, small, *marks):
            wide = [P, NT, e]
            red(small, x, ALU.max, *marks)
            m = tt(V, x, x, spread(small, wide, 2), ALU.subtract)
            m = act(x, x, ACT.Exp, m)
            red(small, x, ALU.add, m)
            recip(small, small)
            return tt(V, x, x, spread(small, wide, 2), ALU.mult)

        def pick_largest(sel, v, rows, n, k, room, *marks):
            r = Region(room.arena, room.at, room.hi)
            key, hit = r.take(rows, n), r.take(rows, n)
            top, first = r.take(rows), r.take(rows)
            wide = [P, rows, n]
            ramp = spread(C["ramp"][:, 0:n], wide, 1)
            V.wait(marks)
            for i in range(k):
                red(top, v, ALU.max)
                tt(V, key, v, spread(top, wide, 2), ALU.is_equal)
                tt(V, key, key, ramp, ALU.mult)
                red(first, key, ALU.max)
                tgt = sel if i == 0 else hit
                m = tt(V, tgt, key, spread(first, wide, 2), ALU.is_equal)
                if i + 1 < k:
                    stt(v, tgt, -BIG, v, ALU.mult, ALU.add)
                if i:
                    m = tt(V, sel, sel, hit, ALU.add)
            return m

        NS_CTX = 4
        key_slots = [Arrivals(sem(f"s_ctx_keys{i}")) for i in range(NS_CTX)]
        row_slots = [Arrivals(sem(f"s_ctx_rows{i}")) for i in range(NS_CTX)]

        mixed_slots = [Arrivals(sem(f"s_mixed{c}")) for c in range(4)]

        def cross_attention(room, qT, ready, scale, O, row_term=None, then=None):
            NS = NS_CTX
            kT = [room.take(BT * U) for _ in range(NS)]
            kR = [room.take(BT * 2, D) for _ in range(NS)]
            kL = [room.take(D, parts=BT) for _ in range(NS)]
            pr = [room.take(U) for _ in range(2)]
            lastp = [room.take(BT) for _ in range(2)]
            pT = [room.take(2 * P) for _ in range(2)]
            pL = [room.take(P, parts=BT) for _ in range(2)]
            st = [room.take(4) for _ in range(3)]
            tile_done, turned, summed = {}, {}, {}

            def load_keys(i, *marks):
                if i < NT:
                    keys_in[i] = transfer(SP, kT[i % NS], t["ctxT"][i], key_slots[i % NS], *marks)

            def load_rows(i, *marks):
                if i < NT:
                    a = row_slots[i % NS]
                    transfer(SP, kR[i % NS], t["ctxR"][i].rearrange("p (a d) -> p a d", d=D), a, *marks)
                    rows_in[i] = transfer(SP, kL[i % NS], t["ctxL"][i], a)

            keys_in, rows_in = {}, {}
            for i in range(NS):
                load_keys(i)
                load_rows(i)
            if then is not None:
                then()

            def scores(i):
                s, h = i % NS, i % 2
                b, freed = bank()
                for j in range(BT):
                    m = mm(PS[S * j:S * j + S, b, 0:U], qT[:, P * i + S * j:P * i + S * j + S],
                           kT[s][:, U * j:U * j + U], freed, ready[i // 4], keys_in[i], start=True,
                           stop=row_term is None, mark=j == BT - 1)
                if row_term is not None:
                    m = mm(PS[:, b, 0:U], row_term[:, P * i:P * i + P], C["ones_row"], start=False, stop=True, mark=True)
                load_keys(i + NS, m)
                mx, nm, sm = (st[i % 3][:, k:k + 1] for k in range(3))
                red(mx, PS[:, b, 0:U], ALU.max, m)
                m = ts(V, nm, mx, -scale, None, ALU.mult, None)
                m = act(pr[h], PS[:, b, 0:U], ACT.Exp, m, turned.get(i - 2), bias=nm, scale=scale, accum_out=sm)
                free[b] = [m]
                return m

            def last_row(i, m):
                recip(st[i % 3][:, 3:4], st[i % 3][:, 2:3], m)
                return tt(V, lastp[i % 2], pr[i % 2][:, UA:U].broadcast_to([P, BT]), C["rowmask"], ALU.mult,
                          turned.get(i - 2))

            def turn(i, m, alone):
                h = i % 2
                b, freed = bank()
                for j in range(2):
                    x = tr(PS[:, b, P * j:P * j + P], pr[h][:, P * j:P * j + P], freed, m, mark=j == 1)
                c0 = copy(A, pT[h], PS[:, b, 0:2 * P], x, summed.get(i - 2))
                free[b] = [c0]
                b, freed = bank()
                x = tr(PS[0:BT, b, 0:P], lastp[h], freed, alone, mark=True)
                c1 = copy(V, pL[h], PS[0:BT, b, 0:P], x, summed.get(i - 2))
                free[b] = [c1]
                turned[i] = x
                return [c0, c1]

            def sums(i, marks):
                s, h = i % NS, i % 2
                b, freed = bank()
                for j in range(BT):
                    for k in range(2):
                        mm(PS[S * j:S * j + S, b, 0:D], pT[h][:, P * k + S * j:P * k + S * j + S],
                           kR[s][:, 2 * j + k, :], freed, marks, rows_in[i], start=k == 0, stop=False)
                m = mm(PS[:, b, 0:D], pL[h], kL[s], start=False, stop=True, mark=True)
                summed[i] = [m]
                load_rows(i + NS, m)
                m = ts(V, O[:, i, :], PS[:, b, 0:D], st[i % 3][:, 3:4], None, ALU.mult, None, m)
                free[b] = [m]
                tile_done[i] = m

            exps, copies = {0: scores(0)}, {}
            for i in range(NT + 1):
                if i < NT:
                    alone = last_row(i, exps[i])
                if i + 1 < NT:
                    exps[i + 1] = scores(i + 1)
                if i < NT:
                    copies[i] = turn(i, exps.pop(i), alone)
                if i:
                    sums(i - 1, copies.pop(i - 1))
            return [tile_done[4 * q + 3] for q in range(NQ)]

        def repeat(dst, xT, i, *marks):
            d4 = dst.rearrange("p (b h k) -> p b h k", b=BT, h=HG)
            x3 = xT[:, P * i:P * i + P].rearrange("p (b k) -> p b k", b=BT)
            return copy(A, d4, spread(x3, [P, BT, HG, S], 2), *marks)

        def head_attention(room, qT, kT, ready, xT, wv, scale, OT, *, key_mask=None, softcap=None,
                           bias_col=None, bias_row=None, choose=None, repeated=None, block=None):
            keepall = choose is not None
            NK = 3
            kB = [room.take(BT * HG * S) for _ in range(NK)]
            if repeated is None:
                xR = [room.take(BT * HG * S) for _ in range(3)]
            pr = [room.take(H, S) for _ in range(NT if keepall else 3)]
            pT = [room.take(NG * P) for _ in range(2)]
            vB = [room.take(BT * D) for _ in range(3)]
            mx, sm = room.take(NT, H), room.take(NT, H)
            kb_used, pt_used, vb_used, pr_used, xr_used = {}, {}, {}, {}, {}
            s_used = {0: [], NG: []}
            st = {}
            pend_av = {}

            def spread_keys(i):
                src = kT[:, P * i:P * i + P].rearrange("p (b k) -> p b k", b=BT)
                dst = kB[i % NK].rearrange("p (b h k) -> p b h k", b=BT, h=HG)
                for b in range(BT):
                    m = tt(G, dst[:, b], spread(src[:, b, :], [P, HG, S], 1),
                           spread(C["headmask"], [P, HG, S], 2), ALU.mult,
                           ready[i // 4], kb_used.get(i - NK), chain=False)
                return m

            def scores(i):
                m = st.pop(("k", i))
                at0 = NG * (i % 2) if keepall else 0
                for g in range(NG):
                    for b in range(BT):
                        at = P * i + S * b
                        r = slice(S * g, S * g + S)
                        k = mm(PS[S * b:S * b + S, at0 + g, 0:P], qT[r, at:at + S], kB[i % NK][r, P * b:P * b + P], m,
                               s_used[at0], start=True, stop=key_mask is None, mark=(g, b) == (NG - 1, BT - 1))
                kb_used[i] = k
                for g in range(NG if key_mask is not None else 0):
                    k = mm(PS[:, at0 + g, 0:P], block, spread(key_mask(i), [P, HG, S], 1), start=False, stop=True,
                           mark=g == NG - 1)
                sc = PS[:, at0:at0 + NG, 0:P].rearrange("p g (h k) -> p g h k", h=HG)
                p = pr[i % len(pr)]
                p4 = p.rearrange("p (g h) k -> p g h k", g=NG)
                m4 = mx[:, i, :].rearrange("p (g h) -> p g h", g=NG)
                if softcap is not None:
                    m = None
                    for g in range(NG):
                        m = act(p4[:, g], sc[:, g], ACT.Tanh, k, pr_used.get(i - len(pr)), scale=scale / softcap)
                    s_used[at0] = [m]
                    stt(p, p, softcap, spread(C["causal"], [P, H, S], 1), ALU.mult, ALU.add, m)
                    red(mx[:, i, :], p, ALU.max)
                    m = tt(V, p, p, spread(mx[:, i, :], [P, H, S], 2), ALU.subtract)
                    m = act(p, p, ACT.Exp, m)
                else:
                    red(m4, sc, ALU.max, k)
                    m = tt(V, p4, sc, spread(m4, [P, NG, HG, S], 3), ALU.subtract, pr_used.get(i - len(pr)))
                    s_used[at0] = [m]
                    m = act(p, p, ACT.Exp, m, scale=scale)
                return m

            def repeat_tokens(i):
                if repeated is not None:
                    return repeated[i]
                return xR[i % 3], repeat(xR[i % 3], xT, i, ready[i // 4], xr_used.get(i - 3))

            def values(i):
                xr, xm = st.pop(("x", i))
                b, freed = hibank()
                for j in range(BT):
                    m = mm(PS[:, b, D * j:D * j + D], xr[:, P * j:P * j + P], wv, freed, xm,
                           mark=j == BT - 1)
                xr_used[i] = m
                if bias_row is not None:
                    v = vB[i % 3].rearrange("p (b d) -> p b d", b=BT)
                    m = tt(V, v, PS[:, b, :].rearrange("p (b d) -> p b d", b=BT), spread(bias_row, [P, BT, D], 1),
                           ALU.add, m, vb_used.get(i - 3), chain=False)
                    free[b] = [m]
                    return tt(V, vB[i % 3].rearrange("p (g h d) -> p g h d", h=HG, d=HD),
                              vB[i % 3].rearrange("p (g h d) -> p g h d", h=HG, d=HD),
                              spread(spread(C["rowmask"], [P, BT * NG, HG], 1), [P, BT * NG, HG, HD], 3), ALU.mult)
                m = tt(V, vB[i % 3].rearrange("p (g h d) -> p g h d", h=HG, d=HD),
                       PS[:, b, :].rearrange("p (g h d) -> p g h d", h=HG, d=HD),
                       spread(spread(C["rowmask"], [P, BT * NG, HG], 1), [P, BT * NG, HG, HD], 3), ALU.mult,
                       m, vb_used.get(i - 3), chain=False)
                free[b] = [m]
                return m

            def total(i, m):
                red(sm[:, i, :], pr[i % len(pr)], ALU.add, m)
                return recip(sm[:, i, :], sm[:, i, :])

            def normal(i, m):
                p = pr[i % len(pr)]
                return tt(G, p, p, spread(sm[:, i, :], [P, H, S], 2), ALU.mult, m)

            def turn_weights(i, m):
                b, freed = hibank()
                p = pr[i % len(pr)].rearrange("p (g h) k -> p g (h k)", g=NG)
                for g in range(NG):
                    m = tr(PS[:, b, P * g:P * g + P], p[:, g, :], freed, m, mark=g == NG - 1)
                pr_used[i] = m
                m = copy(A, pT[i % 2], PS[:, b, :], m, pt_used.get(i - 2))
                free[b] = [m]
                return m

            def average(i, m):
                b, freed = hibank()
                for j in range(BT):
                    for g in range(NG):
                        k = mm(PS[S * g:S * g + S, b, S * j:S * j + S], vB[i % 3][:, D * j + S * g:D * j + S * g + S],
                               pT[i % 2][:, P * g + S * j:P * g + S * j + S], freed, m, st[("v", i)],
                               mark=(j, g) == (BT - 1, NG - 1))
                pt_used[i] = vb_used[i] = k
                o = OT[:, P * i:P * i + P]
                m = copy(A, o, PS[:, b, 0:P], k) if bias_col is None else \
                    act(o, PS[:, b, 0:P], ACT.Identity, k, bias=bias_col)
                free[b] = [m]
                pend_av[i] = m

            def keys_ahead(i):
                if i < NT:
                    st[("k", i)] = spread_keys(i)
                    if not keepall:
                        st[("x", i)] = repeat_tokens(i)

            def start():
                keys_ahead(0)
                keys_ahead(1)

            def run(fill=None):
                for at0 in s_used:
                    s_used[at0] = [list(free[at0 + g]) for g in range(NG)]
                if keepall:
                    for i in range(NT + 1):
                        if i < NT:
                            st[("p", i)] = scores(i)
                        keys_ahead(i + 2)
                        if i:
                            red(sm[:, i - 1, :], pr[i - 1], ALU.add, st.pop(("p", i - 1)))
                    for g in range(2 * NG):
                        free[g] = list(s_used[NG * (g // NG)])
                    chosen = choose(mx, sm)
                    for i in range(3):
                        st[("x", i)] = repeat_tokens(i)
                    for i in range(NT + 2):
                        if i < NT:
                            if 3 <= i + 2 < NT:
                                st[("x", i + 2)] = repeat_tokens(i + 2)
                            st[("v", i)] = values(i)
                            st[("n", i)] = normal(i, chosen)
                        if 0 <= i - 1 < NT:
                            st[("t", i - 1)] = turn_weights(i - 1, st.pop(("n", i - 1)))
                        if i >= 2:
                            average(i - 2, st.pop(("t", i - 2)))
                else:
                    for i in range(NT + 2):
                        if 0 <= i - 1 < NT:
                            m = total(i - 1, st.pop(("p", i - 1)))
                            st[("n", i - 1)] = normal(i - 1, m)
                        keys_ahead(i + 2)
                        if i < NT:
                            st[("p", i)] = scores(i)
                            st[("v", i)] = values(i)
                        if i == NT and fill is not None:
                            fill()
                        if 0 <= i - 1 < NT:
                            st[("t", i - 1)] = turn_weights(i - 1, st.pop(("n", i - 1)))
                        if 0 <= i - 2 < NT:
                            average(i - 2, st.pop(("t", i - 2)))
                for g in range(NG):
                    free[g] = list(s_used[0])
                return [pend_av[4 * q + 3] for q in range(NQ)]

            return start, run

        def all_heads(*args, **kw):
            start, run = head_attention(*args, **kw)
            start()
            return run()

        arrived = {n: Arrivals(sem(f"s_{n}")) for n in ("const", "x", "w0", "mid", "late", "scratch", "scattered", "gathered", "out")}
        transfer(SP, X, t["x"].rearrange("(t p) d -> p t d", p=P), arrived["x"])
        transfer(SP, const_words, t["const"], arrived["const"])

        def load_first_weights():
            transfer(SP, w0_words, t["w0"], arrived["w0"])

        if min(LAYERS) > 0:
            load_first_weights()
        for lane in (PE, V, A, G):
            lane.wait([arrived["const"].mark, arrived["x"].mark])
        C["ones_row"] = keep.take(U, parts=1)
        ones_row = V.do(lambda e: e.memset(C["ones_row"], 1.0))
        PE.wait([ones_row])

        def start_layer(room, eps=1e-5, by_position=False):
            m = normalise(XN, X, eps, Region(arena, room.hi - 8 * NT, room.hi).take(NT, 8))
            return rows_to_cols(XT, XN, m, by_position=by_position)

        def L0_xattn(room):
            xt = start_layer(room)
            O = room.take(NT, D)
            o = cross_attention(room, XT, xt, 1.0 / float(np.sqrt(np.float32(D) + np.float32(1e-8))), O,
                                then=load_first_weights)
            for lane in (PE, V, A, G):
                lane.wait([arrived["w0"].mark])
            tmp, small = room.take(NT, D), room.take(NT, 8)
            m = [[tt(V, quarter(O, q), quarter(O, q), quarter(XN, q), ALU.add, o[q])] for q in range(NQ)]
            m = normalise(O, O, 1e-6, small, m, gamma=W["x0_gamma"], beta=W["x0_beta"])
            oT, hT = room.take(NTOK), room.take(NTOK)
            ot = rows_to_cols(oT, O, m)
            done = []
            for q in range(NQ):
                b, freed = bank()
                m = mm(PS[:, b, :], W["x0_W1"], oT[:, QW * q:QW * q + QW], freed, ot[q], mark=True)
                m = act(hT[:, QW * q:QW * q + QW], PS[:, b, :], ACT.Relu, m, bias=W["x0_b1"])
                free[b] = [m]
                done.append(m)
            f = linear_rows(hT, W["x0_W2"], done, to_rows(tmp, bias=W["x0_b2"], base=O))
            normalise(O, tmp, 1e-6, small, [[a, b] for a, b in zip(f, ot)], gamma=W["x0_gamma"], beta=W["x0_beta"])
            tt(V, X, X, O, ALU.add)

        def L0_attn(room):
            SN, E, F = 16, 4, 256
            RING = 8
            xt = start_layer(room)
            delta, dab, negA = room.take(NTOK), room.take(NTOK), room.take(SN)
            parts = room.take(NTOK // 2).bitcast(BF16)
            select = room.take(SN).bitcast(BF16)
            rest = [room.take(QW) for _ in range(2)]
            Ar, Ur = room.take(RING, QW), room.take(RING, QW)
            acc, acc_m = room.take(NT, D), []
            sel_m = copy(G, select, C["select"])
            zm = G.do(lambda e: e.memset(Ar.rearrange("p r (b t) -> p (r b) t", t=S)[:, :, 0:1], 0.0))
            parts_m = []
            for q in range(NQ):
                c = slice(QW * q, QW * q + QW)
                b, freed = bank()
                r = rest[q % 2]
                m = mm(PS[0:96, b, :], W["a0_WBC"], XT[:, c], freed, xt[q], mark=True)
                m = copy(A, parts[0:96, c], PS[0:96, b, :], m)
                m = tt(V, r[0:96], PS[0:96, b, :], parts[0:96, c], ALU.subtract, m, parts_m[q - 2:q - 1])
                free[b] = [m]
                m = copy(A, parts[32:64, c], r[32:64], m)
                m = copy(A, parts[64:96, c], r[64:96], m)
                m = tt(V, r[64:96], r[64:96], parts[64:96, c], ALU.subtract, m)
                parts_m.append(copy(A, parts[64:96, c], r[64:96], m))
            quarters = [slice(QW * q, QW * q + QW) for q in range(NQ)]
            zs = []
            for q, c in enumerate(quarters):
                b, freed = bank()
                m = mm(PS[:, b, :], W["a0_Wdelta"], XT[:, c], freed, xt[q], mark=True)
                m = ts(V, delta[:, c], PS[:, b, :], W["a0_bdelta"], None, ALU.add, None, m)
                free[b] = [m]
                zs.append(m)
            zs = [act(dab[:, c], delta[:, c], ACT.Abs, m) for c, m in zip(quarters, zs)]
            zs = [act(dab[:, c], dab[:, c], ACT.Exp, m, scale=-1.0) for c, m in zip(quarters, zs)]
            m = act(negA, W["a0_A"], ACT.Exp)
            nm = ts(V, negA, negA, -1.0, None, ALU.mult, None, m)
            zs = [act(dab[:, c], dab[:, c], ACT.Ln, m, bias=1.0) for c, m in zip(quarters, zs)]
            delta_m = [stt(delta[:, c], delta[:, c], 0.0, dab[:, c], ALU.max, ALU.add, m)
                       for c, m in zip(quarters, zs)]
            yT = dab

            assert S * 10.0 * np.sqrt(D) < 1.0e4
            a_ready, u_ready, scanned, read, ys = {}, {}, {}, {}, []

            def part(i):
                return slice(QW * (i // SN), QW * (i // SN) + QW)

            def over_partitions(b, i, row, *marks):
                lhs = select[0:96, row:row + 1].broadcast_to([96, P])
                return mm(PS[:, b, :], lhs, parts[0:96, part(i)], free[b], parts_m[i // SN], *marks, mark=True)

            N = NQ * SN
            for i in range(N + 4):
                r = i % RING
                clip_i = None
                if i < N:
                    q, s = divmod(i, SN)
                    a_view = Ar[:, r, :].rearrange("p (b t) -> p b t", t=S)[:, :, 1:S]
                    d_view = delta[:, part(i)].rearrange("p (b t) -> p b t", t=S)[:, :, 1:S]
                    a_ready[i] = act(a_view, d_view, ACT.Exp, delta_m[q], nm, scanned.get(i - RING), zm,
                                     scale=negA[:, s:s + 1])
                    b = 2 + i % 3
                    m = over_partitions(b, i, s, sel_m)
                    m = tt(V, Ur[:, r, :], PS[:, b, :], delta[:, part(i)], ALU.mult, m, delta_m[q],
                           read.get(("sum", i - RING)), chain=False)
                    free[b] = [m]
                    clip_i = m
                j = i - 2
                if 0 <= j < N:
                    rj = j % RING
                    m = [a_ready[j], u_ready[j]]
                    scanned[j] = V.do(lambda e, rj=rj: e.tensor_tensor_scan(
                        Ur[:, rj, :], Ar[:, rj, :], Ur[:, rj, :], 0.0, ALU.mult, ALU.add), m)
                if i < N:
                    m = ts(V, Ur[:, r, :], Ur[:, r, :], -10.0, 10.0, ALU.max, ALU.min, clip_i, chain=False)
                    u_ready[i] = tt(G, Ur[:, r, :], Ur[:, r, :], XT[:, part(i)], ALU.mult, m, chain=False)
                j = i - 3
                if 0 <= j < N:
                    b = 5 + j % 3
                    m = over_partitions(b, j, SN + j % SN)
                    m = tt(V, Ur[:, j % RING, :], PS[:, b, :], Ur[:, j % RING, :], ALU.mult, m, scanned[j], chain=False)
                    free[b] = [m]
                    read[j] = m
                j = i - 4
                if 0 <= j < N:
                    q, s = divmod(j, SN)
                    yb = q % 2
                    m = mm(PS[:, yb, :], C["ident"], Ur[:, j % RING, :], free[yb], read[j],
                           start=s == 0, stop=s == SN - 1, mark=True)
                    read[("sum", j)] = m
                    if s == SN - 1:
                        m = stt(yT[:, part(j)], XT[:, part(j)], W["a0_D"], PS[:, yb, :], ALU.mult, ALU.add, m)
                        ys.append(m)
                        for k in range(4):
                            at = QW * q + P * k
                            m = tr(PS[:, yb, P * k:P * k + P], yT[:, at:at + P], ys[q], mark=k == 3)
                        m = copy(A, quarter(acc, q), PS[:, yb, :].rearrange("p (a d) -> p a d", a=4), m)
                        free[yb] = [m]
                        acc_m.append(m)

            probs, small, sel, work = room.take(NT, E), room.take(NT), room.take(NT, E), room.take(NT, E)
            ms, gate, total = room.take(NT), room.take(NT), room.take(NT)
            tmp = [room.take(4, D) for _ in range(2)]
            sg, gT, sq = ([room.take(2, QW) for _ in range(3)] for _ in range(3))
            wd = room.take(E * 2, D)
            for i in range(E * 2):
                wd_m = ts(V, wd[:, i, :], W["a0_Wd"][:, D * i:D * i + D], W["a0_wn"][:, i:i + 1], None, ALU.mult, None,
                          chain=False)
            gated, squared, gT_used, sq_used, tmp_used = {}, {}, {}, {}, {}

            def hidden(n):
                e, q = divmod(n, NQ)
                k = n % 3
                col = slice(QW * q, QW * q + QW)
                for f in range(2):
                    at = F * e + P * f
                    b1, b2 = 2 * f, 2 * f + 1
                    m1 = mm(PS[:, b1, :], W["a0_Wg"][:, at:at + P], yT[:, col], free[b1], ys[q], mark=True)
                    m2 = mm(PS[:, b2, :], W["a0_Wu"][:, at:at + P], yT[:, col], free[b2], mark=True)
                    m = act(sg[k][:, f, :], PS[:, b1, :], ACT.Silu, m1, gated.get(n - 3))
                    free[b1] = [m]
                    m = tt(V, gT[k][:, f, :], PS[:, b2, :], sg[k][:, f, :], ALU.mult, m, m2, gT_used.get(n - 3),
                           chain=False)
                    free[b2] = [m]
                    gated[n] = m
                    if f == 0:
                        s0 = act(sq[k][:, 0, :], gT[k][:, 0, :], ACT.Square, m, sq_used.get(n - 3))
                m = tt(G, sq[k][:, 1, :], gT[k][:, 1, :], gT[k][:, 1, :], ALU.mult, gated[n], sq_used.get(n - 3),
                       chain=False)
                squared[n] = tt(G, sq[k][:, 0, :], sq[k][:, 0, :], sq[k][:, 1, :], ALU.add, s0)

            def sums(n):
                e, q = divmod(n, NQ)
                k = n % 3
                b1, b2 = 4 + n % 2, 6 + n % 2
                for j in range(4):
                    for f in range(2):
                        c = slice(P * j, P * j + P)
                        m = mm(PS[:, b2, D * j:D * j + D], gT[k][:, f, c], wd[:, 2 * e + f, :], free[b2], gated[n], wd_m,
                               start=f == 0, stop=f == 1, mark=(j, f) == (3, 1))
                gT_used[n] = down = m
                for j in range(4):
                    m = mm(PS[:, b1, j:j + 1], sq[k][:, 0, P * j:P * j + P], C["ones"][:, 0:1], free[b1], squared[n],
                           mark=j == 3)
                sq_used[n] = m
                ms_q, gt_q = ms[:, 4 * q:4 * q + 4], gate[:, 4 * q:4 * q + 4]
                m = ts(V, ms_q, PS[:, b1, 0:4], 1.0 / F, 1e-6, ALU.mult, ALU.add, m)
                free[b1] = [m]
                return b2, down, root(ms_q, m)

            def scaled(n, b2, down, root_m):
                e, q = divmod(n, NQ)
                ms_q, gt_q = ms[:, 4 * q:4 * q + 4], gate[:, 4 * q:4 * q + 4]
                tt(V, gt_q, ms_q, probs[:, 4 * q:4 * q + 4, e], ALU.mult, root_m)
                m = tt(V, tmp[n % 2], PS[:, b2, :].rearrange("p (a d) -> p a d", a=4),
                       spread(gt_q, [P, 4, D], 2), ALU.mult, down, tmp_used.get(n - 2))
                free[b2] = [m]
                m = tt(G, quarter(acc, q), quarter(acc, q), tmp[n % 2], ALU.add, m, acc_m[q])
                tmp_used[n] = acc_m[q] = m

            def finish(q):
                a, rows = quarter(acc, q), slice(4 * q, 4 * q + 4)
                squares = sg[q // 2][:, q % 2, :]
                m = act(squares, a.rearrange("p a d -> p (a d)"), ACT.Square, acc_m[q], gated[NQ * E - 1])
                red(total[:, rows], squares.rearrange("p (a d) -> p a d", a=4), ALU.add, m)
                m = ts(V, total[:, rows], total[:, rows], 1.0 / D, 1e-6, ALU.mult, ALU.add)
                m = root(total[:, rows], m)
                tt(V, a, a, spread(total[:, rows], [P, 4, D], 2), ALU.mult, m)
                tt(V, a, a, spread(W["a0_normw"], [P, 4, D], 1), ALU.mult)
                tt(V, quarter(X, q), quarter(X, q), a, ALU.add)

            N = E * NQ
            pending = []
            for n in range(N + 1):
                if n < N:
                    hidden(n)
                if n == 0:
                    lg = linear_rows(yT, W["a0_Wr"], ys, to_rows(probs))
                if n == 1:
                    m = softmax_rows(probs, E, small, *lg)
                    copy(V, work, probs, m, chain=True)
                    pick_largest(sel, work, NT, E, 2, room)
                    tt(V, probs, probs, sel, ALU.mult)
                    red(small, probs, ALU.add)
                    ts(V, small, small, 1e-9, None, ALU.add, None)
                    recip(small, small)
                    tt(V, probs, probs, spread(small, [P, NT, E], 2), ALU.mult)
                if n:
                    pending.append((n - 1, *sums(n - 1)))
                if len(pending) > 1 or n == N:
                    scaled(*pending.pop(0))
            scaled(*pending.pop(0)) if pending else None
            for q in range(NQ):
                finish(q)

        def L0_ffn(room):
            E = 4
            xt = start_layer(room)
            qT, OT = [room.take(NTOK), XN.rearrange("p t d -> p (t d)")], room.take(NTOK)
            kT = [room.take(NTOK) for _ in range(2)]
            probs, small, sel, work = room.take(NT, E), room.take(NT), room.take(NT, E), room.take(NT, E)
            tmp = [room.take(4, D) for _ in range(2)]
            diag = [room.take(NT, S // 2).bitcast(BF16) for _ in range(E)]
            block = room.take(P // 2).bitcast(BF16)
            late_room = Region(arena, LATE_LO, MID_LO)
            xR = [late_room.take(BT * HG * S) for _ in range(NT)]

            def columns_of(e):
                return slice(D * e, D * e + D)

            def queries_keys(e):
                c = columns_of(e)
                q = linear_cols(qT[e % 2], W["f0_wq"][:, c], XT, xt, bias=W["f0_bq"][:, e:e + 1], nextbank=hibank)
                k = linear_cols(kT[e % 2], W["f0_wk"][:, c], XT, xt, bias=W["f0_bk"][:, e:e + 1], nextbank=hibank)
                return [[a, b] for a, b in zip(q, k)]

            lg = linear_rows(XT, W["f0_rw"], xt, to_rows(probs, bias=W["f0_rb"]), nextbank=hibank)
            qk = {0: queries_keys(0)}
            m = softmax_rows(probs, E, small, *lg)
            copy(V, work, probs, m, chain=True)
            pick_largest(sel, work, NT, E, 2, room)
            tt(V, probs, probs, sel, ALU.mult)
            big = 2.0 ** 30
            ts(V, sel, sel, big, -big, ALU.mult, ALU.add)
            copy(V, block, C["block"])
            masks = [tt(V, diag[e], spread(C["rowid"], [P, NT, S], 1), spread(sel[:, :, e], [P, NT, S], 2), ALU.mult)
                     for e in range(E)]
            repeated = {}
            for i in range(NT):
                repeated[i] = (xR[i], repeat(xR[i], XT, i, xt[i // 4]))
            at = room.at
            rooms = [Region(arena, at, room.hi), Region(arena, late_room.at, MID_LO)]
            tmp_used = [[], []]

            def expert(e):
                r = Region(arena, rooms[e % 2].at, rooms[e % 2].hi)
                return head_attention(r, qT[e % 2], kT[e % 2], [[*m, masks[e]] for m in qk[e]], XT,
                                      W["f0_wv"][:, columns_of(e)], 0.5, OT, key_mask=lambda i: diag[e][:, i, :],
                                      bias_col=W["f0_bv"][:, e:e + 1], repeated=repeated, block=block)

            def output(e, q, m):
                b, freed = hibank()
                for j in range(4):
                    at = QW * q + P * j
                    m = mm(PS[:, b, P * j:P * j + P], OT[:, at:at + P], W["f0_wo"][:, columns_of(e)], freed, m,
                           mark=j == 3)
                w = tmp[q % 2]
                m = tt(V, w, PS[:, b, :].rearrange("p (a d) -> p a d", a=4),
                       spread(W["f0_bo"][:, columns_of(e)], [P, 4, D], 1), ALU.add, m, tmp_used[q % 2])
                free[b] = [m]
                m = tt(V, w, w, spread(probs[:, 4 * q:4 * q + 4, e], [P, 4, D], 2), ALU.mult)
                tmp_used[q % 2] = [tt(G, quarter(X, q), quarter(X, q), w, ALU.add, m)]

            start, run = expert(0)
            start()
            for e in range(E):
                def next_queries(e=e):
                    if e + 1 < E:
                        qk[e + 1] = queries_keys(e + 1)

                done = run(next_queries)
                if e + 1 < E:
                    start, run = expert(e + 1)
                    start()
                for q in range(NQ):
                    output(e, q, done[q])

        def L1_xattn(room):
            xt = start_layer(room)
            qT, kqT, qb = room.take(NTOK), room.take(NTOK), room.take(NTOK, parts=1)
            qm = linear_cols(qT, W["x1_WqT"], XT, xt, bias=W["x1_bq"])
            km = linear_cols(kqT, W["x1_Wk"], qT, qm)
            bm = linear_cols(qb, W["x1_bk"], qT, qm)
            O = room.take(NT, D)
            o = cross_attention(room, kqT, [[a, b] for a, b in zip(km, bm)], float(D) ** -0.5, O, row_term=qb)
            ot = rows_to_cols(qT, O, o)
            linear_rows(qT, W["x1_WvT"], ot, add_to_x(W["x1_bv"], room))

        def add_to_x(bias, room):
            tmp = [room.take(4, D) for _ in range(2)] if bias is not None else None

            def take(q, ps, m):
                if bias is None:
                    return tt(V, quarter(X, q), ps, quarter(X, q), ALU.add, m)
                m = tt(V, tmp[q % 2], ps, spread(bias, [P, 4, D], 1), ALU.add, m)
                tt(V, quarter(X, q), quarter(X, q), tmp[q % 2], ALU.add)
                return m
            return take

        def L1_attn(room):
            xt = start_layer(room)
            qT, kT = room.take(NTOK), room.take(NTOK)
            rows, ms = [room.take(NT, D) for _ in range(2)], [room.take(NT, H) for _ in range(2)]
            squares = [room.take(4 * H, HD) for _ in range(2)]
            squares_used, ready = {}, []
            for k, (w, dst) in enumerate((("a1_wqT", qT), ("a1_wkT", kT))):
                normed = []

                def take(q, ps, m, k=k):
                    n = NQ * k + q
                    r = quarter(rows[k], q).rearrange("p t (h d) -> p (t h) d", d=HD)
                    mq = quarter(ms[k], q).rearrange("p t h -> p (t h)")
                    c = copy(A, quarter(rows[k], q), ps, m)
                    m = act(squares[n % 2], ps.rearrange("p t (h d) -> p (t h) d", d=HD), ACT.Square, m,
                            squares_used.get(n - 2))
                    squares_used[n] = v = red(mq, squares[n % 2], ALU.add, m)
                    v = ts(V, mq, mq, 1.0 / HD, 1.1920929e-07, ALU.mult, ALU.add, v)
                    v = act(mq, mq, ACT.Sqrt, v)
                    recip(mq, mq, v)
                    normed.append(tt(V, r, r, spread(mq, [P, 4 * H, HD], 2), ALU.mult, c))
                    return m
                linear_rows(XT, W[w], xt, take)
                ready.append(rows_to_cols(dst, rows[k], normed))
            OT = room.take(NTOK)
            om = all_heads(room, qT, kT, [[a, b] for a, b in zip(*ready)], XT, W["a1_wvT"], float(1.0 / np.sqrt(np.float32(HD))), OT,
                                softcap=50.0)
            linear_rows(OT, W["a1_woT"], om, add_to_x(None, room))

        def gated_experts(room, experts, add_gate, n_hidden, hidden, down):
            hT = [room.take(n_hidden, QW) for _ in range(2)]
            tmp = [room.take(4, D) for _ in range(2)]
            h_used, tmp_used = [[], []], [[], []]
            pend = None

            def finish(e, q, k2, m):
                b, freed = bank()
                for j in range(4):
                    for f in range(n_hidden):
                        k = mm(PS[:, b, D * j:D * j + D], hT[k2][:, f, P * j:P * j + P], down(e, f), freed, *m,
                               start=f == 0, stop=f == n_hidden - 1, mark=(j, f) == (3, n_hidden - 1))
                h_used[k2] = [k]
                ps = PS[:, b, :].rearrange("p (a d) -> p a d", a=4)
                g = add_gate(e, q)
                if g is None:
                    k = copy(V, tmp[k2], ps, k, tmp_used[k2])
                else:
                    k = tt(V, tmp[k2], ps, spread(g, [P, 4, D], 2), ALU.mult, k, tmp_used[k2])
                free[b] = [k]
                tmp_used[k2] = [tt(G, quarter(X, q), quarter(X, q), tmp[k2], ALU.add, k)]

            n = 0
            for e in experts:
                for q in range(NQ):
                    k2 = n % 2
                    n += 1
                    ms = [hidden(e, q, f, hT[k2][:, f, :], h_used[k2]) for f in range(n_hidden)]
                    if pend is not None:
                        finish(*pend)
                    pend = (e, q, k2, ms)
            finish(*pend)

        def L1_ffn(room):
            E, HS = 8, 512
            xt = start_layer(room)
            sc, sel, work = room.take(NT, E), room.take(NT, E), room.take(NT, E)
            lg = linear_rows(XT, W["f1_rwT"], xt, to_rows(sc))
            m = act(sc, sc, ACT.Exp, *lg, scale=-1.0)
            ts(V, sc, sc, 1.0, None, ALU.add, None, m)
            recip(sc, sc)
            tt(V, work, sc, spread(W["f1_eb"], [P, NT, E], 1), ALU.add)
            pick_largest(sel, work, NT, E, 2, room)
            gm = tt(V, sc, sc, sel, ALU.mult)
            room.take(600)
            sg = [room.take(QW) for _ in range(3)]
            sg_used = [[] for _ in range(3)]
            turns = {"n": 0}

            def hidden(e, q, f, dst, marks):
                if e < E:
                    w1 = W["f1_w12T"][:, 256 * e:256 * e + P]
                    w2 = W["f1_w12T"][:, 256 * e + P:256 * e + 2 * P]
                else:
                    at = P * (4 * (e - E) + f)
                    w1, w2 = W["f1_s1T"][:, at:at + P], W["f1_s2T"][:, at:at + P]
                col = slice(QW * q, QW * q + QW)
                k = turns["n"] % 3
                turns["n"] += 1
                b1, f1 = bank()
                m1 = mm(PS[:, b1, :], w1, XT[:, col], f1, xt[q], mark=True)
                b2, f2 = bank()
                m2 = mm(PS[:, b2, :], w2, XT[:, col], f2, mark=True)
                m = act(sg[k], PS[:, b1, :], ACT.Silu, m1, sg_used[k])
                free[b1] = [m]
                m = tt(V, dst, PS[:, b2, :], sg[k], ALU.mult, m, m2, marks, chain=False)
                free[b2] = [m]
                sg_used[k] = [m]
                return m

            G.wait([gm])
            r = Region(arena, room.at, room.hi)
            gated_experts(r, range(E), lambda e, q: sc[:, 4 * q:4 * q + 4, e], 1, hidden,
                          lambda e, f: W["f1_w3T"][:, D * e:D * e + D])
            G.wait([PE.last])
            gated_experts(r, [E], lambda e, q: None, HS // P, hidden,
                          lambda e, f: W["f1_s3T"][:, D * f:D * f + D])

        def L2_xattn(room):
            xt = start_layer(room)
            hT, qT, cqT = room.take(NTOK), room.take(NTOK), room.take(NTOK)
            qb, kc = room.take(NTOK, parts=1), room.take(1)
            hm = linear_cols(hT, W["x2_hWT"], XT, xt, bias=W["x2_hb"])
            qm = linear_cols(qT, W["x2_qWT"], hT, hm, bias=W["x2_qb"])
            b, freed = bank()
            m = mm(PS[:, b, 0:1], W["x2_kWT"], W["x2_cb"], freed, mark=True)
            kcm = tt(V, kc, PS[:, b, 0:1], W["x2_kb"], ALU.add, m)
            free[b] = [kcm]
            km = linear_cols(hT, W["x2_kW"], qT, [[a, qm[-1]] for a in qm])
            cm = linear_cols(cqT, W["x2_cW"], hT, km)
            bm = linear_cols(qb, kc, qT, [[a, kcm] for a in qm])
            O = room.take(NT, D)
            o = cross_attention(room, cqT, [[a, b] for a, b in zip(cm, bm)], float(1.0 / np.sqrt(np.float32(D))), O,
                                row_term=qb)
            ot = rows_to_cols(cqT, O, o)
            c1 = linear_cols(hT, W["x2_cWT"], cqT, ot, bias=W["x2_cb"])
            v1 = linear_cols(cqT, W["x2_vWT"], hT, c1, bias=W["x2_vb"])
            sums = []
            for q, m in enumerate(v1):
                c = slice(QW * q, QW * q + QW)
                sums.append(tt(V, cqT[:, c], cqT[:, c], qT[:, c], ALU.add, m))
            linear_rows(cqT, W["x2_oWT"], sums, add_to_x(W["x2_ob"], room))

        def L2_attn(room):
            KEEP = min(S, max(1, int(np.log(S))))
            xt = start_layer(room)
            qT, kT = room.take(NTOK), room.take(NTOK)
            qm = linear_cols(qT, W["a2_wqT"], XT, xt, bias=W["a2_bq"])
            km = linear_cols(kT, W["a2_wkT"], XT, xt, bias=W["a2_bk"])

            def choose(mx, sm):
                r = Region(arena, room.at, room.hi)
                v, sel = r.take(2 * BT, S), r.take(2 * BT, S)
                mf = mx.rearrange("p t h -> p (t h)")
                b, freed = hibank()
                for g in range(2):
                    m = tr(PS[:, b, P * g:P * g + P], mf[:, P * g:P * g + P], freed, V.last, mark=g == 1)
                m = copy(V, v, PS[:, b, 0:2 * P].rearrange("p (a s) -> p a s", s=S), m, chain=True)
                free[b] = [m]
                m = pick_largest(sel, v, 2 * BT, S, KEEP, r)
                b, freed = hibank()
                sf = sel.rearrange("p a s -> p (a s)")
                for g in range(2):
                    m = tr(PS[:, b, P * g:P * g + P], sf[:, P * g:P * g + P], freed, m, mark=g == 1)
                recip(sm, sm)
                smf = sm.rearrange("p t h -> p (t h)")
                m = tt(V, smf, smf, PS[:, b, 0:2 * P], ALU.mult, m)
                free[b] = [m]
                return m

            OT = room.take(NTOK)
            om = all_heads(room, qT, kT, [[a, b] for a, b in zip(qm, km)], XT, W["a2_wvT"],
                                float(np.float32(1.0) / np.sqrt(np.float32(HD))), OT, bias_row=W["a2_bv"],
                                choose=choose)
            linear_rows(OT, W["a2_woT"], om, add_to_x(W["a2_bo"], room))

        def L2_ffn(room):
            E, F = 16, 512
            CAP = int(1.25 * NTOK / E)
            NSLOT = E * CAP
            xt = start_layer(room)
            probs, small, sel, work = room.take(NT, E), room.take(NT), room.take(NT, E), room.take(NT, E)
            zero = room.take(NSLOT // P * D)
            wslot = [(room.take(4 * P), room.take(4 * D)) for _ in range(4)]
            w_used = [[] for _ in range(4)]
            w_arr = [Arrivals(sem(f"s_w2_{i}")) for i in range(4)]

            def load(e):
                k = e % 4
                transfer(SP, wslot[k][0], t["f2_w1"][e], w_arr[k], *w_used[k])
                return transfer(SP, wslot[k][1], t["f2_w2"][e], w_arr[k])

            m = V.do(lambda e: e.memset(zero, 0.0))
            zeroed = transfer(SP, t["slots_in"].rearrange("(p a) d -> p (a d)", p=P), zero, arrived["scratch"], m)
            back = room.take(NT, D)
            cleared = G.do(lambda e: e.memset(back, 0.0))
            w_landed = {e: load(e) for e in range(4)}
            lg = linear_rows(XT, W["f2_gwT"], xt, to_rows(probs))
            m = softmax_rows(probs, E, small, *lg)
            copy(V, work, probs, m, chain=True)
            pick_largest(sel, work, NT, E, 1, room)
            room.take(1200)
            selh = room.take(NT * E // 2).bitcast(BF16)
            upto, ones = room.take(P // 2).bitcast(BF16), room.take(P // 2).bitcast(BF16)
            copy(V, selh, sel.rearrange("p t e -> p (t e)"), chain=True)
            before, other = room.take(NT, E), room.take(NT, E)
            V.do(lambda e: e.memset(before[:, 0:1, :], 0.0))
            copy(V, before[:, 1:NT, :], sel[:, 0:NT - 1, :])
            d = 1
            while d < NT:
                copy(V, other[:, 0:d, :], before[:, 0:d, :], chain=True)
                tt(V, other[:, d:NT, :], before[:, d:NT, :], before[:, 0:NT - d, :], ALU.add)
                before, other, d = other, before, 2 * d
            beforeh = room.take(NT * E // 2).bitcast(BF16)
            copy(V, beforeh, before.rearrange("p t e -> p (t e)"), chain=True)
            copy(V, upto, C["upto"])
            m = copy(V, ones, C["ones"])
            b, freed = bank()
            mm(PS[:, b, 0:NT * E], upto, selh, freed, m, start=True, stop=False)
            m = mm(PS[:, b, 0:NT * E], ones, beforeh, start=False, stop=True, mark=True)
            loc = PS[:, b, 0:NT * E].rearrange("p (t e) -> p t e", e=E)
            fit = work
            ts(V, fit, loc, float(CAP) + 0.5, None, ALU.is_lt, None, m)
            tt(V, fit, fit, sel, ALU.mult)
            place = sel
            m = stt(place, loc, -1.0, spread(C["slotbase"], [P, NT, E], 1), ALU.add, ALU.add)
            free[b] = [m]
            ts(V, place, place, -float(2 * NSLOT), None, ALU.add, None)
            tt(V, place, place, fit, ALU.mult)
            slotf, slot, gate = room.take(NT), room.take(NT).bitcast(I32), room.take(NT)
            red(slotf, place, ALU.add)
            ts(V, slotf, slotf, float(2 * NSLOT), None, ALU.add, None)
            sm_ = copy(V, slot, slotf, chain=True)
            tt(V, probs, probs, fit, ALU.mult)
            gm = red(gate, probs, ALU.add)
            slot_u = slot.bitcast(mybir.dt.uint32)
            G.wait([sm_, zeroed])
            for i in range(NT):
                G.steps.append(lambda e, i=i: e.indirect_dma_start(
                    t["slots_in"][:, :], bass.IndirectOffsetOnAxis(ap=slot_u[:, i:i + 1], axis=0), XN[:, i, :], None,
                    bounds_check=NSLOT - 1, oob_is_err=False).then_inc(arrived["scattered"].sem, 16))
                arrived["scattered"].total += 16
            NST = NSLOT // P
            rows = room.take(NST, D)
            got = transfer(SP, rows, t["slots_in"].rearrange("(a p) d -> p a d", p=P), arrived["scratch"],
                           arrived["scattered"].mark)
            sT = room.take(NSLOT)
            turned = []
            for a in range(NST // 4):
                b, freed = bank()
                for j in range(4):
                    m = tr(PS[:, b, P * j:P * j + P], rows[:, 4 * a + j, :], freed, got, mark=j == 3)
                m = copy((A, V)[a % 2], sT[:, 512 * a:512 * a + 512], PS[:, b, :], m)
                free[b] = [m]
                turned.append(m)
            HC = CAP // 2
            hT = [room.take(4, CAP) for _ in range(2)]
            yo = [room.take(2, D, parts=HC) for _ in range(2)]
            h_used, y_used = [[], []], [[], []]
            y_arr = [Arrivals(sem(f"s_y2_{i}")) for i in range(2)]
            for e in range(E):
                k, k2 = e % 4, e % 2
                w1, w2 = wslot[k]
                c = slice(CAP * e, CAP * e + CAP)
                for f in range(4):
                    b, freed = bank()
                    m = mm(PS[:, b, 0:CAP], w1[:, P * f:P * f + P], sT[:, c], freed, w_landed[e], *turned, mark=True)
                    m = act(hT[k2][:, f, :], PS[:, b, 0:CAP], ACT.Relu, m, h_used[k2])
                    free[b] = [m]
                b, freed = bank()
                for j in range(2):
                    for f in range(4):
                        m2 = mm(PS[0:HC, b, D * j:D * j + D], hT[k2][:, f, HC * j:HC * j + HC],
                                w2[:, D * f:D * f + D], freed, m, start=f == 0, stop=f == 3, mark=(j, f) == (1, 3))
                h_used[k2] = w_used[k] = [m2]
                m = copy(V, yo[k2], PS[0:HC, b, 0:2 * D].rearrange("p (a d) -> p a d", a=2), m2, y_used[k2])
                free[b] = [m]
                y_used[k2] = [transfer(SP, t["slots_out"][c, :].rearrange("(a p) d -> p a d", p=HC), yo[k2],
                                       y_arr[k2], m)]
                if e + 4 < E:
                    w_landed[e + 4] = load(e + 4)
            G.wait([y_arr[0].mark, y_arr[1].mark, cleared])
            for i in range(NT):
                G.steps.append(lambda e, i=i: e.indirect_dma_start(
                    back[:, i, :], None, t["slots_out"][:, :], bass.IndirectOffsetOnAxis(ap=slot_u[:, i:i + 1], axis=0),
                    bounds_check=NSLOT - 1, oob_is_err=False).then_inc(arrived["gathered"].sem, 16))
                arrived["gathered"].total += 16
            V.wait([arrived["gathered"].mark])
            tt(V, back, back, per_token(gate), ALU.mult)
            tt(V, X, X, back, ALU.add)

        def L3_xattn(room):
            NH, DH = 16, 64
            UL = U + S
            NS = 3
            kr = [room.take(BT * 2, D) for _ in range(NS)]
            kr_used = [[] for _ in range(NS)]

            def load(i):
                return transfer(SP, kr[i % NS], t["ctxR"][i].rearrange("p (a d) -> p a d", d=D), row_slots[i % NS],
                                *kr_used[i % NS])

            landed = {i: load(i) for i in range(NS)}
            last = room.take(D, parts=NB)
            last_landed = transfer(SP, last, t["ctx_last"], key_slots[0])
            qk, vo = room.take(NH, D), room.take(NH, D)
            scale = DH ** -0.5
            for dst, half in ((qk, slice(0, DH)), (vo, slice(DH, 2 * DH))):
                for g in range(4):
                    b, freed = bank()
                    for j in range(4):
                        h = 4 * g + j
                        m = mm(PS[:, b, P * j:P * j + P], W["x3_left"][half, P * h:P * h + P],
                               W["x3_right"][half, P * h:P * h + P],
                               freed, mark=j == 3)
                    o, ps = dst[:, 4 * g:4 * g + 4, :], PS[:, b, :].rearrange("p (a d) -> p a d", a=4)
                    if dst is qk:
                        m = act(o, ps, ACT.Copy, m, scale=scale)
                    else:
                        m = copy(A, o, ps, m)
                    free[b] = [m]
            spent = PE.last
            lat, small = XN, room.take(NT, 8)
            xt0 = normalise(XN, X, 1e-5, small)
            lm = normalise(lat, XN, 1e-5, small, [[m] for m in xt0], gamma=W["x3_g2"], beta=W["x3_b2"])
            lt = rows_to_cols(XT, lat, lm)
            n3 = S + 1
            v3 = room.take(NB, D, parts=n3)
            lsq, lst = room.take(D, parts=NB), room.take(2, parts=NB)
            lastT = room.take(NB)
            a = arrived["scratch"]
            transfer(SP, t["lat_rows"].rearrange("(t p) d -> p t d", p=P), lat, a, *lm)
            V.wait([last_landed])
            g1, b1 = W["x3_g1"], W["x3_b1"]

            def norm_small(x, sq, st2, n):
                m = red(st2[:, 0:1], x, ALU.add)
                ts(V, st2[:, 0:1], st2[:, 0:1], -1.0 / D, None, ALU.mult, None)
                ts(V, x, x, st2[:, 0:1], None, ALU.add, None)
                tt(V, sq, x, x, ALU.mult)
                red(st2[:, 1:2], sq, ALU.add)
                ts(V, st2[:, 1:2], st2[:, 1:2], 1.0 / D, 1e-5, ALU.mult, ALU.add)
                inverse_root(st2[:, 1:2])
                stt(x, x, st2[:, 1:2], g1[0:n, :], ALU.mult, ALU.mult)
                return tt(V, x, x, b1[0:n, :], ALU.add)

            m = norm_small(last, lsq, lst, NB)
            transfer(SP, t["last_rows"], last, a, m)
            transfer(SP, v3[0:S], t["lat_rows"].rearrange("(b s) d -> s b d", s=S), a, a.mark)
            v3m = transfer(SP, v3[S:n3], t["last_rows"].rearrange("b d -> (b d)").unsqueeze(0).rearrange(
                "o (b d) -> o b d", d=D), a)
            b, freed = bank()
            m = tr(PS[:, b, 0:NB], last, freed, m, mark=True)
            lastTm = copy(V, lastT, PS[:, b, 0:NB], m)
            free[b] = [lastTm]
            kst = room.take(BT * 2, 8)
            kt = [room.take(BT, UL) for _ in range(NS)]
            qt = [W[f"x3_{side}"].rearrange("p (b n) -> p b n", b=BT) for side in ("left", "right")]
            pr = [room.take(4, UL) for _ in range(2)]
            pT = [room.take(3, NH * S) for _ in range(2)]
            oT = [room.take(NH, P) for _ in range(2)]
            st = room.take(2, 12)
            kt_used, qt_used = [[] for _ in range(NS)], [[spent], [spent]]
            oT_used, pT_used, pr_used = [[], []], [[], []], [[], []]
            s_used = [free[g] for g in range(4)]

            def key_stats(i):
                k = kr[i % NS]
                V.wait([landed[i]])
                for j in range(BT * 2):
                    V.do(lambda e, j=j: e.bn_stats(kst[:, j, 0:6], k[:, j, :]), [])
                m = V.last
                for j in range(BT * 2):
                    a = V.do(lambda e, j=j: e.bn_aggr(kst[:, j, 6:8], kst[:, j, 0:6]), [m])
                var = kst[:, :, 7]
                return root(var, ts(V, var, var, 1e-5, None, ALU.add, None, a))

            def key_norm(i, m):
                k = kr[i % NS]
                w = [P, BT * 2, D]
                V.wait([m])
                for j in range(BT * 2):
                    m = ts(V, k[:, j, :], k[:, j, :], kst[:, j, 6:7], kst[:, j, 7:8], ALU.subtract, ALU.mult, chain=False)
                tt(G, k, k, spread(g1, w, 1), ALU.mult, m)
                m = tt(G, k, k, spread(b1, w, 1), ALU.add)
                kk = kt[i % NS]
                c0 = copy(G, kk[:, :, UA:UA + S], XT[:, P * i:P * i + P].rearrange("p (b s) -> p b s", s=S),
                          kt_used[i % NS], lt)
                c1 = copy(G, kk[:, :, UA + S:UL], lastT[:, BT * i:BT * i + BT].unsqueeze(2), lastTm)
                return [m, c0, c1]

            def key_turn(i, marks):
                k, kk = kr[i % NS], kt[i % NS]
                out_marks = list(marks)
                for g in range(2):
                    b, freed = hibank()
                    for j in range(4):
                        x = tr(PS[:, b, P * j:P * j + P], k[:, 4 * g + j, :], freed, marks, mark=j == 3)
                    c = copy(A, kk[:, 2 * g:2 * g + 2, 0:UA], PS[:, b, :].rearrange("p (b s) -> p b s", s=UA), x,
                             kt_used[i % NS])
                    free[b] = [c]
                    out_marks.append(c)
                return out_marks

            def queries(i):
                marks = []
                for g in range(4):
                    b, freed = hibank()
                    for j in range(4):
                        m = mm(PS[:, b, P * j:P * j + P], qk[:, 4 * g + j, :], XT[:, P * i:P * i + P], freed, lt,
                               mark=j == 3)
                    src = PS[:, b, :].rearrange("p (h b s) -> p h b s", h=4, s=S)
                    dst = qt[i % 2].rearrange("p b (h s) -> p h b s", s=S)[:, 4 * g:4 * g + 4]
                    m = copy((A, V)[g % 2], dst, src, m, qt_used[i % 2])
                    free[b] = [m]
                    marks.append(m)
                return marks

            def scores(n, ready):
                i, j, h = n // BT, n % BT, n % 2
                least, exps = st[:, h, 0:4], []
                for g in range(4):
                    m = mm(PS[:, g, 0:UL], qt[i % 2][:, j, P * g:P * g + P], kt[i % NS][:, j, :], s_used[g], ready,
                           mark=True)
                    k = V.do(lambda e, g=g: e.tensor_reduce(least[:, g:g + 1], PS[:, g, 0:UL], AXX, ALU.max,
                                                            negate=True), [m])
                    k = act(pr[h][:, g, :], PS[:, g, 0:UL], ACT.Exp, k, pr_used[h], bias=least[:, g:g + 1],
                            accum_out=st[:, h, 4 + g:5 + g])
                    s_used[g] = [k]
                    exps.append(k)
                if j == BT - 1:
                    qt_used[i % 2], kt_used[i % NS] = [m], [m]
                return exps

            def normal(n, exps):
                h, marks = n % 2, []
                for g in range(4):
                    if g % 2 == 0:
                        r = recip(st[:, h, 8 + g:10 + g], st[:, h, 4 + g:6 + g], exps[g], exps[g + 1])
                    marks.append(ts(V, pr[h][:, g, :], pr[h][:, g, :], st[:, h, 8 + g:9 + g], None, ALU.mult, None, r,
                                    chain=False))
                return marks

            def turn(n, m):
                h, marks = n % 2, []
                hibanks_from(4)
                for k in range(3):
                    b, freed = hibank()
                    n_, c = (P, slice(P * k, P * k + P)) if k < 2 else (n3, slice(UA, UL))
                    for g in range(4):
                        x = tr(PS[0:n_, b, P * g:P * g + P], pr[h][:, g, c], freed, m[g], mark=g == 3)
                    x = copy((A, V, A)[k], pT[h][0:n_, k, :], PS[0:n_, b, :], x, pT_used[h])
                    free[b] = [x]
                    marks.append(x)
                pr_used[h] = [PE.last]
                return marks

            def weigh(n, marks):
                i, j, h = n // BT, n % BT, n % 2
                b, freed = hibank()
                k, d = kr[i % NS], pT[h]
                mm(PS[:, b, :], k[:, 2 * j, :], d[:, 0, :], freed, marks, start=True, stop=False)
                mm(PS[:, b, :], k[:, 2 * j + 1, :], d[:, 1, :], start=False, stop=False)
                m = mm(PS[:, b, :], v3[:, n, :], d[0:n3, 2, :], v3m, start=False, stop=True, mark=True)
                pT_used[h] = [m]
                m = copy((A, V)[h], oT[i % 2][:, :, S * j:S * j + S],
                         PS[:, b, :].rearrange("p (h s) -> p h s", s=S), m, oT_used[i % 2])
                free[b] = [m]
                return m

            def project(i, marks):
                b, freed = hibank()
                for h in range(NH):
                    m = mm(PS[:, b, 0:D], oT[i % 2][:, h, :], vo[:, h, :], freed, marks, start=h == 0,
                           stop=h == NH - 1, mark=h == NH - 1)
                oT_used[i % 2] = [m]
                m = tt(V, X[:, i, :], PS[:, b, 0:D], X[:, i, :], ALU.add, m)
                free[b] = [m]

            ready = {0: [key_turn(0, key_norm(0, key_stats(0))), queries(0)]}
            outs = {i: [] for i in range(NT)}
            exps = {0: scores(0, ready[0])}
            turned = {}
            for n in range(NB + 1):
                i, j = n // BT, n % BT
                if n < NB:
                    scaled = normal(n, exps.pop(n))
                    if n + 1 < NB:
                        exps[n + 1] = scores(n + 1, ready[(n + 1) // BT])
                    turned[n] = turn(n, scaled)
                if i + 1 < NT and j == 0:
                    stats_m = key_stats(i + 1)
                if i + 1 < NT and j == 1:
                    norm_m = key_norm(i + 1, stats_m)
                if n:
                    outs[(n - 1) // BT].append(weigh(n - 1, turned.pop(n - 1)))
                if j == 0 and n:
                    kr_used[(i - 1) % NS] = [PE.last]
                    if i - 1 + NS < NT:
                        landed[i - 1 + NS] = load(i - 1 + NS)
                if i + 1 < NT and j == 0:
                    ready[i + 1] = [queries(i + 1)]
                if j == 0 and n:
                    project(i - 1, outs[i - 1])
                if i + 1 < NT and j == 2:
                    ready[i + 1].append(key_turn(i + 1, norm_m))

        def L3_attn(room):
            NP, J, Cn = 16, 16, 4
            JU, NU = J // 2, 2 * Cn
            xt = start_layer(room, by_position=True)
            z = room.take(NP, 4 * D)
            zm = []
            for c in range(Cn):
                zm.append([])
                for g in range(4):
                    b, freed = bank()
                    for k in range(4):
                        h = 4 * g + k
                        m = mm(PS[:, b, P * k:P * k + P], XT[:, P * h:P * h + P], W["a3_w"][:, P * c:P * c + P], freed,
                               *xt, mark=k == 3)
                    m = copy(A if c or g % 2 == 0 else V, z[:, 4 * g:4 * g + 4, P * c:P * c + P],
                             PS[:, b, :].rearrange("p (a d) -> p a d", a=4), m)
                    free[b] = [m]
                    zm[c].append(m)
            z6 = z.rearrange("p h (c r j e) -> p c r e j h", c=Cn, r=4, e=2)
            pa, pb, ex = ([room.take(JU, NP * NP) for _ in range(2)] for _ in range(3))
            vp = [room.take(2, JU * NP * NP) for _ in range(2)]
            least, total = room.take(2, JU * NP), room.take(2, JU * NP)
            mixed = room.take(2, 2 * JU * NP)
            o = XN.rearrange("p t d -> p (t d)").rearrange("p (c h f) -> p c h f", c=Cn, h=NP)
            back = [z[:, 0:4, P * c:P * c + P] for c in range(Cn)]
            backT = XT
            scale = float(2 ** -0.5)
            made, least_m, exp_m, mixed_m, added, subtracted = {}, {}, {}, {}, {}, {}

            def feature(u, r, e):
                return z6[:, u // 2, r, e, JU * (u % 2):JU * (u % 2) + JU, :]

            def four(ap):
                return ap.rearrange("p j (h g) -> p j h g", h=NP)

            wide = [P, JU, NP, NP]

            def products(u):
                k = u % 2
                made[u] = [tt(G, four(pa[k]), spread(feature(u, 0, 0), wide, 3), spread(feature(u, 1, 0), wide, 2),
                              ALU.mult, zm[u // 2], added.get(u - 2), chain=False),
                           tt((V, G)[k], four(pb[k]), spread(feature(u, 0, 1), wide, 3),
                              spread(feature(u, 1, 1), wide, 2), ALU.mult, zm[u // 2], added.get(u - 2), chain=False)]

            def banks(u):
                return range(4 * (u % 2), 4 * (u % 2) + 4)

            def add_products(u):
                for n, b in enumerate(banks(u)):
                    mm(PS[:, b, :], C["ident"], pa[u % 2][:, 2 * n:2 * n + 2, :], free[b], made[u],
                       start=True, stop=False)
                    m = mm(PS[:, b, :], C["ident"], pb[u % 2][:, 2 * n:2 * n + 2, :], start=False, stop=True,
                           mark=True)
                added[u] = m

            def rows_of(u):
                return PS[:, 4 * (u % 2):4 * (u % 2) + 4, :].rearrange("p b (r g) -> p (b r) g", g=NP)

            def maxima(u):
                out = least[:, u % 2]
                least_m[u] = V.do(lambda e: e.tensor_reduce(out, rows_of(u), AXX, ALU.max, negate=True),
                                  [added[u], subtracted.get(u - 2)])

            def subtract(u):
                for n, b in enumerate(banks(u)):
                    w = 2 * NP
                    x = spread(least[:, u % 2, w * n:w * n + w], [P, w, NP], 2)
                    m = mm(PS[:, b, :].rearrange("p (r g) -> p r g", g=NP), C["ident"], x, least_m[u], start=False,
                           stop=True, mark=True, check=False)
                subtracted[u] = m
                e = act(ex[u % 2].rearrange("p j g -> p (j g)").rearrange("p (b n) -> p b n", b=4),
                        PS[:, 4 * (u % 2):4 * (u % 2) + 4, :], ACT.Exp, m, mixed_m.get(u - 2), scale=scale)
                exp_m[u] = e
                for b in banks(u):
                    free[b] = [e]

            def weigh(u):
                k = u % 2
                e4 = four(ex[k])
                v2 = vp[k].rearrange("p e (j h g) -> p e j h g", j=JU, h=NP)
                v0 = tt(G, v2[:, 0], e4, spread(feature(u, 2, 0), wide, 2), ALU.mult, exp_m[u], mixed_m.get(u - 2),
                        chain=False)
                red(total[:, k], ex[k].rearrange("p j (h g) -> p (j h) g", h=NP), ALU.add, exp_m[u], chain=False)
                v1 = tt(V, v2[:, 1], e4, spread(feature(u, 2, 1), wide, 2), ALU.mult, chain=False)
                recip(total[:, k], total[:, k])
                red(mixed[:, k], vp[k].rearrange("p e (r g) -> p (e r) g", g=NP), ALU.add, v0, v1)
                mixed3 = mixed[:, k].rearrange("p (e r) -> p e r", e=2)
                tt(V, mixed3, mixed3, spread(total[:, k], [P, 2, JU * NP], 1), ALU.mult)
                half = slice(D // 4 // 2 * (u % 2), D // 4 // 2 * (u % 2) + D // 4 // 2)
                dst = o[:, u // 2, :, half].rearrange("p h (j e) -> p e j h", e=2)
                for e in range(2):
                    m = tt(V, dst[:, e], mixed3[:, e].rearrange("p (j h) -> p j h", h=NP), feature(u, 3, e), ALU.mult,
                           chain=e == 0)
                mixed_m[u] = m

            def project(c):
                a = mixed_slots[c]
                for r in range(2):
                    m = transfer(SP, t["mixed"][c].rearrange("b (h r f) -> r b h f", h=NP, r=2)[r],
                                 o[NB * r:NB * r + NB, c], a, mixed_m[2 * c + 1])
                return transfer(SP, back[c],
                                t["mixed"][c].rearrange("b (i d) -> (b i) d", d=D).rearrange("(t p) d -> p t d", p=P),
                                a, m)

            def finish(c, got, b):
                for j in range(4):
                    m = tr(PS[:, b, P * j:P * j + P], back[c][:, j, :], free[b], got, mark=j == 3)
                bt = backT[:, QW * c:QW * c + QW]
                m = copy(A, bt, PS[:, b, :], m)
                for j in range(4):
                    m = mm(PS[:, b, P * j:P * j + P], bt[:, P * j:P * j + P], W["a3_wo"], m, mark=j == 3)
                x = quarter(X, c)
                m = tt(V, x, PS[:, b, :].rearrange("p (a d) -> p a d", a=4), x, ALU.add, m)
                free[b] = [m]

            fetched = {}
            products(0)
            add_products(0)
            for u in range(NU + 1):
                if u + 1 < NU:
                    products(u + 1)
                if u < NU:
                    maxima(u)
                    subtract(u)
                if u + 1 < NU:
                    add_products(u + 1)
                if u:
                    weigh(u - 1)
                    if u % 2 == 0:
                        fetched[u // 2 - 1] = project(u // 2 - 1)
            for c in range(Cn):
                finish(c, fetched[c], c)

        def L3_ffn(room):
            E, F = 8, 512
            small = room.take(NT, 8)
            m = normalise(XN, X, 1e-5, small)
            hr = room.take(NT, D)
            m = normalise(hr, XN, 1e-5, small, [[k] for k in m], gamma=W["f3_g1"], beta=W["f3_b1"])
            xt = rows_to_cols(XT, hr, m)
            base = room.at
            qT, kT, OT = room.take(NTOK), room.take(NTOK), room.take(NTOK)
            qm = linear_cols(qT, W["f3_Wq"], XT, xt)
            km = linear_cols(kT, W["f3_Wk"], XT, xt)
            om = all_heads(room, qT, kT, [[a, b] for a, b in zip(qm, km)], XT, W["f3_Wv"],
                                float(1.0 / np.sqrt(np.float32(HD))), OT)
            linear_rows(OT, W["f3_Wo"], om, lambda q, ps, m: tt(V, quarter(XN, q), ps, quarter(XN, q), ALU.add, m))
            barrier()
            room = Region(arena, base, room.hi)
            m = normalise(hr, XN, 1e-5, small, gamma=W["f3_g2"], beta=W["f3_b2"])
            tt(G, X, X, XN, ALU.add, *m)
            xt = rows_to_cols(XT, hr, m)
            probs, sel, work, sm = room.take(NT, E), room.take(NT, E), room.take(NT, E), room.take(NT)
            lg = linear_rows(XT, W["f3_Wg"], xt, to_rows(probs))
            m = softmax_rows(probs, E, sm, *lg)
            copy(V, work, probs, m, chain=True)
            pick_largest(sel, work, NT, E, 2, room)
            room.take(600)
            tt(V, probs, probs, sel, ALU.mult)
            red(sm, probs, ALU.add)
            recip(sm, sm)
            gm = tt(V, probs, probs, spread(sm, [P, NT, E], 2), ALU.mult)
            def hidden(e, q, f, dst, marks):
                b, freed = bank()
                at = F * e + P * f
                m = mm(PS[:, b, :], W["f3_W1"][:, at:at + P], XT[:, QW * q:QW * q + QW], freed, xt[q], mark=True)
                m = act(dst, PS[:, b, :], ACT.Gelu_apprx_tanh, m, marks, bias=W["f3_b1f"][:, 4 * e + f:4 * e + f + 1])
                free[b] = [m]
                return m

            gated_experts(room, range(E), lambda e, q: probs[:, 4 * q:4 * q + 4, e], F // P, hidden,
                          lambda e, f: W["f3_W2"][:, D * (4 * e + f):D * (4 * e + f) + D])

            V.wait([G.last])
            wT = room.take(NTOK, parts=E)
            for q in range(NQ):
                b, freed = bank()
                for j in range(4):
                    m = tr(PS[0:E, b, P * j:P * j + P], probs[:, 4 * q + j, :], freed, gm, mark=j == 3)
                m = copy(A, wT[:, QW * q:QW * q + QW], PS[0:E, b, :], m)
                free[b] = [m]
                b, freed = bank()
                for j in range(4):
                    at = QW * q + P * j
                    m = mm(PS[:, b, D * j:D * j + D], wT[:, at:at + P], W["f3_bo"][0:E, :], freed, m, mark=j == 3)
                m = tt(V, quarter(X, q), PS[:, b, :].rearrange("p (a d) -> p a d", a=4), quarter(X, q), ALU.add, m)
                free[b] = [m]

        order = [L0_xattn, L0_attn, L0_ffn, L1_xattn, L1_attn, L1_ffn, L2_xattn, L2_attn, L2_ffn,
                 L3_xattn, L3_attn, L3_ffn]
        mid = late = None
        for n in LAYERS:
            if n >= 2 and mid is None:
                mid = transfer(SP, mid_words, t["mid"], arrived["mid"])
            if n >= 4 and late is None:
                late = transfer(SP, late_words, t["late"], arrived["late"])
            if n >= 1:
                for lane in (PE, V, A, G):
                    lane.wait([arrived["w0"].mark])
            if n >= 3:
                for lane in (PE, V, A, G):
                    lane.wait([mid])
                SP.wait([arrived["w0"].mark])
            if n >= 9:
                for lane in (PE, V, A, G):
                    lane.wait([late])
                SP.wait([mid])
            order[n](Region(arena, *scratch[n]))
            barrier()

        rows_out = out.rearrange("b s d -> (b s) d").rearrange("(t p) d -> p t d", p=P)
        transfer(SP, rows_out, X, arrived["out"], V.last, G.last)
        SP.wait([a.mark for a in arrived.values()])

        block = stack.enter_context(nc.Block())

        @block.tensor
        def _(e):
            PE.play(e)

        @block.vector
        def _(e):
            V.play(e)

        @block.scalar
        def _(e):
            A.play(e)

        @block.gpsimd
        def _(e):
            G.play(e)

        @block.sync
        def _(e):
            SP.play(e)


def constants():
    p = np.arange(P)
    rows = {
        "ident": np.eye(P),
        "ones": np.ones((P, P)),
        "upto": p[:, None] <= p[None, :],
        "block": p[:, None] // S == p[None, :] // S,
        "headmask": (p[:, None] // HD) % HG == np.arange(HG),
        "rowmask": p[:, None] // S == np.arange(BT),
        "causal": np.where(np.arange(S)[None, :] <= p[:, None] % S, 0.0, -BIG),
        "ramp": np.broadcast_to(S - np.arange(S), (P, S)),
        "rowid": p[:, None] % S == np.arange(S),
        "minus_half": np.full((P, 1), -0.5),
        "select": (p[:, None] % 32 == np.arange(32)) & (p[:, None] < 96),
        "slotbase": np.broadcast_to(np.arange(16) * int(1.25 * NTOK / 16), (P, 16)),
    }
    return np.concatenate([np.asarray(rows[n], np.float32) for n, _ in CONST_PACK], axis=1)


def kernel(**inputs):
    import concourse.bacc as bacc
    from concourse.bass_utils import run_bass_kernel_spmd

    a = {k: np.asarray(v) for k, v in inputs.items()}

    def col(v):
        return v.reshape(P, 1)

    def row(v):
        return np.broadcast_to(v.reshape(1, -1), (P, v.size))

    def stacked(w):
        return w.transpose(1, 0, 2).reshape(P, -1)

    def deep(w):
        return w.reshape(w.shape[0], -1, P, w.shape[-1]).transpose(2, 0, 1, 3).reshape(P, -1)

    def pad(w):
        return np.concatenate([w, np.zeros((P - w.shape[0],) + w.shape[1:], w.dtype)], axis=0)

    Wkv = a["L3_xattn_Wkv"]

    def heads_T(w):
        return w.reshape(P, 16, 64).transpose(2, 1, 0).reshape(64, -1)

    parts = {
        "x0_W1": a["L0_xattn_W1"], "x0_W2": a["L0_xattn_W2"], "x0_b1": col(a["L0_xattn_b1"]),
        "x0_b2": row(a["L0_xattn_b2"]), "x0_gamma": row(a["L0_xattn_gamma"]), "x0_beta": row(a["L0_xattn_beta"]),
        "a0_A": a["L0_attn_A_log"], "a0_D": col(a["L0_attn_D_param"]), "a0_Wdelta": a["L0_attn_W_delta"],
        "a0_bdelta": col(a["L0_attn_b_delta"]),
        "a0_WBC": np.concatenate([a["L0_attn_W_B"], a["L0_attn_W_C"]] * 3, axis=1),
        "a0_Wr": a["L0_attn_W_router"], "a0_Wg": stacked(a["L0_attn_Wg"]), "a0_Wu": stacked(a["L0_attn_Wu"]),
        "a0_Wd": deep(a["L0_attn_Wd"]), "a0_wn": a["L0_attn_wn_exp"].reshape(8, P).T,
        "a0_normw": row(a["L0_attn_norm_w"]),
        "f0_rw": a["L0_ffn_router_w"], "f0_rb": row(a["L0_ffn_router_b"]), "f0_wq": stacked(a["L0_ffn_wq"]),
        "f0_wk": stacked(a["L0_ffn_wk"]), "f0_wv": stacked(a["L0_ffn_wv"]), "f0_wo": stacked(a["L0_ffn_wo"]),
        "f0_bq": a["L0_ffn_bq"].T, "f0_bk": a["L0_ffn_bk"].T, "f0_bv": a["L0_ffn_bv"].T, "f0_bo": row(a["L0_ffn_bo"]),
        "x1_WqT": a["L1_xattn_Wq"].T, "x1_Wk": a["L1_xattn_Wk"], "x1_WvT": a["L1_xattn_Wv"].T,
        "x1_bq": col(a["L1_xattn_bq"]), "x1_bk": col(a["L1_xattn_bk"]), "x1_bv": row(a["L1_xattn_bv"]),
        "a1_wqT": a["L1_attn_w_q"].T, "a1_wkT": a["L1_attn_w_k"].T, "a1_wvT": a["L1_attn_w_v"].T,
        "a1_woT": a["L1_attn_w_o"].T,
        "f1_w12T": a["L1_ffn_w12"].transpose(2, 0, 1).reshape(P, -1),
        "f1_w3T": a["L1_ffn_w3"].transpose(2, 0, 1).reshape(P, -1),
        "f1_s1T": a["L1_ffn_shared_w1"].T, "f1_s2T": a["L1_ffn_shared_w2"].T,
        "f1_s3T": deep(a["L1_ffn_shared_w3"].T[None]), "f1_rwT": a["L1_ffn_router_w"].T,
        "f1_eb": row(a["L1_ffn_expert_bias"]),
        "x2_hWT": a["L2_xattn_hW"].T, "x2_cW": a["L2_xattn_cW"], "x2_cWT": a["L2_xattn_cW"].T,
        "x2_qWT": a["L2_xattn_qW"].T, "x2_kW": a["L2_xattn_kW"], "x2_kWT": a["L2_xattn_kW"].T,
        "x2_vWT": a["L2_xattn_vW"].T, "x2_oWT": a["L2_xattn_oW"].T, "x2_hb": col(a["L2_xattn_hb"]),
        "x2_cb": col(a["L2_xattn_cb"]), "x2_qb": col(a["L2_xattn_qb"]), "x2_kb": col(a["L2_xattn_kb"]),
        "x2_vb": col(a["L2_xattn_vb"]), "x2_ob": row(a["L2_xattn_ob"]),
        "a2_wqT": a["L2_attn_wq"].T, "a2_wkT": a["L2_attn_wk"].T, "a2_wvT": a["L2_attn_wv"].T,
        "a2_woT": a["L2_attn_wo"].T, "a2_bq": col(a["L2_attn_bq"]), "a2_bk": col(a["L2_attn_bk"]),
        "a2_bv": row(a["L2_attn_bv"]), "a2_bo": row(a["L2_attn_bo"]), "f2_gwT": a["L2_ffn_gate_w"].T,
        "x3_g1": row(a["L3_xattn_ln1_g"]), "x3_b1": row(a["L3_xattn_ln1_b"]), "x3_g2": row(a["L3_xattn_ln2_g"]),
        "x3_b2": row(a["L3_xattn_ln2_b"]),
        "x3_left": np.concatenate([heads_T(a["L3_xattn_Wq"]), heads_T(Wkv[:, 1024:2048])], axis=0),
        "x3_right": np.concatenate([heads_T(Wkv[:, 0:1024]),
                                    a["L3_xattn_Wo"].reshape(16, 64, D).transpose(1, 0, 2).reshape(64, -1)], axis=0),
        "a3_w": a["L3_attn_w_qkvw"], "a3_wo": a["L3_attn_w_out"],
        "f3_g1": row(a["L3_ffn_ln1_g"]), "f3_b1": row(a["L3_ffn_ln1_b"]), "f3_g2": row(a["L3_ffn_ln2_g"]),
        "f3_b2": row(a["L3_ffn_ln2_b"]),
        "f3_Wq": a["L3_ffn_Wq"], "f3_Wk": a["L3_ffn_Wk"], "f3_Wv": a["L3_ffn_Wv"], "f3_Wo": a["L3_ffn_Wo"],
        "f3_Wg": a["L3_ffn_Wg"], "f3_W1": stacked(a["L3_ffn_W1"]),
        "f3_b1f": a["L3_ffn_b1"].reshape(32, P).T, "f3_W2": deep(a["L3_ffn_W2"]), "f3_bo": pad(a["L3_ffn_b2"]),
    }
    ctx = a["ctx_1024"]
    rows = ctx[:, 0:UA].reshape(NT, BT, 2, P, D)
    arrays = {
        "x": a["x"].reshape(NTOK, D),
        "const": constants(),
        "w0": np.concatenate([parts[n] for n, _ in L0_PACK], axis=1),
        "mid": np.concatenate([parts[n] for n, _ in MID_PACK], axis=1),
        "late": np.concatenate([parts[n] for n, _ in LATE_PACK], axis=1),
        "ctxT": ctx.reshape(NT, BT * U, D).transpose(0, 2, 1),
        "ctxR": rows.transpose(0, 3, 1, 2, 4).reshape(NT, P, -1),
        "ctxL": ctx[:, UA].reshape(NT, BT, D),
        "ctx_last": ctx[:, UA],
        "f2_w1": a["L2_ffn_w1"],
        "f2_w2": a["L2_ffn_w2"].reshape(16, 4, P, D).transpose(0, 2, 1, 3).reshape(16, P, -1),
    }
    arrays = {k: np.ascontiguousarray(v) for k, v in arrays.items()}
    nc = bacc.Bacc("TRN2", target_bir_lowering=False, num_devices=1)
    t = {k: nc.dram_tensor(f"in_{k}", v.shape, F32, kind="ExternalInput").ap() for k, v in arrays.items()}
    nslot = 16 * int(1.25 * NTOK / 16)
    for name, shape in (("slots_in", (nslot, D)), ("slots_out", (nslot, D)), ("lat_rows", (NTOK, D)),
                        ("last_rows", (NB, D)), ("mixed", (4, NB, S * S))):
        t[name] = nc.dram_tensor(name, shape, F32, kind="Internal").ap()
    out = nc.dram_tensor("out", (NB, S, D), F32, kind="ExternalOutput").ap()
    program(nc, t, out)
    r = run_bass_kernel_spmd(nc, [{f"in_{k}": v for k, v in arrays.items()}], core_ids=[0])
    return r.results[0]["out"]
```
